# Optimizing a Trainium2 kernel written in Bass

```python
import numpy as np
import jax
import jax.numpy as jnp

def _softmax(x, axis=-1):
    return jax.nn.softmax(x, axis=axis)

def _gelu(x):
    return jax.nn.gelu(x, approximate=True)

def _silu(x):
    return jax.nn.silu(x)

def _sigmoid(x):
    return jax.nn.sigmoid(x)

def _layernorm(x, axis=-1, eps=1e-05):
    m = jnp.mean(x, axis=axis, keepdims=True)
    v = jnp.var(x, axis=axis, keepdims=True)
    return (x - m) / jnp.sqrt(v + eps)

def _scatter_add(tgt, idx, src, axis=0):
    return tgt.at[idx].add(src)

def _segment_sum(src, seg, n):
    return jax.ops.segment_sum(src, seg, n)
kernel_name = 'mk_adaln_d2_jaxref_r8_c544aa'

def setup_inputs(seed: int=0):
    np.random.seed(seed)
    _w = jnp.asarray

    def _L0_attn_setup():
        import jax, jax.numpy as jnp
        import numpy as np
        B, S, D, H, F = (4, 1024, 128, 16, 64)
        DK = D // H
        EPS = 1e-06

        def _heads(x, W, b):
            y = jnp.einsum('bsd,de->bse', x, W) + b
            return y.reshape(x.shape[0], x.shape[1], H, DK).transpose(0, 2, 1, 3)
        key = jax.random.key(seed)
        ks = jax.random.split(key, 6)
        scale = 1.0 / np.sqrt(D)
        x = jax.random.normal(ks[0], (B, S, D), dtype=jnp.float32)
        Wq = jax.random.normal(ks[1], (D, D), dtype=jnp.float32) * scale
        Wk = jax.random.normal(ks[2], (D, D), dtype=jnp.float32) * scale
        Wv = jax.random.normal(ks[3], (D, D), dtype=jnp.float32) * scale
        Wo = jax.random.normal(ks[4], (D, D), dtype=jnp.float32) * scale
        rw = jax.random.normal(ks[5], (H, DK, F), dtype=jnp.float32) / np.sqrt(DK)
        zb = jnp.zeros((D,), dtype=jnp.float32)
        return {'x': x, 'Wq': Wq, 'bq': zb, 'Wk': Wk, 'bk': zb, 'Wv': Wv, 'bv': zb, 'Wo': Wo, 'bo': zb, 'rw': rw}
    _L0_attn_in = _L0_attn_setup()

    def _L0_ffn_setup():
        import jax, jax.numpy as jnp
        import numpy as np
        B, P, D, D_MLP, E, K = (2, 256, 128, 512, 8, 2)
        key = jax.random.key(seed)
        k_x, k_g, k_in, k_out = jax.random.split(key, 4)
        s_in = 1.0 / np.sqrt(D).astype(np.float32)
        s_out = 1.0 / np.sqrt(D_MLP).astype(np.float32)
        return {'x': jax.random.normal(k_x, (B, P, D), dtype=jnp.float32), 'W_gate': jax.random.normal(k_g, (D, E), dtype=jnp.float32) * s_in, 'W_in': jax.random.normal(k_in, (E, D, D_MLP), dtype=jnp.float32) * s_in, 'b_in': jnp.zeros((E, D_MLP), dtype=jnp.float32), 'W_out': jax.random.normal(k_out, (E, D_MLP, D), dtype=jnp.float32) * s_out, 'b_out': jnp.zeros((E, D), dtype=jnp.float32)}
    _L0_ffn_in = _L0_ffn_setup()
    _L0_c = _w((lambda *s: np.random.randn(*s).astype(np.float32) * 0.05)(8, 128))
    _L0_wmod = _w((lambda *s: np.random.randn(*s).astype(np.float32) * 0.05)(128, 6 * 128) * 128 ** (-0.5))

    def _L1_attn_setup():
        import jax, jax.numpy as jnp
        import numpy as np
        D_MODEL = 128
        THRESH = 0.01
        key = jax.random.key(seed)
        kx, kw = jax.random.split(key)
        x = jax.random.normal(kx, (4, 256, D_MODEL), dtype=jnp.float32)
        W = jax.random.normal(kw, (D_MODEL, D_MODEL), dtype=jnp.float32) / np.sqrt(D_MODEL)
        return {'x': x, 'W': W}
    _L1_attn_in = _L1_attn_setup()

    def _L1_ffn_setup():
        import jax, jax.numpy as jnp
        import numpy as np
        DIM = 128
        DEPTH = 6
        HEADS = 16
        DIM_HEAD = 64
        WINDOW = 32
        INNER = HEADS * DIM_HEAD
        DIM_INNER = int(DIM * 4 * 2 / 3)
        QK_SCALE = 8.0

        def shift_tokens(t):
            a, s = jnp.split(t, 2, -1)
            s = jnp.pad(s, ((0, 0), (1, 0), (0, 0)))[:, :-1]
            return jnp.concatenate([a, s], -1)

        def l2norm(t):
            return t / jnp.maximum(jnp.linalg.norm(t, axis=-1, keepdims=True), 1e-12)

        def rotate_half(x):
            x1, x2 = jnp.split(x, 2, -1)
            return jnp.concatenate([-x2, x1], -1)

        def rotary_tables(n):
            half = jnp.arange(0, DIM_HEAD, 2, dtype=jnp.float32)
            inv_freq = 1.0 / 10000.0 ** (half / DIM_HEAD)
            t = jnp.arange(n, dtype=jnp.float32)
            freqs = t[:, None] * inv_freq[None, :]
            freqs = jnp.concatenate([freqs, freqs], -1)
            base_scale = (half + 0.4 * DIM_HEAD) / (1.4 * DIM_HEAD)
            power = (t - n // 2) / (WINDOW // 2)
            scale = base_scale[None, :] ** power[:, None]
            scale = jnp.concatenate([scale, scale], -1)
            return (freqs, scale)

        def local_attention(q, k, v):
            b, h, n, d = q.shape
            w = WINDOW
            nw = n // w
            bq = q.reshape(b, h, nw, w, d)
            bk = k.reshape(b, h, nw, w, d)
            bv = v.reshape(b, h, nw, w, d)

            def look(t):
                p = jnp.pad(t, ((0, 0), (0, 0), (1, 0), (0, 0), (0, 0)))
                return jnp.concatenate([p[:, :, :nw], p[:, :, 1:]], axis=3)
            bk2, bv2 = (look(bk), look(bv))
            seq = jnp.arange(n).reshape(nw, w)
            seq_p = jnp.pad(seq, ((1, 0), (0, 0)), constant_values=-1)
            jt = jnp.concatenate([seq_p[:nw], seq_p[1:]], axis=1)
            it = seq[:, :, None]
            jb = jt[:, None, :]
            mask = (it < jb) | (it > jb + w) | (jb == -1)
            sim = jnp.einsum('bhwie,bhwje->bhwij', bq, bk2) * QK_SCALE
            sim = jnp.where(mask, -jnp.finfo(sim.dtype).max, sim)
            attn = jax.nn.softmax(sim, -1)
            out = jnp.einsum('bhwij,bhwje->bhwie', attn, bv2)
            return out.reshape(b, h, n, d)

        def attn_layer(x, Wqkv, qs, ksc, Wo):
            b, n, _ = x.shape
            qkv = x @ Wqkv
            q, k, v = jnp.split(qkv, 3, -1)
            sh = lambda t: t.reshape(b, n, HEADS, DIM_HEAD).transpose(0, 2, 1, 3)
            q, k, v = (sh(q), sh(k), sh(v))
            q = l2norm(q) * qs
            k = l2norm(k) * ksc
            freqs, scale = rotary_tables(n)
            cos, sin = (jnp.cos(freqs), jnp.sin(freqs))
            q = q * cos * scale + rotate_half(q) * sin * scale
            inv = 1.0 / scale
            k = k * cos * inv + rotate_half(k) * sin * inv
            out = local_attention(q, k, v)
            out = out.transpose(0, 2, 1, 3).reshape(b, n, INNER)
            return out @ Wo

        def ffn_layer(x, g, bln, W1, b1, W2, b2):
            mu = x.mean(-1, keepdims=True)
            var = ((x - mu) ** 2).mean(-1, keepdims=True)
            xn = (x - mu) / jnp.sqrt(var + 1e-05) * g + bln
            hg = xn @ W1 + b1
            a, gate = jnp.split(hg, 2, -1)
            return a * jax.nn.gelu(gate, approximate=False) @ W2 + b2
        key = jax.random.key(seed)
        ks = jax.random.split(key, 8)
        B, N = (2, 256)
        init = lambda k, shape: jax.random.normal(k, shape, jnp.float32) * 0.02
        return {'x': jax.random.normal(ks[0], (B, N, DIM), jnp.float32), 'Wqkv': init(ks[1], (DEPTH, DIM, 3 * INNER)), 'q_scale': jnp.ones((DEPTH, DIM_HEAD), jnp.float32), 'k_scale': jnp.ones((DEPTH, DIM_HEAD), jnp.float32), 'Wo': init(ks[2], (DEPTH, INNER, DIM)), 'ln_g': jnp.ones((DEPTH, DIM), jnp.float32), 'ln_b': jnp.zeros((DEPTH, DIM), jnp.float32), 'W1': init(ks[3], (DEPTH, DIM, 2 * DIM_INNER)), 'b1': jnp.zeros((DEPTH, 2 * DIM_INNER), jnp.float32), 'W2': init(ks[4], (DEPTH, DIM_INNER, DIM)), 'b2': jnp.zeros((DEPTH, DIM), jnp.float32)}
    _L1_ffn_in = _L1_ffn_setup()
    _L1_c = _w((lambda *s: np.random.randn(*s).astype(np.float32) * 0.05)(8, 128))
    _L1_wmod = _w((lambda *s: np.random.randn(*s).astype(np.float32) * 0.05)(128, 6 * 128) * 128 ** (-0.5))
    _d = {'L0_attn_x': _L0_attn_in['x'], 'L0_attn_Wq': _L0_attn_in['Wq'], 'L0_attn_bq': _L0_attn_in['bq'], 'L0_attn_Wk': _L0_attn_in['Wk'], 'L0_attn_bk': _L0_attn_in['bk'], 'L0_attn_Wv': _L0_attn_in['Wv'], 'L0_attn_bv': _L0_attn_in['bv'], 'L0_attn_Wo': _L0_attn_in['Wo'], 'L0_attn_bo': _L0_attn_in['bo'], 'L0_attn_rw': _L0_attn_in['rw'], 'L0_ffn_W_gate': _L0_ffn_in['W_gate'], 'L0_ffn_W_in': _L0_ffn_in['W_in'], 'L0_ffn_b_in': _L0_ffn_in['b_in'], 'L0_ffn_W_out': _L0_ffn_in['W_out'], 'L0_ffn_b_out': _L0_ffn_in['b_out'], 'L0_c': _L0_c, 'L0_wmod': _L0_wmod, 'L1_attn_W': _L1_attn_in['W'], 'L1_ffn_Wqkv': _L1_ffn_in['Wqkv'], 'L1_ffn_q_scale': _L1_ffn_in['q_scale'], 'L1_ffn_k_scale': _L1_ffn_in['k_scale'], 'L1_ffn_Wo': _L1_ffn_in['Wo'], 'L1_ffn_ln_g': _L1_ffn_in['ln_g'], 'L1_ffn_ln_b': _L1_ffn_in['ln_b'], 'L1_ffn_W1': _L1_ffn_in['W1'], 'L1_ffn_b1': _L1_ffn_in['b1'], 'L1_ffn_W2': _L1_ffn_in['W2'], 'L1_ffn_b2': _L1_ffn_in['b2'], 'L1_c': _L1_c, 'L1_wmod': _L1_wmod}
    _x0 = _d['L0_attn_x']
    _d['L0_attn_x'] = jax.random.normal(jax.random.fold_in(jax.random.key(seed), 1), (8, 256, 128), dtype=_x0.dtype)
    del _x0
    return _d

def reference(L0_attn_x, L0_attn_Wq, L0_attn_bq, L0_attn_Wk, L0_attn_bk, L0_attn_Wv, L0_attn_bv, L0_attn_Wo, L0_attn_bo, L0_attn_rw, L0_ffn_W_gate, L0_ffn_W_in, L0_ffn_b_in, L0_ffn_W_out, L0_ffn_b_out, L0_c, L0_wmod, L1_attn_W, L1_ffn_Wqkv, L1_ffn_q_scale, L1_ffn_k_scale, L1_ffn_Wo, L1_ffn_ln_g, L1_ffn_ln_b, L1_ffn_W1, L1_ffn_b1, L1_ffn_W2, L1_ffn_b2, L1_c, L1_wmod):

    def _L0_attn_ref(x, Wq, bq, Wk, bk, Wv, bv, Wo, bo, rw):
        import jax, jax.numpy as jnp
        import numpy as np
        B, S, D, H, F = (4, 1024, 128, 16, 64)
        DK = D // H
        EPS = 1e-06

        def _heads(x, W, b):
            y = jnp.einsum('bsd,de->bse', x, W) + b
            return y.reshape(x.shape[0], x.shape[1], H, DK).transpose(0, 2, 1, 3)
        q = _heads(x, Wq, bq)
        k = _heads(x, Wk, bk)
        v = _heads(x, Wv, bv)
        qp = jax.nn.relu(jnp.einsum('bhsd,hdf->bhsf', q, rw)) + EPS
        kp = jax.nn.relu(jnp.einsum('bhsd,hdf->bhsf', k, rw)) + EPS
        kv = jnp.einsum('bhsf,bhsd->bhfd', kp, v)
        qkv = jnp.einsum('bhsf,bhfd->bhsd', qp, kv)
        norm = jnp.einsum('bhsf,bhf->bhs', qp, kp.sum(axis=2))
        out = qkv / (norm[..., None] + EPS)
        out = out.transpose(0, 2, 1, 3).reshape(x.shape[0], x.shape[1], D)
        return jnp.einsum('bsd,de->bse', out, Wo) + bo

    def _L0_ffn_ref(x, W_gate, W_in, b_in, W_out, b_out):
        import jax, jax.numpy as jnp
        import numpy as np
        B, P, D, D_MLP, E, K = (2, 256, 128, 512, 8, 2)
        gate_logits = jnp.einsum('bpd,de->bpe', x, W_gate)
        top_w, top_idx = jax.lax.top_k(gate_logits, K)
        top_w = jax.nn.softmax(top_w, axis=-1)
        combine = jnp.einsum('bpke,bpk->bpe', jax.nn.one_hot(top_idx, E, dtype=x.dtype), top_w)
        out = jnp.zeros_like(x)
        for e in range(E):
            h = jax.nn.gelu(jnp.einsum('bpd,dm->bpm', x, W_in[e]) + b_in[e], approximate=False)
            y = jnp.einsum('bpm,md->bpd', h, W_out[e]) + b_out[e]
            out = out + combine[..., e, None] * y
        return out

    def _L1_attn_ref(x, W):
        import jax, jax.numpy as jnp
        import numpy as np
        D_MODEL = 128
        THRESH = 0.01
        B, T, D = x.shape
        scale = 1.0 / jnp.sqrt(jnp.asarray(D, x.dtype))
        scores = jnp.einsum('btd,bsd->bts', x, x) * scale
        probs = jax.nn.softmax(scores, axis=-1)
        vacuum_mask = probs < THRESH
        vacuum_energy = jnp.where(vacuum_mask, probs, 0.0)
        vac_sum = vacuum_energy.sum(axis=-1, keepdims=True)
        vac_in = jnp.broadcast_to(vac_sum, (B, T, D))
        casimir = jnp.einsum('btd,od->bto', vac_in, W)
        sparse_probs = jnp.where(vacuum_mask, 0.0, probs)
        sparse_probs = sparse_probs / (sparse_probs.sum(axis=-1, keepdims=True) + 1e-09)
        attended = jnp.einsum('bts,bsd->btd', sparse_probs, x)
        return attended + casimir * 0.01

    def _L1_ffn_ref(x, Wqkv, q_scale, k_scale, Wo, ln_g, ln_b, W1, b1, W2, b2):
        import jax, jax.numpy as jnp
        import numpy as np
        DIM = 128
        DEPTH = 6
        HEADS = 16
        DIM_HEAD = 64
        WINDOW = 32
        INNER = HEADS * DIM_HEAD
        DIM_INNER = int(DIM * 4 * 2 / 3)
        QK_SCALE = 8.0

        def shift_tokens(t):
            a, s = jnp.split(t, 2, -1)
            s = jnp.pad(s, ((0, 0), (1, 0), (0, 0)))[:, :-1]
            return jnp.concatenate([a, s], -1)

        def l2norm(t):
            return t / jnp.maximum(jnp.linalg.norm(t, axis=-1, keepdims=True), 1e-12)

        def rotate_half(x):
            x1, x2 = jnp.split(x, 2, -1)
            return jnp.concatenate([-x2, x1], -1)

        def rotary_tables(n):
            half = jnp.arange(0, DIM_HEAD, 2, dtype=jnp.float32)
            inv_freq = 1.0 / 10000.0 ** (half / DIM_HEAD)
            t = jnp.arange(n, dtype=jnp.float32)
            freqs = t[:, None] * inv_freq[None, :]
            freqs = jnp.concatenate([freqs, freqs], -1)
            base_scale = (half + 0.4 * DIM_HEAD) / (1.4 * DIM_HEAD)
            power = (t - n // 2) / (WINDOW // 2)
            scale = base_scale[None, :] ** power[:, None]
            scale = jnp.concatenate([scale, scale], -1)
            return (freqs, scale)

        def local_attention(q, k, v):
            b, h, n, d = q.shape
            w = WINDOW
            nw = n // w
            bq = q.reshape(b, h, nw, w, d)
            bk = k.reshape(b, h, nw, w, d)
            bv = v.reshape(b, h, nw, w, d)

            def look(t):
                p = jnp.pad(t, ((0, 0), (0, 0), (1, 0), (0, 0), (0, 0)))
                return jnp.concatenate([p[:, :, :nw], p[:, :, 1:]], axis=3)
            bk2, bv2 = (look(bk), look(bv))
            seq = jnp.arange(n).reshape(nw, w)
            seq_p = jnp.pad(seq, ((1, 0), (0, 0)), constant_values=-1)
            jt = jnp.concatenate([seq_p[:nw], seq_p[1:]], axis=1)
            it = seq[:, :, None]
            jb = jt[:, None, :]
            mask = (it < jb) | (it > jb + w) | (jb == -1)
            sim = jnp.einsum('bhwie,bhwje->bhwij', bq, bk2) * QK_SCALE
            sim = jnp.where(mask, -jnp.finfo(sim.dtype).max, sim)
            attn = jax.nn.softmax(sim, -1)
            out = jnp.einsum('bhwij,bhwje->bhwie', attn, bv2)
            return out.reshape(b, h, n, d)

        def attn_layer(x, Wqkv, qs, ksc, Wo):
            b, n, _ = x.shape
            qkv = x @ Wqkv
            q, k, v = jnp.split(qkv, 3, -1)
            sh = lambda t: t.reshape(b, n, HEADS, DIM_HEAD).transpose(0, 2, 1, 3)
            q, k, v = (sh(q), sh(k), sh(v))
            q = l2norm(q) * qs
            k = l2norm(k) * ksc
            freqs, scale = rotary_tables(n)
            cos, sin = (jnp.cos(freqs), jnp.sin(freqs))
            q = q * cos * scale + rotate_half(q) * sin * scale
            inv = 1.0 / scale
            k = k * cos * inv + rotate_half(k) * sin * inv
            out = local_attention(q, k, v)
            out = out.transpose(0, 2, 1, 3).reshape(b, n, INNER)
            return out @ Wo

        def ffn_layer(x, g, bln, W1, b1, W2, b2):
            mu = x.mean(-1, keepdims=True)
            var = ((x - mu) ** 2).mean(-1, keepdims=True)
            xn = (x - mu) / jnp.sqrt(var + 1e-05) * g + bln
            hg = xn @ W1 + b1
            a, gate = jnp.split(hg, 2, -1)
            return a * jax.nn.gelu(gate, approximate=False) @ W2 + b2
        for i in range(DEPTH):
            x = attn_layer(shift_tokens(x), Wqkv[i], q_scale[i], k_scale[i], Wo[i]) + x
            x = ffn_layer(shift_tokens(x), ln_g[i], ln_b[i], W1[i], b1[i], W2[i], b2[i]) + x
        return x
    x = L0_attn_x
    mod = (_silu(L0_c) @ L0_wmod).reshape(L0_c.shape[0], 6, 1, -1)
    sa, ca, ga, sb, cb, gb = (mod[:, 0], mod[:, 1], mod[:, 2], mod[:, 3], mod[:, 4], mod[:, 5])
    ga = (2 * (ga >= 0) - 1) * jnp.maximum(jnp.abs(ga), 0.25)
    gb = (2 * (gb >= 0) - 1) * jnp.maximum(jnp.abs(gb), 0.25)
    h = _layernorm(x, axis=-1) * (1 + ca) + sa
    x = x + ga * _L0_attn_ref(h, L0_attn_Wq, L0_attn_bq, L0_attn_Wk, L0_attn_bk, L0_attn_Wv, L0_attn_bv, L0_attn_Wo, L0_attn_bo, L0_attn_rw)
    h = _layernorm(x, axis=-1) * (1 + cb) + sb
    x = x + gb * _L0_ffn_ref(h, L0_ffn_W_gate, L0_ffn_W_in, L0_ffn_b_in, L0_ffn_W_out, L0_ffn_b_out)
    mod = (_silu(L1_c) @ L1_wmod).reshape(L1_c.shape[0], 6, 1, -1)
    sa, ca, ga, sb, cb, gb = (mod[:, 0], mod[:, 1], mod[:, 2], mod[:, 3], mod[:, 4], mod[:, 5])
    ga = (2 * (ga >= 0) - 1) * jnp.maximum(jnp.abs(ga), 0.25)
    gb = (2 * (gb >= 0) - 1) * jnp.maximum(jnp.abs(gb), 0.25)
    h = _layernorm(x, axis=-1) * (1 + ca) + sa
    x = x + ga * _L1_attn_ref(h, L1_attn_W)
    h = _layernorm(x, axis=-1) * (1 + cb) + sb
    x = x + gb * _L1_ffn_ref(h, L1_ffn_Wqkv, L1_ffn_q_scale, L1_ffn_k_scale, L1_ffn_Wo, L1_ffn_ln_g, L1_ffn_ln_b, L1_ffn_W1, L1_ffn_b1, L1_ffn_W2, L1_ffn_b2)
    return x

_drawn_inputs = setup_inputs


def setup_inputs(seed=0):
    import zlib

    import numpy as np

    out = dict(_drawn_inputs(seed))
    spreads = {'L0_attn_bq': (0.0, 2.0),
     'L0_attn_bk': (0.0, 2.0),
     'L0_attn_bv': (0.0, 0.28),
     'L0_attn_bo': (0.0, 0.277),
     'L0_ffn_b_in': (0.0, 0.643),
     'L0_ffn_b_out': (0.0, 0.428),
     'L1_ffn_q_scale': (1.0, 0.6),
     'L1_ffn_k_scale': (1.0, 0.6),
     'L1_ffn_ln_g': (1.0, 0.6),
     'L1_ffn_ln_b': (0.0, 0.8),
     'L1_ffn_b1': (0.0, 0.8),
     'L1_ffn_b2': (0.0, 0.648)}
    factors = {'L0_attn_Wq': 2.993,
     'L0_attn_Wk': 2.836,
     'L0_attn_rw': 18.953,
     'L1_attn_W': 64.0,
     'L1_ffn_W1': 7.778,
     'L1_ffn_W2': 7.636}
    for name, (base, spread) in spreads.items():
        noise = np.random.default_rng([zlib.crc32(name.encode()), seed]).standard_normal(out[name].shape)
        drawn = base * np.exp(spread * noise) if base else spread * noise
        out[name] = jnp.asarray(drawn.astype(out[name].dtype))
    for name, factor in factors.items():
        out[name] = (out[name] * factor).astype(out[name].dtype)
    return out
```

```python
from contextlib import ExitStack

import numpy as np

import concourse.bass as bass
from concourse import mybir

F32 = mybir.dt.float32
BF16 = mybir.dt.bfloat16
U32 = mybir.dt.uint32
ALU = mybir.AluOpType
ACT = mybir.ActivationFunctionType
AX = mybir.AxisListType

P = 128
D = 128
B, S = 8, 256
NT = B * S
TC = S // P
H0, DK0, F0 = 16, 8, 64
NF = H0 * F0
FC = NF // P
KVW = 2 * DK0 + 2
EPS0 = 1e-6
NE, DM = 8, 512
MC = DM // P
THRESH = 0.01
DEPTH, HEADS, DH, WIN = 6, 16, 64, 32
INNER = HEADS * DH
DI = int(D * 4 * 2 / 3)
DIC = [(j * P, min(P, DI - j * P)) for j in range((DI + P - 1) // P)]
QK_SCALE = 8.0
HP = HEADS // 2
NW = P // WIN
LN_EPS = 1e-5
NEG = -1.0e30

ROWS = {}
for _name, _n in (("bq", 1), ("bk", 1), ("bo", 1), ("b_in", NE * MC), ("ln_g", DEPTH), ("ln_b", DEPTH),
                  ("b2", DEPTH), ("b1", DEPTH * 2 * len(DIC)), ("c0", B), ("c1", B)):
    ROWS[_name] = sum(n for _, n in ROWS.values()), _n
NROWS = sum(n for _, n in ROWS.values())
CONST = {}
for _name, _n in (("ident", P), ("rot", TC * 4 * DH), ("kvmask", FC * KVW), ("iota", NE), ("mask", 2 * 2 * WIN)):
    CONST[_name] = sum(n for _, n in CONST.values()), _n
NCONST = sum(n for _, n in CONST.values())
KEPT = CONST["kvmask"][0]


def constants():
    out = np.zeros((P, NCONST), np.float32)

    def put(name, a):
        at, n = CONST[name]
        out[:, at:at + n] = a.reshape(P, n)

    put("ident", np.eye(P, dtype=np.float32))
    f = np.float32
    half = np.arange(0, DH, 2, dtype=f)
    inv_freq = (f(1.0) / np.power(f(10000.0), half / f(DH))).astype(f)
    t = np.arange(S, dtype=f)
    freqs = t[:, None] * inv_freq[None, :]
    base = (half + f(0.4 * DH)) / f(1.4 * DH)
    power = (t - f(S // 2)) / f(WIN // 2)
    scale = np.power(base[None, :], power[:, None]).astype(f)
    cos, sin = np.cos(freqs).astype(f), np.sin(freqs).astype(f)
    two = lambda a, b: np.concatenate([a, b], -1)
    q_cos = two(cos * scale, cos * scale) * f(QK_SCALE)
    q_sin = two(-sin * scale, sin * scale) * f(QK_SCALE)
    inv = f(1.0) / scale
    k_cos = two(cos * inv, cos * inv)
    k_sin = two(-sin * inv, sin * inv)
    rot = np.stack([q_cos, q_sin, k_cos, k_sin], 1)
    put("rot", rot.reshape(TC, P, 4, DH).transpose(1, 0, 2, 3))
    m = np.zeros((P, FC, KVW), f)
    for h in range(2):
        m[h * F0:(h + 1) * F0, :, h * DK0:(h + 1) * DK0] = 1
        m[h * F0:(h + 1) * F0, :, 2 * DK0 + h] = 1
    put("kvmask", m)
    put("iota", np.tile(np.arange(NE, dtype=f), (P, 1)))
    i, j = (np.arange(P) % WIN)[:, None], np.arange(2 * WIN)[None, :]
    bad = (j < i) | (j > i + WIN)
    first = bad | ((np.arange(P)[:, None] < WIN) & (j < WIN))
    put("mask", np.stack([np.where(first, f(NEG), f(0)), np.where(bad, f(NEG), f(0))], 1))
    return out


class Signals:

    def __init__(self, nc, ctx):
        self.nc, self.ctx = nc, ctx
        self.sems, self.count, self.seen, self.last = {}, {}, {}, {}

    def mark(self, stage, instruction, by=1):
        if stage not in self.sems:
            self.sems[stage] = self.ctx.enter_context(self.nc.semaphore("s_" + stage))
            self.count[stage] = 0
        self.count[stage] += by
        instruction.then_inc(self.sems[stage], by)
        self.last[stage] = (stage, self.count[stage])
        return self.last[stage]

    def dma(self, stage, instruction):
        return self.mark(stage, instruction, 16)

    def wait(self, engine, *events):
        for stage, value in events:
            key = (id(engine), stage)
            if self.seen.get(key, 0) < value:
                self.seen[key] = value
                engine.wait_ge(self.sems[stage], value)


class Slot:
    def __init__(self, ring, k):
        self.ring, self.k, self.t, self.free = ring, k, ring.bufs[k], ring.freed[k]

    def release(self, *events):
        self.ring.freed[self.k] = events


class Ring:

    def __init__(self, bufs):
        self.bufs, self.freed, self.n = bufs, [()] * len(bufs), 0

    def take(self):
        k = self.n % len(self.bufs)
        self.n += 1
        assert self.freed[k] is not None, "a buffer is taken before its last user is done with it"
        slot = Slot(self, k)
        self.freed[k] = None
        return slot


def interleave(units, spacing):
    live, n = [], 0
    slot = 0
    while live or n < len(units):
        if n < len(units) and slot >= n * spacing:
            live.append(units[n]())
            n += 1
        for g in list(live):
            try:
                next(g)
            except StopIteration:
                live.remove(g)
        slot += 1


def build(nc, a, out):
    ctx = ExitStack()
    sg = Signals(nc, ctx)
    mark, wait = sg.mark, sg.wait
    pe, dve, act, pool, sp = nc.tensor, nc.vector, nc.scalar, nc.gpsimd, nc.sync

    def mark_pool(stage, instruction):
        e = mark(stage, instruction)
        wait(pool, e)
        return e

    def sb(name, shape, dt=F32, where=ctx):
        return where.enter_context(nc.sbuf_tensor(name, shape, dt))

    def sb_ring(name, n, shape, dt=F32, where=ctx):
        return Ring([sb(f"{name}{k}", shape, dt, where) for k in range(n)])

    banks = [ctx.enter_context(nc.psum_tensor(f"bank{k}", [P, 512], F32)) for k in range(8)]

    xT = sb("xT", [P, NT])
    zT = sb("zT", [P, NT])
    const = sb("const", [P, KEPT])
    ones_d = sb("ones_d", [P, P])
    eps_ln = sb("eps_ln", [P, 1])
    ident_b = sb("ident_b", [P, P], BF16)
    mask_b = sb("mask_b", [P, 2, HP, 2 * WIN], BF16)
    cols = sb("cols", [P, NROWS])
    mod = [sb(f"mod{k}", [P, 6, B]) for k in range(2)]
    wqk = sb_ring("wqk", 2, [P, 2 * INNER])
    wv = sb_ring("wv", 2, [P, INNER])
    wo = sb_ring("wo", 1, [P, INNER // P, D])
    w1 = sb_ring("w1", 1, [P, 2 * DI])
    w2 = sb_ring("w2", 1, [P, len(DIC), D])
    rot = sb_ring("rot", 2, [P, TC, 4, DH])
    gain = sb_ring("gain", 2, [P, 2, DH])

    early = ExitStack()
    const_e = sb("const_e", [P, NCONST - KEPT], F32, early)

    def cst(name):
        at, n = CONST[name]
        return const[:, at:at + n] if at < KEPT else const_e[:, at - KEPT:at - KEPT + n]

    ident = cst("ident")

    def col(name, k=0, rows=P):
        at = ROWS[name][0] + k
        return cols[0:rows, at:at + 1]

    def mcol(block, k, b):
        return mod[block][:, k, b:b + 1]

    def esb(name, shape, dt=F32):
        return sb(name, shape, dt, early)

    rows_m = esb("rows_m", [P, P])
    e_zero = mark("zero", dve.memset(rows_m[:, :], 0.0))
    x_rows = esb("x_rows", [P, NT // P, D])
    sg.dma("ld_const", sp.dma_start(const[:, :], a["const"][:, 0:KEPT]))
    ev_const = sg.dma("ld_const", sp.dma_start(const_e[:, :], a["const"][:, KEPT:]))
    xr = a["L0_attn_x"].rearrange("b (c p) d -> p (b c) d", p=P)
    ev_x = [sg.dma(f"ld_x{q}", sp.dma_start(x_rows[:, 4 * q:4 * q + 4, :], xr[:, 4 * q:4 * q + 4, :]))
            for q in range(NT // P // 4)]
    wait(act, e_zero)

    def load_rows(name, src, n, k=0, width=P):
        at = ROWS[name][0] + k
        return sg.dma("ld_rows", act.dma_start(rows_m[at:at + n, 0:width], src))

    one_row = lambda v: v.rearrange("(o n) -> o n", o=1)
    load_rows("bq", one_row(a["L0_attn_bq"]), 1)
    load_rows("bk", one_row(a["L0_attn_bk"]), 1)
    load_rows("bo", one_row(a["L0_attn_bo"]), 1)
    load_rows("b_in", a["L0_ffn_b_in"].rearrange("e (m p) -> (e m) p", p=P), NE * MC)
    load_rows("ln_g", a["L1_ffn_ln_g"], DEPTH)
    load_rows("ln_b", a["L1_ffn_ln_b"], DEPTH)
    load_rows("b2", a["L1_ffn_b2"], DEPTH)
    for part in range(2):
        for j, (at, n) in enumerate(DIC):
            k = (part * len(DIC) + j) * DEPTH
            load_rows("b1", a["L1_ffn_b1"][:, part * DI + at:part * DI + at + n], DEPTH, k, n)
    load_rows("c0", a["L0_c"], B)
    ev_rows = load_rows("c1", a["L1_c"], B)

    wmod = [esb(f"wmod{k}", [P, 6 * D]) for k in range(2)]
    w_q, w_k, w_v, w_o = (esb(n, [P, D]) for n in ("w_q", "w_k", "w_v", "w_o"))
    w_rf = esb("w_rf", [P, NF])
    bv_b = esb("bv_b", [P, D])
    w_gate = esb("w_gate", [P, NE])
    w_in = esb("w_in", [P, NE, DM])
    w_out = esb("w_out", [P, NE, MC, D])
    b_out = esb("b_out", [NE, D])
    w_c = esb("w_c", [P, D])
    ev_wmod = [sg.dma(f"ld_wmod{k}", sp.dma_start(wmod[k][:, :], a[f"L{k}_wmod"])) for k in range(2)]
    for t, n in ((w_q, "L0_attn_Wq"), (w_k, "L0_attn_Wk"), (w_v, "L0_attn_Wv"), (w_o, "L0_attn_Wo")):
        ev_w0 = sg.dma("ld_w0", sp.dma_start(t[:, :], a[n]))
    ev_w0 = sg.dma("ld_w0", sp.dma_start(bv_b[:, :], one_row(a["L0_attn_bv"]).to_broadcast([P, D])))
    e_rf0 = mark_pool("rf_zero", pool.memset(w_rf[:, :], 0.0))
    wait(act, e_rf0)
    for h in range(H0):
        ev_rf = sg.dma("ld_rf", act.dma_start(w_rf[h * DK0:(h + 1) * DK0, h * F0:(h + 1) * F0],
                                              a["L0_attn_rw"][h]))
    ev_moe = sg.dma("ld_moe", sp.dma_start(w_gate[:, :], a["L0_ffn_W_gate"]))
    ev_moe = sg.dma("ld_moe", sp.dma_start(b_out[:, :], a["L0_ffn_b_out"]))
    ev_moe = sg.dma("ld_moe", sp.dma_start(w_in[:, :, :], a["L0_ffn_W_in"].rearrange("e d m -> d e m")))
    for e in range(NE):
        ev_moe = sg.dma("ld_moe", sp.dma_start(w_out[:, e, :, :],
                                               a["L0_ffn_W_out"][e].rearrange("(m p) n -> p m n", p=P)))
    ev_wc = sg.dma("ld_wc", sp.dma_start(w_c[:, :], a["L1_attn_W"]))

    layer_w = {l: {} for l in range(DEPTH)}

    def take_weights(l, name, ring):
        slot = ring.take()
        wait(sp, *slot.free)
        return slot

    def load_projections(l):
        k, src = l % 2, a["L1_ffn_Wqkv"][l]
        slot = take_weights(l, "qk", wqk)
        layer_w[l]["qk"] = slot, sg.dma(f"ld_wqk{k}", sp.dma_start(slot.t[:, :], src[:, 0:2 * INNER]))
        slot = take_weights(l, "v", wv)
        vsrc = src[:, 2 * INNER:].rearrange("d (hp r e) -> d r hp e", r=2, e=DH)
        for r in range(2):
            vdst = slot.t[:, r * HP * DH:(r + 1) * HP * DH].rearrange("d (hp e) -> d hp e", e=DH)
            e = sg.dma(f"ld_wv{k}", sp.dma_start(vdst, vsrc[:, r, :, :]))
        layer_w[l]["v"] = slot, e
        slot = take_weights(l, "gain", gain)
        for j, n in enumerate(("q", "k")):
            e = sg.dma(f"ld_gain{k}", sp.dma_start(slot.t[:, j, :],
                                                   a[f"L1_ffn_{n}_scale"][l:l + 1, :].to_broadcast([P, DH])))
        layer_w[l]["gain"] = slot, e

    def load_output(l):
        slot = take_weights(l, "o", wo)
        layer_w[l]["o"] = slot, sg.dma("ld_wo", sp.dma_start(
            slot.t[:, :, :], a["L1_ffn_Wo"][l].rearrange("(c p) n -> p c n", p=P)))

    def load_ffn(l):
        slot = take_weights(l, "w1", w1)
        layer_w[l]["w1"] = slot, sg.dma("ld_w1", sp.dma_start(slot.t[:, :], a["L1_ffn_W1"][l]))
        slot = take_weights(l, "w2", w2)
        for j, (at, n) in enumerate(DIC):
            e = sg.dma("ld_w2", sp.dma_start(slot.t[0:n, j, :], a["L1_ffn_W2"][l][at:at + n, :]))
        layer_w[l]["w2"] = slot, e

    load_projections(0)
    load_output(0)
    load_ffn(0)

    e_ones = mark_pool("ones", pool.memset(ones_d[:, :], 1.0 / D))
    e_eps = mark_pool("ones", pool.memset(eps_ln[:, :], LN_EPS))
    wait(dve, ev_const)
    dve.tensor_copy(ident_b[:, :], ident)
    mview = cst("mask").rearrange("p (k j) -> p k j", k=2)
    for k in range(2):
        e_cst = mark("cst", dve.tensor_copy(mask_b[:, k, :, :],
                                            mview[:, k, :].unsqueeze(1).to_broadcast([P, HP, 2 * WIN])))

    work = Ring(banks[0:4])
    hid_banks = Ring(banks[4:6])
    y_banks = Ring(banks[6:8])

    bk = work.take()
    wait(pe, ev_const, ev_rows)
    e = mark("pe_misc", pe.transpose(bk.t[:, 0:NROWS], rows_m[0:NROWS, :], ident[0:NROWS, 0:NROWS]))
    wait(dve, e)
    e_cols = mark("cols", dve.tensor_copy(cols[:, :], bk.t[:, 0:NROWS]))
    bk.release(e_cols)

    tmp = esb("mod_tmp", [P, 4, 2 * B])
    for k in range(2):
        silu = esb(f"silu{k}", [P, B])
        at = ROWS[f"c{k}"][0]
        wait(act, e_cols)
        e_silu = mark("silu", act.activation(silu[:, :], cols[:, at:at + B], ACT.Silu))
        bk = work.take()
        wait(pe, e_silu, ev_wmod[k], *bk.free)
        for j in range(6):
            e = mark("pe_misc", pe.matmul(bk.t[:, j * B:(j + 1) * B], wmod[k][:, j * D:(j + 1) * D],
                                          silu[:, :], start=True, stop=True))
        wait(dve, e)
        e = mark("mod", dve.tensor_copy(mod[k][:, :, :], bk.t[:, 0:6 * B].rearrange("p (j b) -> p j b", b=B)))
        bk.release(e)
        wait(dve, e)
        for j in (1, 4):
            e = mark("mod", dve.tensor_scalar(mod[k][:, j, :], mod[k][:, j, :], 1.0, None, ALU.add))
        for j in (2, 5):
            g = mod[k][:, j, :]
            neg, mag, sgn = tmp[:, 0, 0:B], tmp[:, 1, 0:B], tmp[:, 2, 0:B]
            wait(dve, e)
            e = mark("mod", dve.tensor_scalar(neg, g, -1.0, None, ALU.mult))
            wait(dve, e)
            e = mark("mod", dve.tensor_tensor(mag, neg, g, ALU.max))
            e = mark("mod", dve.tensor_scalar(sgn, g, 0.0, 2.0, ALU.is_ge, ALU.mult))
            wait(dve, e)
            e = mark("mod", dve.tensor_scalar(mag, mag, 0.25, None, ALU.max))
            e = mark("mod", dve.tensor_scalar(sgn, sgn, -1.0, None, ALU.add))
            wait(dve, e)
            e = mark("mod", dve.tensor_tensor(g, mag, sgn, ALU.mult))
        e_mod = e

    e_xT = []
    for q in range(NT // P // 4):
        bk = work.take()
        wait(pe, ev_x[q], *bk.free)
        for k in range(4):
            e = mark("pe_x", pe.transpose(bk.t[:, k * P:(k + 1) * P], x_rows[:, 4 * q + k, :], ident))
        wait(act, e)
        e_xT.append(mark("xT", act.activation(xT[:, q * 512:(q + 1) * 512], bk.t[:, :], ACT.Copy)))
        bk.release(e_xT[-1])

    wcT = esb("wcT", [P, D])
    wsum = esb("wsum", [P, D])
    ones1 = esb("ones1", [P, P])
    e_one1 = mark_pool("ones", pool.memset(ones1[:, :], 1.0))
    bk = work.take()
    wait(pe, ev_wc, *bk.free)
    e = mark("pe_misc", pe.transpose(bk.t[:, 0:P], w_c[:, :], ident))
    wait(dve, e)
    e = mark("wsum", dve.tensor_copy(wcT[:, :], bk.t[:, 0:P]))
    bk.release(e)
    bk = work.take()
    wait(pe, e, e_one1, *bk.free)
    e = mark("pe_misc", pe.matmul(bk.t[:, 0:D], ones1[:, :], wcT[:, :], start=True, stop=True))
    wait(dve, e)
    e_wsum = mark("wsum", dve.tensor_copy(wsum[:, :], bk.t[:, 0:D]))
    bk.release(e_wsum)

    def layer_norm(src, ready, ring, buf, gain, shift, dst, dst_free, tag):
        xc, sq = buf[:, 0, :], buf[:, 1, :]
        bank = ring.take()
        mean = bank.t[:, 0:S]
        wait(pe, e_ones, *ready, *bank.free)
        e = mark("ln_mean", pe.matmul(mean, ones_d[:, :], src, start=True, stop=True))
        wait(dve, e, *ready)
        e_xc = mark("ln_xc", dve.tensor_tensor(xc, src, mean, ALU.subtract))
        wait(act, e_xc)
        bank.release(e_xc)
        e = mark("ln_sq", act.activation(sq, xc, ACT.Square))
        yield
        bank = ring.take()
        var = bank.t[:, 0:S]
        wait(pe, e, *bank.free)
        e = mark("ln_var", pe.matmul(var, ones_d[:, :], sq, start=True, stop=True))
        wait(act, e, e_eps)
        e_sd = mark("ln_sd", act.activation(sq, var, ACT.Sqrt, bias=eps_ln[:, :]))
        bank.release(e_sd)
        yield
        wait(dve, e_sd)
        e = mark("ln_out", dve.reciprocal(sq, sq))
        wait(dve, e)
        e = mark("ln_out", dve.tensor_tensor(xc, xc, sq, ALU.mult))
        wait(dve, e, *dst_free)
        return mark("ln_out", dve.tensor_scalar(dst, xc, gain, shift, ALU.mult, ALU.add))

    def er(name, n, shape, dt=F32):
        return sb_ring(name, n, shape, dt, early)

    ln_buf = er("e_ln", 4, [P, 2, S])
    h_buf = er("e_h", 4, [P, S])
    qkT_b = er("e_qkT", 2, [P, 2, S])
    v_ext = er("e_vext", 2, [P, TC, FC, KVW])
    kp_b = er("e_kp", 1, [P, TC, NF])
    qp_b = er("e_qp", 1, [P, FC, S])
    kv_b = er("e_kv", 2, [P, FC, KVW])
    o_b = er("e_o", 3, [P, TC, D])
    oT_b = er("e_oT", 2, [P, S])
    sm_b = er("e_small", 4, [P, 64])
    hid = er("e_hid", 3, [P, MC, S])
    acc_b = er("e_acc", 2, [P, TC, D])
    gate_b = er("e_gate", 3, [P, TC, 8 * NE])
    idx_b = er("e_idx", 3, [P, TC, NE], U32)
    cT_b = er("e_cT", 3, [NE, S])
    prob_b = er("e_prob", 2, [P, TC, S])
    sp_b = er("e_sp", 1, [P, TC, S])
    spT_b = er("e_spT", 2, [P, TC, S])
    hr_b = er("e_hr", 2, [P, TC, P])

    for slot in v_ext.bufs:
        e_vones = mark_pool("v_ones", pool.memset(slot[:, :, :, 2 * DK0:], 1.0))

    def early_unit(b):
        x = xT[:, b * S:(b + 1) * S]
        tok = lambda t, c: t[:, c * P:(c + 1) * P]
        x_in = e_xT[b * S // 512]

        lb, h = ln_buf.take(), h_buf.take()
        wait(dve, *lb.free, e_mod)
        e_h = yield from layer_norm(x, [x_in], work, lb.t, mcol(0, 1, b), mcol(0, 0, b), h.t[:, :], h.free, "a")
        lb.release(e_h)
        bank, qkT = work.take(), qkT_b.take()
        wait(pe, e_h, ev_w0, *bank.free)
        pe.matmul(bank.t[:, 0:S], w_q[:, :], h.t[:, :], start=True, stop=True)
        e = mark("pe_qk0", pe.matmul(bank.t[:, S:2 * S], w_k[:, :], h.t[:, :], start=True, stop=True))
        wait(act, e, e_cols, *qkT.free)
        act.activation(qkT.t[:, 0, :], bank.t[:, 0:S], ACT.Identity, bias=col("bq"))
        e_qk = mark("qkT0", act.activation(qkT.t[:, 1, :], bank.t[:, S:2 * S], ACT.Identity, bias=col("bk")))
        bank.release(e_qk)
        bank, vx = work.take(), v_ext.take()
        wait(pe, *bank.free)
        for c in range(TC):
            e_v = mark("pe_v0", pe.matmul(bank.t[:, c * D:(c + 1) * D], tok(h.t, c), w_v[:, :],
                                          start=True, stop=True))
        h.release(e_v)
        wait(dve, e_v, ev_w0, e_vones, *vx.free)
        for c in range(TC):
            e_vx = mark("vx", dve.tensor_tensor(
                vx.t[:, c, :, 0:2 * DK0],
                bank.t[:, c * D:(c + 1) * D].rearrange("p (f w) -> p f w", w=2 * DK0),
                bv_b[:, :].rearrange("p (f w) -> p f w", w=2 * DK0), ALU.add))
        bank.release(e_vx)
        yield
        kp = kp_b.take()
        wait(dve, *kp.free)
        for c in range(TC):
            for n in range(NF // 512):
                bank = work.take()
                wait(pe, e_qk, ev_rf, *bank.free)
                e = mark("pe_kp", pe.matmul(bank.t[:, :], qkT.t[:, 1, c * P:(c + 1) * P],
                                            w_rf[:, n * 512:(n + 1) * 512], start=True, stop=True))
                wait(dve, e)
                e_kp = mark("kp", dve.tensor_scalar(kp.t[:, c, n * 512:(n + 1) * 512], bank.t[:, :],
                                                    0.0, EPS0, ALU.max, ALU.add))
                bank.release(e_kp)
            yield
        qp = qp_b.take()
        wait(dve, *qp.free)
        for f in range(0, FC, 2):
            bank = work.take()
            wait(pe, *bank.free)
            for k in range(2):
                e = mark("pe_qp", pe.matmul(bank.t[:, k * S:(k + 1) * S], w_rf[:, (f + k) * P:(f + k + 1) * P],
                                            qkT.t[:, 0, :], start=True, stop=True))
            wait(dve, e)
            e_qp = mark("qp", dve.tensor_scalar(qp.t[:, f:f + 2, :],
                                                bank.t[:, :].rearrange("p (k s) -> p k s", k=2),
                                                0.0, EPS0, ALU.max, ALU.add))
            bank.release(e_qp)
            if f == 2:
                yield
        qkT.release(e)
        yield
        bank, kv = work.take(), kv_b.take()
        wait(pe, e_kp, e_vx, *bank.free)
        for f in range(FC):
            for c in range(TC):
                e_kv = mark("pe_kv", pe.matmul(bank.t[:, f * KVW:(f + 1) * KVW], kp.t[:, c, f * P:(f + 1) * P],
                                               vx.t[:, c, f, :], start=(c == 0), stop=(c == TC - 1)))
        kp.release(e_kv)
        vx.release(e_kv)
        wait(dve, e_kv, *kv.free)
        e_kvm = mark("kvm", dve.tensor_tensor(kv.t[:, :, :], bank.t[:, 0:FC * KVW].rearrange("p (f w) -> p f w", f=FC),
                                              cst("kvmask").rearrange("p (f w) -> p f w", f=FC), ALU.mult))
        bank.release(e_kvm)
        yield
        bank, o, sm = work.take(), o_b.take(), sm_b.take()
        wait(pe, e_kvm, e_qp, *bank.free)
        for c in range(TC):
            for f in range(FC):
                at = c * S + f * KVW
                e = mark("pe_o0", pe.matmul(bank.t[:, at:at + KVW], qp.t[:, f, c * P:(c + 1) * P], kv.t[:, f, :],
                                            start=True, stop=True))
        qp.release(e)
        kv.release(e)
        wait(dve, e, *sm.free, *o.free)
        view = bank.t[:, :].rearrange("p (c n) -> p c n", c=TC)[:, :, 0:FC * KVW]\
            .rearrange("p c (f w) -> p c f w", w=KVW)
        for c in range(TC):
            e = mark("o0", dve.tensor_scalar(sm.t[:, c * H0:(c + 1) * H0].rearrange("p (f h) -> p f h", h=2),
                                             view[:, c, :, 2 * DK0:], EPS0, None, ALU.add))
        wait(dve, e)
        e = mark("o0", dve.reciprocal(sm.t[:, 0:TC * H0], sm.t[:, 0:TC * H0]))
        wait(dve, e)
        for c in range(TC):
            e_o = mark("o0", dve.tensor_tensor(
                o.t[:, c, :].rearrange("p (f h w) -> p f h w", h=2, w=DK0),
                view[:, c, :, 0:2 * DK0].rearrange("p f (h w) -> p f h w", h=2),
                sm.t[:, c * H0:(c + 1) * H0].rearrange("p (f h) -> p f h", h=2).unsqueeze(3)
                .to_broadcast([P, FC, 2, DK0]), ALU.mult))
        sm.release(e_o)
        bank.release(e_o)
        yield
        bank, oT = work.take(), oT_b.take()
        wait(pe, e_o, *bank.free)
        for c in range(TC):
            e = mark("pe_oT0", pe.transpose(bank.t[:, c * P:(c + 1) * P], o.t[:, c, :], ident))
        o.release(e)
        wait(act, e, *oT.free)
        e = mark("oT0", act.activation(oT.t[:, :], bank.t[:, 0:S], ACT.Copy))
        bank.release(e)
        yield
        bank = work.take()
        wait(pe, e, *bank.free)
        e = mark("pe_wo0", pe.matmul(bank.t[:, 0:S], w_o[:, :], oT.t[:, :], start=True, stop=True))
        wait(dve, e)
        e = mark("x1", dve.tensor_scalar(oT.t[:, :], bank.t[:, 0:S], col("bo"), mcol(0, 2, b), ALU.add, ALU.mult))
        bank.release(e)
        wait(dve, e)
        e_x = mark("x1", dve.tensor_tensor(x, x, oT.t[:, :], ALU.add))
        oT.release(e_x)
        yield

        lb, h = ln_buf.take(), h_buf.take()
        wait(dve, *lb.free)
        e_h = yield from layer_norm(x, [e_x], work, lb.t, mcol(0, 4, b), mcol(0, 3, b), h.t[:, :], h.free, "b")
        lb.release(e_h)
        bank, gt, ix = work.take(), gate_b.take(), idx_b.take()
        wait(pe, e_h, ev_moe, *bank.free)
        for c in range(TC):
            e = mark("pe_gate", pe.matmul(bank.t[:, c * NE:(c + 1) * NE], tok(h.t, c), w_gate[:, :],
                                          start=True, stop=True))
        LOG, TOP, IDX, COMB, TMP, SC = (slice(k * NE, (k + 1) * NE) for k in range(6))
        wait(dve, e, *gt.free, *ix.free)
        e = mark("gate", dve.tensor_copy(gt.t[:, :, LOG], bank.t[:, 0:TC * NE].rearrange("p (c n) -> p c n", c=TC)))
        bank.release(e)
        wait(dve, e)
        for c in range(TC):
            e = mark("gate", dve.max(gt.t[:, c, TOP], gt.t[:, c, LOG]))
            wait(dve, e)
            e = mark("gate", dve.max_index(ix.t[:, c, :], gt.t[:, c, TOP], gt.t[:, c, LOG]))
        wait(dve, e)
        e = mark("gate", dve.tensor_copy(gt.t[:, :, IDX], ix.t[:, :, :]))
        s0 = SC.start
        e_d = mark("gate", dve.tensor_tensor(gt.t[:, :, s0:s0 + 1], gt.t[:, :, NE + 1:NE + 2], gt.t[:, :, NE:NE + 1],
                                             ALU.subtract))
        ix.release(e_d)
        wait(act, e_d)
        e = mark("gate_exp", act.activation(gt.t[:, :, s0 + 1:s0 + 2], gt.t[:, :, s0:s0 + 1], ACT.Exp))
        yield
        wait(dve, e)
        e = mark("gate", dve.tensor_scalar(gt.t[:, :, s0 + 2:s0 + 3], gt.t[:, :, s0 + 1:s0 + 2], 1.0, None, ALU.add))
        wait(dve, e)
        e = mark("gate", dve.reciprocal(gt.t[:, :, s0 + 3:s0 + 4], gt.t[:, :, s0 + 2:s0 + 3]))
        wait(dve, e)
        e = mark("gate", dve.tensor_tensor(gt.t[:, :, s0 + 4:s0 + 5], gt.t[:, :, s0 + 3:s0 + 4],
                                           gt.t[:, :, s0 + 1:s0 + 2], ALU.mult))
        wait(dve, e)
        for c in range(TC):
            dve.tensor_scalar(gt.t[:, c, COMB], cst("iota"), gt.t[:, c, 2 * NE:2 * NE + 1],
                              gt.t[:, c, s0 + 3:s0 + 4], ALU.is_equal, ALU.mult)
            e = mark("gate", dve.tensor_scalar(gt.t[:, c, TMP], cst("iota"), gt.t[:, c, 2 * NE + 1:2 * NE + 2],
                                               gt.t[:, c, s0 + 4:s0 + 5], ALU.is_equal, ALU.mult))
        wait(dve, e)
        e_comb = mark("gate", dve.tensor_tensor(gt.t[:, :, COMB], gt.t[:, :, COMB], gt.t[:, :, TMP], ALU.add))
        bank, cT, acc = work.take(), cT_b.take(), acc_b.take()
        wait(pe, e_comb, *bank.free)
        for c in range(TC):
            e = mark("pe_cT", pe.transpose(bank.t[0:NE, c * P:(c + 1) * P], gt.t[:, c, COMB], ident))
        wait(dve, e, *cT.free)
        e = mark("gate", dve.tensor_copy(cT.t[:, :], bank.t[0:NE, 0:S]))
        bank.release(e)
        yield
        bank = work.take()
        wait(pe, e, *bank.free)
        for c in range(TC):
            e = mark("pe_bout", pe.matmul(bank.t[:, c * D:(c + 1) * D], cT.t[:, c * P:(c + 1) * P], b_out[:, :],
                                          start=True, stop=True))
        cT.release(e)
        wait(dve, e, *acc.free)
        e_acc = mark("acc", dve.tensor_copy(acc.t[:, :, :], bank.t[:, 0:TC * D].rearrange("p (c n) -> p c n", c=TC)))
        bank.release(e_acc)
        hidden = {}
        for ex in range(NE + 1):
            if ex < NE:
                hd = hid.take()
                wait(act, *hd.free)
                for m in range(0, MC, 2):
                    bank = hid_banks.take()
                    wait(pe, *bank.free)
                    for k in range(2):
                        e = mark("pe_hid", pe.matmul(bank.t[:, k * S:(k + 1) * S],
                                                     w_in[:, ex, (m + k) * P:(m + k + 1) * P], h.t[:, :],
                                                     start=True, stop=True))
                    wait(act, e)
                    for k in range(2):
                        e_hd = mark("hid", act.activation(hd.t[:, m + k, :], bank.t[:, k * S:(k + 1) * S], ACT.Gelu,
                                                          bias=col("b_in", ex * MC + m + k)))
                    bank.release(e_hd)
                hidden[ex] = hd, e_hd
                if ex == NE - 1:
                    h.release(e)
            if ex > 0:
                hd, e_hd = hidden.pop(ex - 1)
                bank = y_banks.take()
                wait(pe, e_hd, *bank.free)
                for c in range(TC):
                    for m in range(MC):
                        e = mark("pe_y", pe.matmul(bank.t[:, c * D:(c + 1) * D], hd.t[:, m, c * P:(c + 1) * P],
                                                   w_out[:, ex - 1, m, :], start=(m == 0), stop=(m == MC - 1)))
                hd.release(e)
                wait(dve, e, e_acc)
                for c in range(TC):
                    e_acc = mark("acc", dve.scalar_tensor_tensor(
                        out=acc.t[:, c, :], in0=bank.t[:, c * D:(c + 1) * D],
                        scalar=gt.t[:, c, COMB.start + ex - 1:COMB.start + ex], in1=acc.t[:, c, :],
                        op0=ALU.mult, op1=ALU.add))
                bank.release(e_acc)
            yield
        gt.release(e_acc)
        bank = work.take()
        wait(pe, e_acc, *bank.free)
        for c in range(TC):
            e = mark("pe_accT", pe.transpose(bank.t[:, c * P:(c + 1) * P], acc.t[:, c, :], ident))
        acc.release(e)
        wait(dve, e)
        e_x = mark("x2", dve.scalar_tensor_tensor(out=x, in0=bank.t[:, 0:S], scalar=mcol(0, 5, b), in1=x,
                                                  op0=ALU.mult, op1=ALU.add))
        bank.release(e_x)
        yield

        lb, h = ln_buf.take(), h_buf.take()
        wait(dve, *lb.free)
        e_h = yield from layer_norm(x, [e_x], work, lb.t, mcol(1, 1, b), mcol(1, 0, b), h.t[:, :], h.free, "c")
        lb.release(e_h)
        bank, hr = work.take(), hr_b.take()
        wait(pe, e_h, *bank.free)
        for c in range(TC):
            e = mark("pe_hr", pe.transpose(bank.t[:, c * P:(c + 1) * P], tok(h.t, c), ident))
        wait(act, e, *hr.free)
        e_hr = mark("hr", act.activation(hr.t[:, :, :], bank.t[:, 0:S].rearrange("p (c n) -> p c n", c=TC), ACT.Copy))
        bank.release(e_hr)
        bank, pr, sm = work.take(), prob_b.take(), sm_b.take()
        wait(pe, *bank.free)
        for c in range(TC):
            e = mark("pe_s1", pe.matmul(bank.t[:, c * S:(c + 1) * S], tok(h.t, c), h.t[:, :], start=True, stop=True))
        h.release(e)
        NM, SUM, RS, SPS, VAC = (slice(k * TC, (k + 1) * TC) for k in range(5))
        one = lambda s, c: sm.t[:, s.start + c:s.start + c + 1]
        scale = float(np.float32(1.0) / np.sqrt(np.float32(D)))
        wait(dve, e, *sm.free)
        e = mark("p1", dve.tensor_reduce(sm.t[:, NM], bank.t[:, :].rearrange("p (c s) -> p c s", c=TC), AX.X, ALU.max))
        wait(dve, e)
        e = mark("p1", dve.tensor_scalar(sm.t[:, NM], sm.t[:, NM], -scale, None, ALU.mult))
        yield
        wait(act, e, *pr.free)
        for c in range(TC):
            e = mark("exp1", act.activation(pr.t[:, c, :], bank.t[:, c * S:(c + 1) * S], ACT.Exp, bias=one(NM, c),
                                            scale=scale, accum_out=one(SUM, c)))
        bank.release(e)
        yield
        wait(dve, e)
        e = mark("p1", dve.reciprocal(sm.t[:, RS], sm.t[:, SUM]))
        wait(dve, e)
        spb = sp_b.take()
        for c in range(TC):
            e = mark("p1", dve.tensor_scalar(pr.t[:, c, :], pr.t[:, c, :], one(RS, c), None, ALU.mult))
        wait(dve, e, *spb.free)
        for c in range(TC):
            e = mark("p1", dve.scalar_tensor_tensor(out=spb.t[:, c, :], in0=pr.t[:, c, :], scalar=THRESH,
                                                    in1=pr.t[:, c, :], op0=ALU.is_lt, op1=ALU.mult,
                                                    accum_out=one(VAC, c)))
            wait(dve, e)
            e = mark("p1", dve.scalar_tensor_tensor(out=spb.t[:, c, :], in0=pr.t[:, c, :], scalar=THRESH,
                                                    in1=pr.t[:, c, :], op0=ALU.is_ge, op1=ALU.mult,
                                                    accum_out=one(SPS, c)))
        e_sp = e
        pr.release(e)
        wait(dve, e)
        e = mark("p1", dve.tensor_scalar(sm.t[:, SPS], sm.t[:, SPS], 1e-9, None, ALU.add))
        wait(dve, e)
        e = mark("p1", dve.reciprocal(sm.t[:, SPS], sm.t[:, SPS]))
        e = mark("p1", dve.tensor_scalar(sm.t[:, VAC], sm.t[:, VAC], 0.01, None, ALU.mult))
        e_sm = e
        yield
        bank, spT = work.take(), spT_b.take()
        wait(pe, e_sp, *bank.free)
        for k in range(TC):
            for c in range(TC):
                e = mark("pe_spT", pe.transpose(bank.t[:, k * S + c * P:k * S + (c + 1) * P],
                                                spb.t[:, c, k * P:(k + 1) * P], ident))
        spb.release(e)
        wait(act, e, *spT.free)
        e = mark("spT", act.activation(spT.t[:, :, :], bank.t[:, :].rearrange("p (k s) -> p k s", k=TC), ACT.Copy))
        bank.release(e)
        yield
        bank, o = work.take(), o_b.take()
        wait(pe, e, e_hr, *bank.free)
        for c in range(TC):
            for k in range(TC):
                e = mark("pe_at1", pe.matmul(bank.t[:, c * D:(c + 1) * D], spT.t[:, k, c * P:(c + 1) * P],
                                             hr.t[:, k, :], start=(k == 0), stop=(k == TC - 1)))
        spT.release(e)
        hr.release(e)
        wait(dve, e, e_sm, e_wsum, *o.free)
        for c in range(TC):
            e = mark("at1", dve.tensor_scalar(o.t[:, c, :], bank.t[:, c * D:(c + 1) * D], one(SPS, c), None, ALU.mult))
        bank.release(e)
        wait(dve, e)
        for c in range(TC):
            e = mark("at1", dve.scalar_tensor_tensor(out=o.t[:, c, :], in0=wsum[:, :], scalar=one(VAC, c),
                                                     in1=o.t[:, c, :], op0=ALU.mult, op1=ALU.add))
        sm.release(e)
        yield
        bank = work.take()
        wait(pe, e, *bank.free)
        for c in range(TC):
            e = mark("pe_atT", pe.transpose(bank.t[:, c * P:(c + 1) * P], o.t[:, c, :], ident))
        o.release(e)
        wait(dve, e)
        e_x = mark("x3", dve.scalar_tensor_tensor(out=x, in0=bank.t[:, 0:S], scalar=mcol(1, 2, b), in1=x,
                                                  op0=ALU.mult, op1=ALU.add))
        bank.release(e_x)
        yield
        lb = ln_buf.take()
        wait(dve, *lb.free)
        e = yield from layer_norm(x, [e_x], work, lb.t, mcol(1, 4, b), mcol(1, 3, b), zT[:, b * S:(b + 1) * S], (), "d")
        lb.release(e)
        early_done.append(e)

    early_done = []
    interleave([lambda b=b: early_unit(b) for b in range(B)], EARLY_SPACING)

    everything = [sg.last[s] for s in sg.last if not s.startswith("ld_")] + [ev_rows]
    for engine in (pe, dve, act, pool, sp):
        wait(engine, *everything)
    early.close()

    proj_banks = Ring(banks[0:2])
    tr_banks = Ring(banks[2:4])
    s_banks = Ring([banks[4:6]])
    o_banks = Ring([banks[6:8]])

    xs_r = sb_ring("xs", 3, [P, S])
    raw_r = sb_ring("raw", 2, [P, 2 * INNER])
    rt_r = sb_ring("rt", 2, [P, 2 * INNER])
    t2_r = sb_ring("t2", 1, [P, 2 * INNER])
    rn_r = sb_ring("rn", 3, [P, TC, 2 * HEADS])
    qT_r = sb_ring("qT", 3, [P, HP, P])
    kT_r = sb_ring("kT", 2, [P, HP, WIN + S])
    vn_r = sb_ring("vn", 2, [P, INNER])
    v2_r = sb_ring("v2", 3, [P, NW, HP * DH])
    p_r = sb_ring("p", 2, [P, HP, 2, 2 * WIN])
    pT_r = sb_ring("pT", 2, [P, HP, P])
    sm_r = sb_ring("sm", 2, [P, 4, HEADS])
    oa_r = sb_ring("oa", 1, [P, HP, 2, DH])
    oT_r = sb_ring("oT", 1, [P, INNER // P, S])
    xf_r = sb_ring("xf", 2, [P, S])
    lnf_r = sb_ring("lnf", 1, [P, 2, S])
    hn_r = sb_ring("hn", 1, [P, S])
    g_r = sb_ring("g", 2, [P, S])
    hh_r = sb_ring("hh", 1, [P, len(DIC), S])

    for r in (xs_r, xf_r):
        for t in r.bufs:
            e_z = mark_pool("zpad", pool.memset(t[DH:P, 0:1], 0.0))
    for t in kT_r.bufs:
        e_z = mark_pool("zpad", pool.memset(t[:, :, 0:WIN], 0.0))
    for t in v2_r.bufs:
        e_z = mark_pool("zpad", pool.memset(t[:, 0, :], 0.0))

    z_ready = {b: early_done[b] for b in range(B)}
    tables = {}

    def layer_tables(l):
        slot = rot.take()
        src = cst("rot").rearrange("p (c k d) -> p c k d", c=TC, k=4)
        gn, e_gain = layer_w[l]["gain"]
        wait(dve, e_gain, *slot.free)
        for k in range(4):
            g = gn.t[:, k // 2, :].rearrange("p (h d) -> p h d", h=2)
            if k % 2:
                g = g[:, ::-1, :]
            for c in range(TC):
                e = mark("tables", dve.tensor_tensor(
                    slot.t[:, c, k, :].rearrange("p (h d) -> p h d", h=2),
                    src[:, c, k, :].rearrange("p (h d) -> p h d", h=2), g, ALU.mult))
        gn.release(e)
        tables[l] = slot, e

    def shifted(dst, src, ready):
        wait(pool, ready, e_z, *dst.free)
        mark_pool("shift", pool.tensor_copy(dst.t[0:DH, :], src[0:DH, :]))
        return mark_pool("shift", pool.tensor_copy(dst.t[DH:P, 1:S], src[DH:P, 0:S - 1]))

    def unit(l, b):
        z = zT[:, b * S:(b + 1) * S]
        if b == 0:
            layer_tables(l)
        if b == 2 and l + 1 < DEPTH:
            load_projections(l + 1)
        w_qk, e_wqk = layer_w[l]["qk"]
        w_val, e_wv = layer_w[l]["v"]
        tab, e_tab = tables[l]
        tok = lambda t, c: t[:, c * P:(c + 1) * P]
        last_of_layer = b == B - 1

        xs = xs_r.take()
        e_xs = shifted(xs, z, z_ready[b])
        rn = rn_r.take()
        raws, rts, e_rot = [], [], []

        def rotate(c):
            raw, e_raw = raws[c]
            rt, t2 = rt_r.take(), t2_r.take()
            rts.append(rt)
            wait(dve, e_raw, e_tab, *rt.free, *t2.free)
            for k in range(2):
                cosv = tab.t[:, c, 2 * k, :].unsqueeze(1).to_broadcast([P, HEADS, DH])
                sinv = tab.t[:, c, 2 * k + 1, :].rearrange("p (h d) -> p h d", h=2).unsqueeze(1)\
                    .to_broadcast([P, HEADS, 2, DH // 2])
                part = slice(k * INNER, (k + 1) * INNER)
                e_c = mark("rot", dve.tensor_tensor(rt.t[:, part].rearrange("p (n d) -> p n d", d=DH),
                                              raw.t[:, part].rearrange("p (n d) -> p n d", d=DH), cosv, ALU.mult))
                e_s = mark("rot", dve.tensor_tensor(
                    t2.t[:, part].rearrange("p (n h d) -> p n h d", h=2, d=DH // 2),
                    raw.t[:, part].rearrange("p (n h d) -> p n h d", h=2, d=DH // 2)[:, :, ::-1, :], sinv, ALU.mult))
            wait(pool, e_s)
            e = mark_pool("rot_add", pool.tensor_tensor(rt.t[:, :], rt.t[:, :], t2.t[:, :], ALU.add))
            raw.release(e_s)
            t2.release(e)
            e_rot.append(e)
            return e_s

        def square_sums(c):
            raw, e_raw = raws[c]
            t2 = t2_r.take()
            wait(act, e_raw, *t2.free)
            e = mark("sq", act.activation(t2.t[:, :], raw.t[:, :], ACT.Square))
            wait(dve, e, *(rn.free if c == 0 else ()))
            e = mark("ss", dve.tensor_reduce(rn.t[:, c, :], t2.t[:, :].rearrange("p (n d) -> p n d", d=DH),
                                             AX.X, ALU.add))
            t2.release(e)
            return e

        for c in range(TC):
            raw = raw_r.take()
            for n in range(4):
                bank = proj_banks.take()
                wait(pe, e_xs, e_wqk, *bank.free)
                e = mark("pe_qk", pe.matmul(bank.t[:, :], tok(xs.t, c), w_qk.t[:, n * 512:(n + 1) * 512],
                                            start=True, stop=True))
                wait(act, e, *raw.free)
                e_raw = mark("raw", act.activation(raw.t[:, n * 512:(n + 1) * 512], bank.t[:, :], ACT.Copy))
                bank.release(e_raw)
                if c == 1 and n == 0:
                    square_sums(0)
                if c == 1 and n == 2:
                    rotate(0)
                if n < 3 or c == 0:
                    if n == 3:
                        raws.append((raw, e_raw))
                    yield
            if c == 1:
                raws.append((raw, e_raw))
        if last_of_layer:
            w_qk.release(e)
        yield

        e = square_sums(1)
        wait(act, e)
        e = mark("norm", act.activation(rn.t[:, :, :], rn.t[:, :, :], ACT.Sqrt))
        e_last = rotate(1)
        if last_of_layer:
            tab.release(e_last)
        wait(dve, e)
        e = mark("rn", dve.tensor_scalar(rn.t[:, :, :], rn.t[:, :, :], 1e-12, None, ALU.max))
        wait(dve, e)
        e_rn = mark("rn", dve.reciprocal(rn.t[:, :, :], rn.t[:, :, :]))

        def normalise(c):
            rt = rts[c]
            wait(dve, e_rn, e_rot[c])
            v = rt.t[:, :].rearrange("p (n d) -> p n d", d=DH)
            e_nrm[c] = mark("nrm", dve.tensor_tensor(v, v, rn.t[:, c, :].unsqueeze(2)
                                                     .to_broadcast([P, 2 * HEADS, DH]), ALU.mult))
            if c == TC - 1:
                rn.release(e_nrm[c])

        kT = None
        qTs, e_nrm = [None] * TC, [None] * TC
        vn, v2s, e_v2, e_vn = [None] * TC, [None] * TC, [None] * TC, [None] * TC

        def transpose_bank(c, k):
            nonlocal kT
            if c == 0 and k == 0:
                kT = kT_r.take()
            if k == 0:
                qTs[c] = qT_r.take()
            bank = tr_banks.take()
            wait(pe, e_nrm[c], *bank.free)
            for n in range(4):
                e = mark("pe_qkT", pe.transpose(bank.t[:, n * P:(n + 1) * P],
                                                rts[c].t[:, (4 * k + n) * P:(4 * k + n + 1) * P], ident))
            if k == 3:
                rts[c].release(e)
            src = bank.t[:, :].rearrange("p (n i) -> p n i", n=4)
            if k < 2:
                wait(act, e, *qTs[c].free)
                dst = qTs[c].t[:, 4 * k:4 * k + 4, :]
            else:
                wait(act, e, *(kT.free if c == 0 else ()))
                dst = kT.t[:, 4 * (k - 2):4 * (k - 2) + 4, WIN + c * P:WIN + (c + 1) * P]
            e_qkT[c] = mark("qkT", act.activation(dst, src, ACT.Copy))
            bank.release(e_qkT[c])

        def values(c, r):
            if r == 0:
                vn[c] = vn_r.take()
            bank = proj_banks.take()
            wait(pe, e_wv, *bank.free)
            e = mark("pe_v", pe.matmul(bank.t[:, :], tok(xs.t, c), w_val.t[:, r * 512:(r + 1) * 512],
                                       start=True, stop=True))
            wait(act, e, *vn[c].free)
            e_vn[c] = mark("vn", act.activation(vn[c].t[:, r * 512:(r + 1) * 512], bank.t[:, :], ACT.Copy))
            bank.release(e_vn[c])
            if c == TC - 1 and r == 1:
                xs.release(e)
                if last_of_layer:
                    w_val.release(e)

        def pair_values(c):
            v2s[c] = v2_r.take()
            k = v2s[c].k
            wait(sp, e_vn[c], e_z, *v2s[c].free)
            for g in range(NW):
                for half in range(2):
                    v = NW * c + g - 1 + half
                    if v < 0:
                        continue
                    src = vn[v // NW].t[WIN * (v % NW):WIN * (v % NW + 1), :]
                    for r in range(2):
                        at = 2 * WIN * r + WIN * half
                        e = sg.dma(f"v2_{k}", sp.dma_start(v2s[c].t[at:at + WIN, g, :],
                                                           src[:, r * 512:(r + 1) * 512]))
            e_v2[c] = e
            if c == TC - 1:
                vn[0].release(e_v2[0], e)
                vn[1].release(e)

        ps, e_soft, sms = [None] * TC, [None] * TC, [None] * TC
        e_qkT, e_sum = [None] * TC, [None] * TC
        sbk = obk = None

        def scores(c, g):
            nonlocal sbk
            if g == 0:
                sbk = s_banks.take()
                wait(pe, e_cst, e_qkT[c], *sbk.free)
                for r in range(2):
                    pe.matmul(sbk.t[r][:, :], ident_b[:, :], mask_b[:, min(c, 1), :, :].rearrange("p h j -> p (h j)"),
                              start=True, stop=False, skip_group_check=True)
            for hp in range(HP):
                for r in range(2):
                    rows = slice(2 * WIN * r, 2 * WIN * (r + 1))
                    k0 = c * P + g * WIN
                    e = pe.matmul(sbk.t[r][WIN * g:WIN * (g + 1), hp * 2 * WIN:(hp + 1) * 2 * WIN],
                                  qTs[c].t[rows, hp, WIN * g:WIN * (g + 1)], kT.t[rows, hp, k0:k0 + 2 * WIN],
                                  start=False, stop=True, skip_group_check=True)
            if g == NW - 1:
                e = mark("pe_s", e)
                qTs[c].release(e)
                if c == TC - 1:
                    kT.release(e)
                softmax_in(c, e)

        def softmax_in(c, e_s):
            pb, sm = p_r.take(), sm_r.take()
            ps[c], sms[c] = pb, sm
            wait(dve, e_s, *sm.free, *pb.free)
            for r in range(2):
                e_m = mark("smax", dve.tensor_reduce(sm.t[:, r, 0:HP], sbk.t[r][:, :].rearrange("p (h j) -> p h j", h=HP),
                                               AX.X, ALU.max))
            wait(dve, e_m)
            for r in range(2):
                e = mark("smax", dve.tensor_tensor(pb.t[:, :, r, :], sbk.t[r][:, :].rearrange("p (h j) -> p h j", h=HP),
                                                   sm.t[:, r, 0:HP].unsqueeze(2).to_broadcast([P, HP, 2 * WIN]),
                                                   ALU.subtract))
            sbk.release(e)
            wait(act, e)
            e_soft[c] = mark("exp", act.activation(pb.t[:, :, :, :], pb.t[:, :, :, :], ACT.Exp))

        def softmax_sum(c):
            pb, sm = ps[c], sms[c]
            wait(dve, e_soft[c])
            e = mark("ssum", dve.tensor_reduce(sm.t[:, 2, :].rearrange("p (h r) -> p h r", r=2), pb.t[:, :, :, :],
                                               AX.X, ALU.add))
            wait(dve, e)
            e_sum[c] = mark("ssum", dve.reciprocal(sm.t[:, 3, :], sm.t[:, 2, :]))

        oT = None
        pTs = [None] * TC
        e_pT = [None] * TC
        oas, e_oa, e_oT = [None] * TC, [None] * TC, [None] * TC

        def transpose_p(c, k):
            if k == 0:
                pTs[c] = pT_r.take()
            bank = tr_banks.take()
            wait(pe, e_soft[c], *bank.free)
            for n in range(4):
                hp = 4 * k + n
                e = mark("pe_pT", pe.transpose(bank.t[:, n * P:(n + 1) * P],
                                               ps[c].t[:, hp, :, :].rearrange("p r j -> p (r j)"), ident))
            wait(act, e, *pTs[c].free)
            e_pT[c] = mark("pT", act.activation(pTs[c].t[:, 4 * k:4 * k + 4, :],
                                                bank.t[:, :].rearrange("p (n i) -> p n i", n=4), ACT.Copy))
            bank.release(e_pT[c])
            if k == 1:
                ps[c].release(e, e_sum[c])

        def attend(c, g):
            nonlocal obk
            if g == 0:
                obk = o_banks.take()
                wait(pe, e_pT[c], e_v2[c], *obk.free)
            for hp in range(HP):
                for r in range(2):
                    rows = slice(2 * WIN * r, 2 * WIN * (r + 1))
                    e = pe.matmul(obk.t[r][WIN * g:WIN * (g + 1), hp * DH:(hp + 1) * DH],
                                  pTs[c].t[rows, hp, WIN * g:WIN * (g + 1)],
                                  v2s[c].t[rows, g, hp * DH:(hp + 1) * DH], start=True, stop=True)
            if g == NW - 1:
                attended(c, mark("pe_o", e))

        def attended(c, e):
            pTs[c].release(e)
            v2s[c].release(e)
            oas[c] = oa_r.take()
            wait(dve, e, e_sum[c], *oas[c].free)
            for r in range(2):
                e_oa[c] = mark("oa", dve.tensor_tensor(
                    oas[c].t[:, :, r, :], obk.t[r][:, :].rearrange("p (h e) -> p h e", h=HP),
                    sms[c].t[:, 3, :].rearrange("p (h r) -> p h r", r=2)[:, :, r:r + 1].to_broadcast([P, HP, DH]), ALU.mult))
            obk.release(e_oa[c])
            sms[c].release(e_oa[c])

        def transpose_o(c, k):
            nonlocal oT
            if c == 0 and k == 0:
                oT = oT_r.take()
            bank = tr_banks.take()
            wait(pe, e_oa[c], *bank.free)
            for n in range(4):
                e = mark("pe_oT", pe.transpose(bank.t[:, n * P:(n + 1) * P],
                                               oas[c].t[:, 4 * k + n, :, :].rearrange("p r e -> p (r e)"), ident))
            if k == 1:
                oas[c].release(e)
            wait(act, e, *oT.free)
            e_oT[c] = mark("oT", act.activation(oT.t[:, 4 * k:4 * k + 4, c * P:(c + 1) * P],
                                                bank.t[:, :].rearrange("p (n i) -> p n i", n=4), ACT.Copy))
            bank.release(e_oT[c])

        plan = {8: [], 9: [(normalise, 0), (values, 0, 0)], 10: [], 11: [(normalise, 1), (values, 0, 1)],
                12: [(pair_values, 0)], 13: [(values, 1, 0)], 14: [], 15: [(values, 1, 1), (pair_values, 1)]}
        plan |= {n: [] for n in range(16, 29)}
        for k in range(4):
            plan[10 + k].append((transpose_bank, 0, k))
            plan[12 + k].append((transpose_bank, 1, k))
        for g in range(NW):
            plan[14 + g].append((scores, 0, g))
            plan[18 + g].append((scores, 1, g))
            plan[20 + g].append((attend, 0, g))
            plan[24 + g].append((attend, 1, g))
        plan[19].append((softmax_sum, 0))
        plan[23].insert(0, (softmax_sum, 1))
        for k in range(2):
            plan[20].insert(0, (transpose_p, 0, 1 - k))
            plan[24].insert(0, (transpose_p, 1, 1 - k))
            plan[26].append((transpose_o, 0, k))
            plan[28].append((transpose_o, 1, k))
        for n in range(8, 29):
            for step, *args in plan[n]:
                step(*args)
            yield

        w_out_l, e_wo = layer_w[l]["o"]
        bank = proj_banks.take()
        wait(pe, e_oT[0], e_oT[1], e_wo, *bank.free)
        for k in range(INNER // P):
            e = mark("pe_wo", pe.matmul(bank.t[:, 0:S], w_out_l.t[:, k, :], oT.t[:, k, :],
                                        start=(k == 0), stop=(k == INNER // P - 1)))
        oT.release(e)
        if last_of_layer:
            w_out_l.release(e)
            if l + 1 < DEPTH:
                load_output(l + 1)
        wait(dve, e)
        e_z1 = mark("z_mid", dve.tensor_tensor(z, z, bank.t[:, 0:S], ALU.add))
        bank.release(e_z1)
        xf = xf_r.take()
        e_xf = shifted(xf, z, e_z1)
        yield
        yield
        lb, hn = lnf_r.take(), hn_r.take()
        wait(dve, *lb.free)
        e_hn = yield from layer_norm(xf.t[:, :], [e_xf], proj_banks, lb.t, col("ln_g", l), col("ln_b", l), hn.t[:, :],
                                     hn.free, "f")
        lb.release(e_hn)
        xf.release(e_hn)
        yield
        (w_up, e_w1ld), (w_dn, e_w2ld) = layer_w[l]["w1"], layer_w[l]["w2"]
        hh = hh_r.take()
        for j, (at, n) in enumerate(DIC):
            bank, g = proj_banks.take(), g_r.take()
            wait(pe, e_hn, e_w1ld, *bank.free)
            pe.matmul(bank.t[0:n, 0:S], w_up.t[:, at:at + n], hn.t[:, :], start=True, stop=True)
            e_w1 = mark("pe_w1", pe.matmul(bank.t[0:n, S:2 * S], w_up.t[:, DI + at:DI + at + n], hn.t[:, :],
                                           start=True, stop=True))
            wait(act, e_w1, *g.free)
            e = mark("gelu", act.activation(g.t[0:n, :], bank.t[0:n, S:2 * S], ACT.Gelu,
                                            bias=col("b1", (len(DIC) + j) * DEPTH + l, n)))
            wait(dve, e, *(hh.free if j == 0 else ()))
            e_hh = mark("hh", dve.scalar_tensor_tensor(out=hh.t[0:n, j, :], in0=bank.t[0:n, 0:S],
                                                       scalar=col("b1", j * DEPTH + l, n), in1=g.t[0:n, :],
                                                       op0=ALU.add, op1=ALU.mult))
            g.release(e_hh)
            bank.release(e_hh)
            yield
        hn.release(e_w1)
        bank = proj_banks.take()
        wait(pe, e_hh, e_w2ld, *bank.free)
        for j, (at, n) in enumerate(DIC):
            e = mark("pe_w2", pe.matmul(bank.t[:, 0:S], w_dn.t[0:n, j, :], hh.t[0:n, j, :],
                                        start=(j == 0), stop=(j == len(DIC) - 1)))
        hh.release(e)
        if last_of_layer:
            w_up.release(e_w1)
            w_dn.release(e)
            if l + 1 < DEPTH:
                load_ffn(l + 1)
        wait(dve, e, e_xf)
        e = mark("z_out", dve.scalar_tensor_tensor(out=z, in0=bank.t[:, 0:S], scalar=col("b2", l), in1=z,
                                                   op0=ALU.add, op1=ALU.add))
        bank.release(e)
        z_ready[b] = e

    interleave([lambda l=l, b=b: unit(l, b) for l in range(DEPTH) for b in range(B)], LATE_SPACING)

    orow = [raw_r.bufs[k % 2][:, (k // 2) * 512:(k // 2 + 1) * 512] for k in range(4)]
    for q in range(NT // 512):
        for b in (2 * q, 2 * q + 1):
            x, z = xT[:, b * S:(b + 1) * S], zT[:, b * S:(b + 1) * S]
            wait(dve, z_ready[b])
            e = mark("final", dve.scalar_tensor_tensor(out=z, in0=z, scalar=mcol(1, 5, b), in1=x,
                                                       op0=ALU.mult, op1=ALU.add))
        bank = tr_banks.take()
        wait(pe, e, *bank.free)
        for k in range(4):
            e = mark("pe_out", pe.transpose(bank.t[:, k * P:(k + 1) * P],
                                            zT[:, q * 512 + k * P:q * 512 + (k + 1) * P], ident))
        wait(act, e)
        e = mark("out_rows", act.activation(orow[q], bank.t[:, :], ACT.Copy))
        bank.release(e)
        wait(sp, e)
        e_out = sg.dma("st_out", sp.dma_start(
            out.rearrange("b (c p) d -> p (b c) d", p=P)[:, 4 * q:4 * q + 4, :],
            orow[q].rearrange("p (k d) -> p k d", k=4)))
    wait(sp, e_out)
    ctx.close()


EARLY_SPACING = 10
LATE_SPACING = 8

_INS = ["L0_attn_x", "L0_attn_Wq", "L0_attn_bq", "L0_attn_Wk", "L0_attn_bk", "L0_attn_Wv", "L0_attn_bv",
        "L0_attn_Wo", "L0_attn_bo", "L0_attn_rw", "L0_ffn_W_gate", "L0_ffn_W_in", "L0_ffn_b_in", "L0_ffn_W_out",
        "L0_ffn_b_out", "L0_c", "L0_wmod", "L1_attn_W", "L1_ffn_Wqkv", "L1_ffn_q_scale", "L1_ffn_k_scale",
        "L1_ffn_Wo", "L1_ffn_ln_g", "L1_ffn_ln_b", "L1_ffn_W1", "L1_ffn_b1", "L1_ffn_W2", "L1_ffn_b2", "L1_c",
        "L1_wmod"]


def kernel(**inputs):
    import concourse.bacc as _bacc
    from concourse.bass_utils import run_bass_kernel_spmd as _run

    nc = _bacc.Bacc("TRN2", target_bir_lowering=False, num_devices=1)
    arrays, aps = {}, {}
    for name in _INS:
        arr = np.ascontiguousarray(inputs[name])
        arrays[f"in_{name}_dram"] = arr
        aps[name] = nc.dram_tensor(f"in_{name}_dram", arr.shape, mybir.dt.from_np(arr.dtype),
                                   kind="ExternalInput").ap()
    arrays["const_dram"] = constants()
    aps["const"] = nc.dram_tensor("const_dram", (P, NCONST), F32, kind="ExternalInput").ap()
    out = nc.dram_tensor("out_dram", (B, S, D), F32, kind="ExternalOutput").ap()
    build(nc, aps, out)
    r = _run(nc, [arrays], core_ids=[0])
    return r.results[0]["out_dram"]
```

```python
from contextlib import ExitStack

import numpy as np

import concourse.bass as bass
from concourse import mybir

F32 = mybir.dt.float32
BF16 = mybir.dt.bfloat16
U32 = mybir.dt.uint32
ALU = mybir.AluOpType
ACT = mybir.ActivationFunctionType
AX = mybir.AxisListType

P = 128
D = 128
B, S = 8, 256
NT = B * S
TC = S // P
H0, DK0, F0 = 16, 8, 64
NF = H0 * F0
FC = NF // P
KVW = 2 * DK0 + 2
EPS0 = 1e-6
NE, DM = 8, 512
MC = DM // P
THRESH = 0.01
DEPTH, HEADS, DH, WIN = 6, 16, 64, 32
INNER = HEADS * DH
DI = int(D * 4 * 2 / 3)
DIC = [(j * P, min(P, DI - j * P)) for j in range((DI + P - 1) // P)]
QK_SCALE = 8.0
HP = HEADS // 2
NW = P // WIN
LN_EPS = 1e-5
NEG = -1.0e30

ROWS = {}
for _name, _n in (("bq", 1), ("bk", 1), ("bo", 1), ("b_in", NE * MC), ("ln_g", DEPTH), ("ln_b", DEPTH),
                  ("b2", DEPTH), ("b1", DEPTH * 2 * len(DIC)), ("c0", B), ("c1", B)):
    ROWS[_name] = sum(n for _, n in ROWS.values()), _n
NROWS = sum(n for _, n in ROWS.values())
CONST = {}
for _name, _n in (("ident", P), ("rot", TC * 4 * DH), ("kvmask", FC * KVW), ("iota", NE), ("mask", 2 * 2 * WIN)):
    CONST[_name] = sum(n for _, n in CONST.values()), _n
NCONST = sum(n for _, n in CONST.values())
KEPT = CONST["kvmask"][0]


def constants():
    out = np.zeros((P, NCONST), np.float32)

    def put(name, a):
        at, n = CONST[name]
        out[:, at:at + n] = a.reshape(P, n)

    put("ident", np.eye(P, dtype=np.float32))
    f = np.float32
    half = np.arange(0, DH, 2, dtype=f)
    inv_freq = (f(1.0) / np.power(f(10000.0), half / f(DH))).astype(f)
    t = np.arange(S, dtype=f)
    freqs = t[:, None] * inv_freq[None, :]
    base = (half + f(0.4 * DH)) / f(1.4 * DH)
    power = (t - f(S // 2)) / f(WIN // 2)
    scale = np.power(base[None, :], power[:, None]).astype(f)
    cos, sin = np.cos(freqs).astype(f), np.sin(freqs).astype(f)
    two = lambda a, b: np.concatenate([a, b], -1)
    q_cos = two(cos * scale, cos * scale) * f(QK_SCALE)
    q_sin = two(-sin * scale, sin * scale) * f(QK_SCALE)
    inv = f(1.0) / scale
    k_cos = two(cos * inv, cos * inv)
    k_sin = two(-sin * inv, sin * inv)
    rot = np.stack([q_cos, q_sin, k_cos, k_sin], 1)
    put("rot", rot.reshape(TC, P, 4, DH).transpose(1, 0, 2, 3))
    m = np.zeros((P, FC, KVW), f)
    for h in range(2):
        m[h * F0:(h + 1) * F0, :, h * DK0:(h + 1) * DK0] = 1
        m[h * F0:(h + 1) * F0, :, 2 * DK0 + h] = 1
    put("kvmask", m)
    put("iota", np.tile(np.arange(NE, dtype=f), (P, 1)))
    i, j = (np.arange(P) % WIN)[:, None], np.arange(2 * WIN)[None, :]
    bad = (j < i) | (j > i + WIN)
    first = bad | ((np.arange(P)[:, None] < WIN) & (j < WIN))
    put("mask", np.stack([np.where(first, f(NEG), f(0)), np.where(bad, f(NEG), f(0))], 1))
    return out


class Signals:

    def __init__(self, nc, ctx):
        self.nc, self.ctx = nc, ctx
        self.sems, self.count, self.seen, self.last = {}, {}, {}, {}

    def mark(self, stage, instruction, by=1):
        if stage not in self.sems:
            self.sems[stage] = self.ctx.enter_context(self.nc.semaphore("s_" + stage))
            self.count[stage] = 0
        self.count[stage] += by
        instruction.then_inc(self.sems[stage], by)
        self.last[stage] = (stage, self.count[stage])
        return self.last[stage]

    def dma(self, stage, instruction):
        return self.mark(stage, instruction, 16)

    def wait(self, engine, *events):
        for stage, value in events:
            key = (id(engine), stage)
            if self.seen.get(key, 0) < value:
                self.seen[key] = value
                engine.wait_ge(self.sems[stage], value)


class Slot:
    def __init__(self, ring, k):
        self.ring, self.k, self.t, self.free = ring, k, ring.bufs[k], ring.freed[k]

    def release(self, *events):
        self.ring.freed[self.k] = events
        self.ring.idle.append(self.k)


class Ring:

    def __init__(self, bufs):
        self.bufs, self.freed = bufs, [()] * len(bufs)
        self.idle = list(range(len(bufs)))

    def take(self):
        assert self.idle, "a buffer is taken before its last user is done with it"
        return Slot(self, self.idle.pop(0))


def interleave(units, spacing):
    live, n = [], 0
    slot = 0
    while live or n < len(units):
        if n < len(units) and slot >= n * spacing:
            live.append(units[n]())
            n += 1
        for g in list(live):
            try:
                next(g)
            except StopIteration:
                live.remove(g)
        slot += 1


def build(nc, a, out):
    ctx = ExitStack()
    sg = Signals(nc, ctx)
    mark, wait = sg.mark, sg.wait
    pe, dve, act, pool, sp = nc.tensor, nc.vector, nc.scalar, nc.gpsimd, nc.sync

    def mark_pool(stage, instruction):
        e = mark(stage, instruction)
        wait(pool, e)
        return e

    def sb(name, shape, dt=F32, where=ctx):
        return where.enter_context(nc.sbuf_tensor(name, shape, dt))

    def sb_ring(name, n, shape, dt=F32, where=ctx):
        return Ring([sb(f"{name}{k}", shape, dt, where) for k in range(n)])

    banks = [ctx.enter_context(nc.psum_tensor(f"bank{k}", [P, 512], F32)) for k in range(8)]

    xT = sb("xT", [P, NT])
    zT = sb("zT", [P, NT])
    const = sb("const", [P, KEPT])
    ones_d = sb("ones_d", [P, P])
    eps_ln = sb("eps_ln", [P, 1])
    ident_b = sb("ident_b", [P, P], BF16)
    mask_b = sb("mask_b", [P, 2, HP, 2 * WIN], BF16)
    cols = sb("cols", [P, NROWS])
    mod = [sb(f"mod{k}", [P, 6, B]) for k in range(2)]
    wqk = sb_ring("wqk", 2, [P, 2 * INNER])
    wv = sb_ring("wv", 2, [P, INNER])
    wo = sb_ring("wo", 1, [P, INNER // P, D])
    w1 = sb_ring("w1", 1, [P, 2 * DI])
    w2 = sb_ring("w2", 1, [P, len(DIC), D])
    rot = sb_ring("rot", 2, [P, TC, 4, DH])
    gain = sb_ring("gain", 2, [P, 2, DH])

    early = ExitStack()
    const_e = sb("const_e", [P, NCONST - KEPT], F32, early)

    def cst(name):
        at, n = CONST[name]
        return const[:, at:at + n] if at < KEPT else const_e[:, at - KEPT:at - KEPT + n]

    ident = cst("ident")

    def col(name, k=0, rows=P):
        at = ROWS[name][0] + k
        return cols[0:rows, at:at + 1]

    def mcol(block, k, b):
        return mod[block][:, k, b:b + 1]

    def esb(name, shape, dt=F32):
        return sb(name, shape, dt, early)

    rows_m = esb("rows_m", [P, P])
    e_zero = mark("zero", dve.memset(rows_m[:, :], 0.0))
    x_rows = esb("x_rows", [P, NT // P, D])
    sg.dma("ld_const", sp.dma_start(const[:, :], a["const"][:, 0:KEPT]))
    ev_const = sg.dma("ld_const", sp.dma_start(const_e[:, :], a["const"][:, KEPT:]))
    xr = a["L0_attn_x"].rearrange("b (c p) d -> p (b c) d", p=P)
    ev_x = [sg.dma(f"ld_x{q}", sp.dma_start(x_rows[:, 4 * q:4 * q + 4, :], xr[:, 4 * q:4 * q + 4, :]))
            for q in range(NT // P // 4)]
    wait(act, e_zero)

    def load_rows(name, src, n, k=0, width=P):
        at = ROWS[name][0] + k
        return sg.dma("ld_rows", act.dma_start(rows_m[at:at + n, 0:width], src))

    one_row = lambda v: v.rearrange("(o n) -> o n", o=1)
    load_rows("bq", one_row(a["L0_attn_bq"]), 1)
    load_rows("bk", one_row(a["L0_attn_bk"]), 1)
    load_rows("bo", one_row(a["L0_attn_bo"]), 1)
    load_rows("b_in", a["L0_ffn_b_in"].rearrange("e (m p) -> (e m) p", p=P), NE * MC)
    load_rows("ln_g", a["L1_ffn_ln_g"], DEPTH)
    load_rows("ln_b", a["L1_ffn_ln_b"], DEPTH)
    load_rows("b2", a["L1_ffn_b2"], DEPTH)
    for part in range(2):
        for j, (at, n) in enumerate(DIC):
            k = (part * len(DIC) + j) * DEPTH
            load_rows("b1", a["L1_ffn_b1"][:, part * DI + at:part * DI + at + n], DEPTH, k, n)
    load_rows("c0", a["L0_c"], B)
    ev_rows = load_rows("c1", a["L1_c"], B)

    wmod = [esb(f"wmod{k}", [P, 6 * D]) for k in range(2)]
    w_q, w_k, w_v, w_o = (esb(n, [P, D]) for n in ("w_q", "w_k", "w_v", "w_o"))
    w_rf = esb("w_rf", [P, NF])
    bv_b = esb("bv_b", [P, D])
    w_gate = esb("w_gate", [P, NE])
    w_in = esb("w_in", [P, NE, DM])
    w_out = esb("w_out", [P, NE, MC, D])
    b_out = esb("b_out", [NE, D])
    w_c = esb("w_c", [P, D])
    ev_wmod = [sg.dma(f"ld_wmod{k}", sp.dma_start(wmod[k][:, :], a[f"L{k}_wmod"])) for k in range(2)]
    for t, n in ((w_q, "L0_attn_Wq"), (w_k, "L0_attn_Wk"), (w_v, "L0_attn_Wv"), (w_o, "L0_attn_Wo")):
        ev_w0 = sg.dma("ld_w0", sp.dma_start(t[:, :], a[n]))
    ev_w0 = sg.dma("ld_w0", sp.dma_start(bv_b[:, :], one_row(a["L0_attn_bv"]).to_broadcast([P, D])))
    e_rf0 = mark_pool("rf_zero", pool.memset(w_rf[:, :], 0.0))
    wait(act, e_rf0)
    for h in range(H0):
        ev_rf = sg.dma("ld_rf", act.dma_start(w_rf[h * DK0:(h + 1) * DK0, h * F0:(h + 1) * F0],
                                              a["L0_attn_rw"][h]))
    ev_moe = sg.dma("ld_moe", sp.dma_start(w_gate[:, :], a["L0_ffn_W_gate"]))
    ev_moe = sg.dma("ld_moe", sp.dma_start(b_out[:, :], a["L0_ffn_b_out"]))
    ev_moe = sg.dma("ld_moe", sp.dma_start(w_in[:, :, :], a["L0_ffn_W_in"].rearrange("e d m -> d e m")))
    for e in range(NE):
        ev_moe = sg.dma("ld_moe", sp.dma_start(w_out[:, e, :, :],
                                               a["L0_ffn_W_out"][e].rearrange("(m p) n -> p m n", p=P)))
    ev_wc = sg.dma("ld_wc", sp.dma_start(w_c[:, :], a["L1_attn_W"]))

    layer_w = {l: {} for l in range(DEPTH)}

    def take_weights(l, name, ring):
        slot = ring.take()
        wait(sp, *slot.free)
        return slot

    def load_projections(l):
        k, src = l % 2, a["L1_ffn_Wqkv"][l]
        slot = take_weights(l, "qk", wqk)
        layer_w[l]["qk"] = slot, sg.dma(f"ld_wqk{k}", sp.dma_start(slot.t[:, :], src[:, 0:2 * INNER]))
        slot = take_weights(l, "v", wv)
        vsrc = src[:, 2 * INNER:].rearrange("d (hp r e) -> d r hp e", r=2, e=DH)
        for r in range(2):
            vdst = slot.t[:, r * HP * DH:(r + 1) * HP * DH].rearrange("d (hp e) -> d hp e", e=DH)
            e = sg.dma(f"ld_wv{k}", sp.dma_start(vdst, vsrc[:, r, :, :]))
        layer_w[l]["v"] = slot, e
        slot = take_weights(l, "gain", gain)
        for j, n in enumerate(("q", "k")):
            e = sg.dma(f"ld_gain{k}", sp.dma_start(slot.t[:, j, :],
                                                   a[f"L1_ffn_{n}_scale"][l:l + 1, :].to_broadcast([P, DH])))
        layer_w[l]["gain"] = slot, e

    def load_output(l):
        slot = take_weights(l, "o", wo)
        layer_w[l]["o"] = slot, sg.dma("ld_wo", sp.dma_start(
            slot.t[:, :, :], a["L1_ffn_Wo"][l].rearrange("(c p) n -> p c n", p=P)))

    def load_ffn(l):
        slot = take_weights(l, "w1", w1)
        layer_w[l]["w1"] = slot, sg.dma("ld_w1", sp.dma_start(slot.t[:, :], a["L1_ffn_W1"][l]))
        slot = take_weights(l, "w2", w2)
        for j, (at, n) in enumerate(DIC):
            e = sg.dma("ld_w2", sp.dma_start(slot.t[0:n, j, :], a["L1_ffn_W2"][l][at:at + n, :]))
        layer_w[l]["w2"] = slot, e

    load_projections(0)
    load_output(0)
    load_ffn(0)

    e_ones = mark_pool("ones", pool.memset(ones_d[:, :], 1.0 / D))
    e_eps = mark_pool("ones", pool.memset(eps_ln[:, :], LN_EPS))
    wait(dve, ev_const)
    dve.tensor_copy(ident_b[:, :], ident)
    mview = cst("mask").rearrange("p (k j) -> p k j", k=2)
    for k in range(2):
        e_cst = mark("cst", dve.tensor_copy(mask_b[:, k, :, :],
                                            mview[:, k, :].unsqueeze(1).to_broadcast([P, HP, 2 * WIN])))

    work = Ring(banks[0:4])
    hid_banks = Ring(banks[4:6])
    y_banks = Ring(banks[6:8])

    bk = work.take()
    wait(pe, ev_const, ev_rows)
    e = mark("pe_misc", pe.transpose(bk.t[:, 0:NROWS], rows_m[0:NROWS, :], ident[0:NROWS, 0:NROWS]))
    wait(dve, e)
    e_cols = mark("cols", dve.tensor_copy(cols[:, :], bk.t[:, 0:NROWS]))
    bk.release(e_cols)

    tmp = esb("mod_tmp", [P, 4, 2 * B])
    for k in range(2):
        silu = esb(f"silu{k}", [P, B])
        at = ROWS[f"c{k}"][0]
        wait(act, e_cols)
        e_silu = mark("silu", act.activation(silu[:, :], cols[:, at:at + B], ACT.Silu))
        bk = work.take()
        wait(pe, e_silu, ev_wmod[k], *bk.free)
        for j in range(6):
            e = mark("pe_misc", pe.matmul(bk.t[:, j * B:(j + 1) * B], wmod[k][:, j * D:(j + 1) * D],
                                          silu[:, :], start=True, stop=True))
        wait(dve, e)
        e = mark("mod", dve.tensor_copy(mod[k][:, :, :], bk.t[:, 0:6 * B].rearrange("p (j b) -> p j b", b=B)))
        bk.release(e)
        wait(dve, e)
        for j in (1, 4):
            e = mark("mod", dve.tensor_scalar(mod[k][:, j, :], mod[k][:, j, :], 1.0, None, ALU.add))
        for j in (2, 5):
            g = mod[k][:, j, :]
            neg, mag, sgn = tmp[:, 0, 0:B], tmp[:, 1, 0:B], tmp[:, 2, 0:B]
            wait(dve, e)
            e = mark("mod", dve.tensor_scalar(neg, g, -1.0, None, ALU.mult))
            wait(dve, e)
            e = mark("mod", dve.tensor_tensor(mag, neg, g, ALU.max))
            e = mark("mod", dve.tensor_scalar(sgn, g, 0.0, 2.0, ALU.is_ge, ALU.mult))
            wait(dve, e)
            e = mark("mod", dve.tensor_scalar(mag, mag, 0.25, None, ALU.max))
            e = mark("mod", dve.tensor_scalar(sgn, sgn, -1.0, None, ALU.add))
            wait(dve, e)
            e = mark("mod", dve.tensor_tensor(g, mag, sgn, ALU.mult))
        e_mod = e

    e_xT = []
    for q in range(NT // P // 4):
        bk = work.take()
        wait(pe, ev_x[q], *bk.free)
        for k in range(4):
            e = mark("pe_x", pe.transpose(bk.t[:, k * P:(k + 1) * P], x_rows[:, 4 * q + k, :], ident))
        wait(act, e)
        e_xT.append(mark("xT", act.activation(xT[:, q * 512:(q + 1) * 512], bk.t[:, :], ACT.Copy)))
        bk.release(e_xT[-1])

    wcT = esb("wcT", [P, D])
    wsum = esb("wsum", [P, D])
    ones1 = esb("ones1", [P, P])
    e_one1 = mark_pool("ones", pool.memset(ones1[:, :], 1.0))
    bk = work.take()
    wait(pe, ev_wc, *bk.free)
    e = mark("pe_misc", pe.transpose(bk.t[:, 0:P], w_c[:, :], ident))
    wait(dve, e)
    e = mark("wsum", dve.tensor_copy(wcT[:, :], bk.t[:, 0:P]))
    bk.release(e)
    bk = work.take()
    wait(pe, e, e_one1, *bk.free)
    e = mark("pe_misc", pe.matmul(bk.t[:, 0:D], ones1[:, :], wcT[:, :], start=True, stop=True))
    wait(dve, e)
    e_wsum = mark("wsum", dve.tensor_copy(wsum[:, :], bk.t[:, 0:D]))
    bk.release(e_wsum)

    def layer_norm(src, ready, ring, buf, gain, shift, dst, dst_free, tag):
        xc, sq = buf[:, 0, :], buf[:, 1, :]
        bank = ring.take()
        mean = bank.t[:, 0:S]
        wait(pe, e_ones, *ready, *bank.free)
        e = mark("ln_mean", pe.matmul(mean, ones_d[:, :], src, start=True, stop=True))
        wait(dve, e, *ready)
        e_xc = mark("ln_xc", dve.tensor_tensor(xc, src, mean, ALU.subtract))
        wait(act, e_xc)
        bank.release(e_xc)
        e = mark("ln_sq", act.activation(sq, xc, ACT.Square))
        yield
        bank = ring.take()
        var = bank.t[:, 0:S]
        wait(pe, e, *bank.free)
        e = mark("ln_var", pe.matmul(var, ones_d[:, :], sq, start=True, stop=True))
        wait(act, e, e_eps)
        e_sd = mark("ln_sd", act.activation(sq, var, ACT.Sqrt, bias=eps_ln[:, :]))
        bank.release(e_sd)
        yield
        wait(dve, e_sd)
        e = mark("ln_out", dve.reciprocal(sq, sq))
        wait(dve, e)
        e = mark("ln_out", dve.tensor_tensor(xc, xc, sq, ALU.mult))
        wait(dve, e, *dst_free)
        return mark("ln_out", dve.tensor_scalar(dst, xc, gain, shift, ALU.mult, ALU.add))

    def er(name, n, shape, dt=F32):
        return sb_ring(name, n, shape, dt, early)

    ln_buf = er("e_ln", 4, [P, 2, S])
    h_buf = er("e_h", 4, [P, S])
    qkT_b = er("e_qkT", 2, [P, 2, S])
    v_ext = er("e_vext", 2, [P, TC, FC, KVW])
    kp_b = er("e_kp", 1, [P, TC, NF])
    qp_b = er("e_qp", 1, [P, FC, S])
    kv_b = er("e_kv", 2, [P, FC, KVW])
    o_b = er("e_o", 3, [P, TC, D])
    oT_b = er("e_oT", 2, [P, S])
    sm_b = er("e_small", 4, [P, 64])
    hid = er("e_hid", 3, [P, MC, S])
    acc_b = er("e_acc", 2, [P, TC, D])
    gate_b = er("e_gate", 3, [P, TC, 8 * NE])
    idx_b = er("e_idx", 3, [P, TC, NE], U32)
    cT_b = er("e_cT", 3, [NE, S])
    prob_b = er("e_prob", 2, [P, TC, S])
    sp_b = er("e_sp", 1, [P, TC, S])
    spT_b = er("e_spT", 2, [P, TC, S])
    hr_b = er("e_hr", 2, [P, TC, P])

    for slot in v_ext.bufs:
        e_vones = mark_pool("v_ones", pool.memset(slot[:, :, :, 2 * DK0:], 1.0))

    def early_unit(b):
        x = xT[:, b * S:(b + 1) * S]
        tok = lambda t, c: t[:, c * P:(c + 1) * P]
        x_in = e_xT[b * S // 512]

        lb, h = ln_buf.take(), h_buf.take()
        wait(dve, *lb.free, e_mod)
        e_h = yield from layer_norm(x, [x_in], work, lb.t, mcol(0, 1, b), mcol(0, 0, b), h.t[:, :], h.free, "a")
        lb.release(e_h)
        bank, qkT = work.take(), qkT_b.take()
        wait(pe, e_h, ev_w0, *bank.free)
        pe.matmul(bank.t[:, 0:S], w_q[:, :], h.t[:, :], start=True, stop=True)
        e = mark("pe_qk0", pe.matmul(bank.t[:, S:2 * S], w_k[:, :], h.t[:, :], start=True, stop=True))
        wait(act, e, e_cols, *qkT.free)
        act.activation(qkT.t[:, 0, :], bank.t[:, 0:S], ACT.Identity, bias=col("bq"))
        e_qk = mark("qkT0", act.activation(qkT.t[:, 1, :], bank.t[:, S:2 * S], ACT.Identity, bias=col("bk")))
        bank.release(e_qk)
        bank, vx = work.take(), v_ext.take()
        wait(pe, *bank.free)
        for c in range(TC):
            e_v = mark("pe_v0", pe.matmul(bank.t[:, c * D:(c + 1) * D], tok(h.t, c), w_v[:, :],
                                          start=True, stop=True))
        h.release(e_v)
        wait(dve, e_v, ev_w0, e_vones, *vx.free)
        for c in range(TC):
            e_vx = mark("vx", dve.tensor_tensor(
                vx.t[:, c, :, 0:2 * DK0],
                bank.t[:, c * D:(c + 1) * D].rearrange("p (f w) -> p f w", w=2 * DK0),
                bv_b[:, :].rearrange("p (f w) -> p f w", w=2 * DK0), ALU.add))
        bank.release(e_vx)
        yield
        kp = kp_b.take()
        wait(dve, *kp.free)
        for c in range(TC):
            for n in range(NF // 512):
                bank = work.take()
                wait(pe, e_qk, ev_rf, *bank.free)
                e = mark("pe_kp", pe.matmul(bank.t[:, :], qkT.t[:, 1, c * P:(c + 1) * P],
                                            w_rf[:, n * 512:(n + 1) * 512], start=True, stop=True))
                wait(dve, e)
                e_kp = mark("kp", dve.tensor_scalar(kp.t[:, c, n * 512:(n + 1) * 512], bank.t[:, :],
                                                    0.0, EPS0, ALU.max, ALU.add))
                bank.release(e_kp)
            yield
        qp = qp_b.take()
        wait(dve, *qp.free)
        for f in range(0, FC, 2):
            bank = work.take()
            wait(pe, *bank.free)
            for k in range(2):
                e = mark("pe_qp", pe.matmul(bank.t[:, k * S:(k + 1) * S], w_rf[:, (f + k) * P:(f + k + 1) * P],
                                            qkT.t[:, 0, :], start=True, stop=True))
            wait(dve, e)
            e_qp = mark("qp", dve.tensor_scalar(qp.t[:, f:f + 2, :],
                                                bank.t[:, :].rearrange("p (k s) -> p k s", k=2),
                                                0.0, EPS0, ALU.max, ALU.add))
            bank.release(e_qp)
            if f == 2:
                yield
        qkT.release(e)
        yield
        bank, kv = work.take(), kv_b.take()
        wait(pe, e_kp, e_vx, *bank.free)
        for f in range(FC):
            for c in range(TC):
                e_kv = mark("pe_kv", pe.matmul(bank.t[:, f * KVW:(f + 1) * KVW], kp.t[:, c, f * P:(f + 1) * P],
                                               vx.t[:, c, f, :], start=(c == 0), stop=(c == TC - 1)))
        kp.release(e_kv)
        vx.release(e_kv)
        wait(dve, e_kv, *kv.free)
        e_kvm = mark("kvm", dve.tensor_tensor(kv.t[:, :, :], bank.t[:, 0:FC * KVW].rearrange("p (f w) -> p f w", f=FC),
                                              cst("kvmask").rearrange("p (f w) -> p f w", f=FC), ALU.mult))
        bank.release(e_kvm)
        yield
        bank, o, sm = work.take(), o_b.take(), sm_b.take()
        wait(pe, e_kvm, e_qp, *bank.free)
        for c in range(TC):
            for f in range(FC):
                at = c * S + f * KVW
                e = mark("pe_o0", pe.matmul(bank.t[:, at:at + KVW], qp.t[:, f, c * P:(c + 1) * P], kv.t[:, f, :],
                                            start=True, stop=True))
        qp.release(e)
        kv.release(e)
        wait(dve, e, *sm.free, *o.free)
        view = bank.t[:, :].rearrange("p (c n) -> p c n", c=TC)[:, :, 0:FC * KVW]\
            .rearrange("p c (f w) -> p c f w", w=KVW)
        for c in range(TC):
            e = mark("o0", dve.tensor_scalar(sm.t[:, c * H0:(c + 1) * H0].rearrange("p (f h) -> p f h", h=2),
                                             view[:, c, :, 2 * DK0:], EPS0, None, ALU.add))
        wait(dve, e)
        e = mark("o0", dve.reciprocal(sm.t[:, 0:TC * H0], sm.t[:, 0:TC * H0]))
        wait(dve, e)
        for c in range(TC):
            e_o = mark("o0", dve.tensor_tensor(
                o.t[:, c, :].rearrange("p (f h w) -> p f h w", h=2, w=DK0),
                view[:, c, :, 0:2 * DK0].rearrange("p f (h w) -> p f h w", h=2),
                sm.t[:, c * H0:(c + 1) * H0].rearrange("p (f h) -> p f h", h=2).unsqueeze(3)
                .to_broadcast([P, FC, 2, DK0]), ALU.mult))
        sm.release(e_o)
        bank.release(e_o)
        yield
        bank, oT = work.take(), oT_b.take()
        wait(pe, e_o, *bank.free)
        for c in range(TC):
            e = mark("pe_oT0", pe.transpose(bank.t[:, c * P:(c + 1) * P], o.t[:, c, :], ident))
        o.release(e)
        wait(act, e, *oT.free)
        e = mark("oT0", act.activation(oT.t[:, :], bank.t[:, 0:S], ACT.Copy))
        bank.release(e)
        yield
        bank = work.take()
        wait(pe, e, *bank.free)
        e = mark("pe_wo0", pe.matmul(bank.t[:, 0:S], w_o[:, :], oT.t[:, :], start=True, stop=True))
        wait(dve, e)
        e = mark("x1", dve.tensor_scalar(oT.t[:, :], bank.t[:, 0:S], col("bo"), mcol(0, 2, b), ALU.add, ALU.mult))
        bank.release(e)
        wait(dve, e)
        e_x = mark("x1", dve.tensor_tensor(x, x, oT.t[:, :], ALU.add))
        oT.release(e_x)
        yield

        lb, h = ln_buf.take(), h_buf.take()
        wait(dve, *lb.free)
        e_h = yield from layer_norm(x, [e_x], work, lb.t, mcol(0, 4, b), mcol(0, 3, b), h.t[:, :], h.free, "b")
        lb.release(e_h)
        bank, gt, ix = work.take(), gate_b.take(), idx_b.take()
        wait(pe, e_h, ev_moe, *bank.free)
        for c in range(TC):
            e = mark("pe_gate", pe.matmul(bank.t[:, c * NE:(c + 1) * NE], tok(h.t, c), w_gate[:, :],
                                          start=True, stop=True))
        LOG, TOP, IDX, COMB, TMP, SC = (slice(k * NE, (k + 1) * NE) for k in range(6))
        wait(dve, e, *gt.free, *ix.free)
        e = mark("gate", dve.tensor_copy(gt.t[:, :, LOG], bank.t[:, 0:TC * NE].rearrange("p (c n) -> p c n", c=TC)))
        bank.release(e)
        wait(dve, e)
        for c in range(TC):
            e = mark("gate", dve.max(gt.t[:, c, TOP], gt.t[:, c, LOG]))
            wait(dve, e)
            e = mark("gate", dve.max_index(ix.t[:, c, :], gt.t[:, c, TOP], gt.t[:, c, LOG]))
        wait(dve, e)
        e = mark("gate", dve.tensor_copy(gt.t[:, :, IDX], ix.t[:, :, :]))
        s0 = SC.start
        e_d = mark("gate", dve.tensor_tensor(gt.t[:, :, s0:s0 + 1], gt.t[:, :, NE + 1:NE + 2], gt.t[:, :, NE:NE + 1],
                                             ALU.subtract))
        ix.release(e_d)
        wait(act, e_d)
        e = mark("gate_exp", act.activation(gt.t[:, :, s0 + 1:s0 + 2], gt.t[:, :, s0:s0 + 1], ACT.Exp))
        yield
        wait(dve, e)
        e = mark("gate", dve.tensor_scalar(gt.t[:, :, s0 + 2:s0 + 3], gt.t[:, :, s0 + 1:s0 + 2], 1.0, None, ALU.add))
        wait(dve, e)
        e = mark("gate", dve.reciprocal(gt.t[:, :, s0 + 3:s0 + 4], gt.t[:, :, s0 + 2:s0 + 3]))
        wait(dve, e)
        e = mark("gate", dve.tensor_tensor(gt.t[:, :, s0 + 4:s0 + 5], gt.t[:, :, s0 + 3:s0 + 4],
                                           gt.t[:, :, s0 + 1:s0 + 2], ALU.mult))
        wait(dve, e)
        for c in range(TC):
            dve.tensor_scalar(gt.t[:, c, COMB], cst("iota"), gt.t[:, c, 2 * NE:2 * NE + 1],
                              gt.t[:, c, s0 + 3:s0 + 4], ALU.is_equal, ALU.mult)
            e = mark("gate", dve.tensor_scalar(gt.t[:, c, TMP], cst("iota"), gt.t[:, c, 2 * NE + 1:2 * NE + 2],
                                               gt.t[:, c, s0 + 4:s0 + 5], ALU.is_equal, ALU.mult))
        wait(dve, e)
        e_comb = mark("gate", dve.tensor_tensor(gt.t[:, :, COMB], gt.t[:, :, COMB], gt.t[:, :, TMP], ALU.add))
        bank, cT, acc = work.take(), cT_b.take(), acc_b.take()
        wait(pe, e_comb, *bank.free)
        for c in range(TC):
            e = mark("pe_cT", pe.transpose(bank.t[0:NE, c * P:(c + 1) * P], gt.t[:, c, COMB], ident))
        wait(dve, e, *cT.free)
        e = mark("gate", dve.tensor_copy(cT.t[:, :], bank.t[0:NE, 0:S]))
        bank.release(e)
        yield
        bank = work.take()
        wait(pe, e, *bank.free)
        for c in range(TC):
            e = mark("pe_bout", pe.matmul(bank.t[:, c * D:(c + 1) * D], cT.t[:, c * P:(c + 1) * P], b_out[:, :],
                                          start=True, stop=True))
        cT.release(e)
        wait(dve, e, *acc.free)
        e_acc = mark("acc", dve.tensor_copy(acc.t[:, :, :], bank.t[:, 0:TC * D].rearrange("p (c n) -> p c n", c=TC)))
        bank.release(e_acc)
        hidden = {}
        for ex in range(NE + 1):
            if ex < NE:
                hd = hid.take()
                wait(act, *hd.free)
                for m in range(0, MC, 2):
                    bank = hid_banks.take()
                    wait(pe, *bank.free)
                    for k in range(2):
                        e = mark("pe_hid", pe.matmul(bank.t[:, k * S:(k + 1) * S],
                                                     w_in[:, ex, (m + k) * P:(m + k + 1) * P], h.t[:, :],
                                                     start=True, stop=True))
                    wait(act, e)
                    for k in range(2):
                        e_hd = mark("hid", act.activation(hd.t[:, m + k, :], bank.t[:, k * S:(k + 1) * S], ACT.Gelu,
                                                          bias=col("b_in", ex * MC + m + k)))
                    bank.release(e_hd)
                hidden[ex] = hd, e_hd
                if ex == NE - 1:
                    h.release(e)
            if ex > 0:
                hd, e_hd = hidden.pop(ex - 1)
                bank = y_banks.take()
                wait(pe, e_hd, *bank.free)
                for c in range(TC):
                    for m in range(MC):
                        e = mark("pe_y", pe.matmul(bank.t[:, c * D:(c + 1) * D], hd.t[:, m, c * P:(c + 1) * P],
                                                   w_out[:, ex - 1, m, :], start=(m == 0), stop=(m == MC - 1)))
                hd.release(e)
                wait(dve, e, e_acc)
                for c in range(TC):
                    e_acc = mark("acc", dve.scalar_tensor_tensor(
                        out=acc.t[:, c, :], in0=bank.t[:, c * D:(c + 1) * D],
                        scalar=gt.t[:, c, COMB.start + ex - 1:COMB.start + ex], in1=acc.t[:, c, :],
                        op0=ALU.mult, op1=ALU.add))
                bank.release(e_acc)
            yield
        gt.release(e_acc)
        bank = work.take()
        wait(pe, e_acc, *bank.free)
        for c in range(TC):
            e = mark("pe_accT", pe.transpose(bank.t[:, c * P:(c + 1) * P], acc.t[:, c, :], ident))
        acc.release(e)
        wait(dve, e)
        e_x = mark("x2", dve.scalar_tensor_tensor(out=x, in0=bank.t[:, 0:S], scalar=mcol(0, 5, b), in1=x,
                                                  op0=ALU.mult, op1=ALU.add))
        bank.release(e_x)
        yield

        lb, h = ln_buf.take(), h_buf.take()
        wait(dve, *lb.free)
        e_h = yield from layer_norm(x, [e_x], work, lb.t, mcol(1, 1, b), mcol(1, 0, b), h.t[:, :], h.free, "c")
        lb.release(e_h)
        bank, hr = work.take(), hr_b.take()
        wait(pe, e_h, *bank.free)
        for c in range(TC):
            e = mark("pe_hr", pe.transpose(bank.t[:, c * P:(c + 1) * P], tok(h.t, c), ident))
        wait(act, e, *hr.free)
        e_hr = mark("hr", act.activation(hr.t[:, :, :], bank.t[:, 0:S].rearrange("p (c n) -> p c n", c=TC), ACT.Copy))
        bank.release(e_hr)
        bank, pr, sm = work.take(), prob_b.take(), sm_b.take()
        wait(pe, *bank.free)
        for c in range(TC):
            e = mark("pe_s1", pe.matmul(bank.t[:, c * S:(c + 1) * S], tok(h.t, c), h.t[:, :], start=True, stop=True))
        h.release(e)
        NM, SUM, RS, SPS, VAC = (slice(k * TC, (k + 1) * TC) for k in range(5))
        one = lambda s, c: sm.t[:, s.start + c:s.start + c + 1]
        scale = float(np.float32(1.0) / np.sqrt(np.float32(D)))
        wait(dve, e, *sm.free)
        e = mark("p1", dve.tensor_reduce(sm.t[:, NM], bank.t[:, :].rearrange("p (c s) -> p c s", c=TC), AX.X, ALU.max))
        wait(dve, e)
        e = mark("p1", dve.tensor_scalar(sm.t[:, NM], sm.t[:, NM], -scale, None, ALU.mult))
        yield
        wait(act, e, *pr.free)
        for c in range(TC):
            e = mark("exp1", act.activation(pr.t[:, c, :], bank.t[:, c * S:(c + 1) * S], ACT.Exp, bias=one(NM, c),
                                            scale=scale, accum_out=one(SUM, c)))
        bank.release(e)
        yield
        wait(dve, e)
        e = mark("p1", dve.reciprocal(sm.t[:, RS], sm.t[:, SUM]))
        wait(dve, e)
        spb = sp_b.take()
        for c in range(TC):
            e = mark("p1", dve.tensor_scalar(pr.t[:, c, :], pr.t[:, c, :], one(RS, c), None, ALU.mult))
        wait(dve, e, *spb.free)
        for c in range(TC):
            e = mark("p1", dve.scalar_tensor_tensor(out=spb.t[:, c, :], in0=pr.t[:, c, :], scalar=THRESH,
                                                    in1=pr.t[:, c, :], op0=ALU.is_lt, op1=ALU.mult,
                                                    accum_out=one(VAC, c)))
            wait(dve, e)
            e = mark("p1", dve.scalar_tensor_tensor(out=spb.t[:, c, :], in0=pr.t[:, c, :], scalar=THRESH,
                                                    in1=pr.t[:, c, :], op0=ALU.is_ge, op1=ALU.mult,
                                                    accum_out=one(SPS, c)))
        e_sp = e
        pr.release(e)
        wait(dve, e)
        e = mark("p1", dve.tensor_scalar(sm.t[:, SPS], sm.t[:, SPS], 1e-9, None, ALU.add))
        wait(dve, e)
        e = mark("p1", dve.reciprocal(sm.t[:, SPS], sm.t[:, SPS]))
        e = mark("p1", dve.tensor_scalar(sm.t[:, VAC], sm.t[:, VAC], 0.01, None, ALU.mult))
        e_sm = e
        yield
        bank, spT = work.take(), spT_b.take()
        wait(pe, e_sp, *bank.free)
        for k in range(TC):
            for c in range(TC):
                e = mark("pe_spT", pe.transpose(bank.t[:, k * S + c * P:k * S + (c + 1) * P],
                                                spb.t[:, c, k * P:(k + 1) * P], ident))
        spb.release(e)
        wait(act, e, *spT.free)
        e = mark("spT", act.activation(spT.t[:, :, :], bank.t[:, :].rearrange("p (k s) -> p k s", k=TC), ACT.Copy))
        bank.release(e)
        yield
        bank, o = work.take(), o_b.take()
        wait(pe, e, e_hr, *bank.free)
        for c in range(TC):
            for k in range(TC):
                e = mark("pe_at1", pe.matmul(bank.t[:, c * D:(c + 1) * D], spT.t[:, k, c * P:(c + 1) * P],
                                             hr.t[:, k, :], start=(k == 0), stop=(k == TC - 1)))
        spT.release(e)
        hr.release(e)
        wait(dve, e, e_sm, e_wsum, *o.free)
        for c in range(TC):
            e = mark("at1", dve.tensor_scalar(o.t[:, c, :], bank.t[:, c * D:(c + 1) * D], one(SPS, c), None, ALU.mult))
        bank.release(e)
        wait(dve, e)
        for c in range(TC):
            e = mark("at1", dve.scalar_tensor_tensor(out=o.t[:, c, :], in0=wsum[:, :], scalar=one(VAC, c),
                                                     in1=o.t[:, c, :], op0=ALU.mult, op1=ALU.add))
        sm.release(e)
        yield
        bank = work.take()
        wait(pe, e, *bank.free)
        for c in range(TC):
            e = mark("pe_atT", pe.transpose(bank.t[:, c * P:(c + 1) * P], o.t[:, c, :], ident))
        o.release(e)
        wait(dve, e)
        e_x = mark("x3", dve.scalar_tensor_tensor(out=x, in0=bank.t[:, 0:S], scalar=mcol(1, 2, b), in1=x,
                                                  op0=ALU.mult, op1=ALU.add))
        bank.release(e_x)
        yield
        lb = ln_buf.take()
        wait(dve, *lb.free)
        e = yield from layer_norm(x, [e_x], work, lb.t, mcol(1, 4, b), mcol(1, 3, b), zT[:, b * S:(b + 1) * S], (), "d")
        lb.release(e)
        early_done.append(e)

    early_done = []
    interleave([lambda b=b: early_unit(b) for b in range(B)], EARLY_SPACING)

    everything = [sg.last[s] for s in sg.last if not s.startswith("ld_")] + [ev_rows]
    for engine in (pe, dve, act, pool, sp):
        wait(engine, *everything)
    early.close()

    one_bank = Ring(banks[0:4])
    s_banks = Ring([banks[4:6]])
    o_banks = Ring([banks[6:8]])

    xs_r = sb_ring("xs", 2, [P, S])
    raw_r = sb_ring("raw", 2, [P, 2 * INNER])
    rt_r = sb_ring("rt", 2, [P, 2 * INNER])
    t2_r = sb_ring("t2", 1, [P, 2 * INNER])
    rn_r = sb_ring("rn", 3, [P, TC, 2 * HEADS])
    qT_r = sb_ring("qT", 2, [P, HP, P])
    kT_r = sb_ring("kT", 2, [P, HP, WIN + S])
    vn_r = sb_ring("vn", 2, [P, INNER])
    v2_r = sb_ring("v2", 3, [P, NW, HP * DH])
    p_r = sb_ring("p", 2, [P, HP, 2, 2 * WIN])
    pT_r = sb_ring("pT", 2, [P, HP, P])
    sm_r = sb_ring("sm", 2, [P, 4, HEADS])
    oa_r = sb_ring("oa", 1, [P, HP, 2, DH])
    oT_r = sb_ring("oT", 1, [P, INNER // P, S])
    xf_r = sb_ring("xf", 2, [P, S])
    lnf_r = sb_ring("lnf", 1, [P, 2, S])
    hn_r = sb_ring("hn", 1, [P, S])
    g_r = sb_ring("g", 2, [P, S])
    hh_r = sb_ring("hh", 1, [P, len(DIC), S])

    for r in (xs_r, xf_r):
        for t in r.bufs:
            e_z = mark_pool("zpad", pool.memset(t[DH:P, 0:1], 0.0))
    for t in kT_r.bufs:
        e_z = mark_pool("zpad", pool.memset(t[:, :, 0:WIN], 0.0))
    for t in v2_r.bufs:
        e_z = mark_pool("zpad", pool.memset(t[:, 0, :], 0.0))

    z_ready = {b: early_done[b] for b in range(B)}
    tables = {}

    def layer_tables(l):
        slot = rot.take()
        src = cst("rot").rearrange("p (c k d) -> p c k d", c=TC, k=4)
        gn, e_gain = layer_w[l]["gain"]
        wait(dve, e_gain, *slot.free)
        for k in range(4):
            g = gn.t[:, k // 2, :].rearrange("p (h d) -> p h d", h=2)
            if k % 2:
                g = g[:, ::-1, :]
            for c in range(TC):
                e = mark("tables", dve.tensor_tensor(
                    slot.t[:, c, k, :].rearrange("p (h d) -> p h d", h=2),
                    src[:, c, k, :].rearrange("p (h d) -> p h d", h=2), g, ALU.mult))
        gn.release(e)
        tables[l] = slot, e

    def shifted(dst, src, ready):
        wait(act, ready, e_z, *dst.free)
        act.activation(dst.t[0:DH, :], src[0:DH, :], ACT.Copy)
        return mark("shift", act.activation(dst.t[DH:P, 1:S], src[DH:P, 0:S - 1], ACT.Copy))

    def unit(l, b):
        z = zT[:, b * S:(b + 1) * S]
        last_of_layer = b == B - 1
        pairs = lambda t, n=HEADS: t.rearrange("p (n h d) -> p n h d", h=2, d=DH // 2)
        heads = lambda t: t.rearrange("p (n d) -> p n d", d=DH)
        four = lambda bank: bank.t[:, :].rearrange("p (n i) -> p n i", n=4)
        per_chunk = lambda: [None] * TC
        raw, rt, vn, v2, qT, pb, sm, pT, oa = (per_chunk() for _ in range(9))
        e_raw, e_ss, e_rot, e_nrm, e_qkT, e_vn, e_v2, e_s, e_exp, e_sum, e_pT, e_o, e_oa, e_oT = \
            (per_chunk() for _ in range(14))
        held = {}

        def start():
            if b == 0:
                layer_tables(l)
            if b == 2 and l + 1 < DEPTH:
                load_projections(l + 1)
            held["xs"] = xs_r.take()
            held["e_xs"] = shifted(held["xs"], z, z_ready[b])

        def project(c, n):
            w, e_w = layer_w[l]["qk"]
            if n == 0:
                raw[c] = raw_r.take()
            bank = one_bank.take()
            wait(pe, held["e_xs"], e_w, *bank.free)
            e = mark("pe_qk", pe.matmul(bank.t[:, :], held["xs"].t[:, c * P:(c + 1) * P],
                                        w.t[:, n * 512:(n + 1) * 512], start=True, stop=True))
            wait(act, e, *raw[c].free)
            e_raw[c] = mark("raw", act.activation(raw[c].t[:, n * 512:(n + 1) * 512], bank.t[:, :], ACT.Copy))
            bank.release(e_raw[c])
            if last_of_layer and (c, n) == (TC - 1, 3):
                w.release(e)

        def square(c):
            held["sq"] = t2_r.take()
            wait(act, e_raw[c], *held["sq"].free)
            held["e_sq"] = mark("sq", act.activation(held["sq"].t[:, :], raw[c].t[:, :], ACT.Square))

        def sum_squares(c):
            if c == 0:
                held["rn"] = rn_r.take()
            rn = held["rn"]
            wait(dve, held["e_sq"], *(rn.free if c == 0 else ()))
            e_ss[c] = mark("ss", dve.tensor_reduce(rn.t[:, c, :], heads(held["sq"].t[:, :]), AX.X, ALU.add))
            held["sq"].release(e_ss[c])

        def rotate(c):
            tab, e_tab = tables[l]
            rt[c], t2 = rt_r.take(), t2_r.take()
            wait(dve, e_raw[c], e_tab, *rt[c].free, *t2.free)
            for k in range(2):
                part = slice(k * INNER, (k + 1) * INNER)
                cosv = tab.t[:, c, 2 * k, :].unsqueeze(1).to_broadcast([P, HEADS, DH])
                sinv = tab.t[:, c, 2 * k + 1, :].rearrange("p (h d) -> p h d", h=2).unsqueeze(1)\
                    .to_broadcast([P, HEADS, 2, DH // 2])
                mark("rot", dve.tensor_tensor(heads(rt[c].t[:, part]), heads(raw[c].t[:, part]), cosv, ALU.mult))
                e = mark("rot", dve.tensor_tensor(pairs(t2.t[:, part]), pairs(raw[c].t[:, part])[:, :, ::-1, :],
                                                  sinv, ALU.mult))
            raw[c].release(e)
            if last_of_layer and c == TC - 1:
                tab.release(e)
            wait(pool, e)
            e_rot[c] = mark_pool("rot_add", pool.tensor_tensor(rt[c].t[:, :], rt[c].t[:, :], t2.t[:, :], ALU.add))
            t2.release(e_rot[c])

        def norm_root():
            rn = held["rn"]
            wait(act, *e_ss)
            held["e_norm"] = mark("norm", act.activation(rn.t[:, :, :], rn.t[:, :, :], ACT.Sqrt))

        def norm_inverse():
            rn = held["rn"]
            wait(dve, held["e_norm"])
            e = mark("rn", dve.tensor_scalar(rn.t[:, :, :], rn.t[:, :, :], 1e-12, None, ALU.max))
            wait(dve, e)
            held["e_rn"] = mark("rn", dve.reciprocal(rn.t[:, :, :], rn.t[:, :, :]))

        def normalise(c):
            v, rn = heads(rt[c].t[:, :]), held["rn"]
            wait(dve, held["e_rn"], e_rot[c])
            e_nrm[c] = mark("nrm", dve.tensor_tensor(v, v, rn.t[:, c, :].unsqueeze(2)
                                                     .to_broadcast([P, 2 * HEADS, DH]), ALU.mult))
            if c == TC - 1:
                rn.release(e_nrm[c])

        def transpose_qk(c, k):
            if k == 0:
                qT[c] = qT_r.take()
                if c == 0:
                    held["kT"] = kT_r.take()
            bank = one_bank.take()
            wait(pe, e_nrm[c], *bank.free)
            for n in range(4):
                at = (4 * k + n) * P
                e = mark("pe_qkT", pe.transpose(bank.t[:, n * P:(n + 1) * P], rt[c].t[:, at:at + P], ident))
            if k == 3:
                rt[c].release(e)
            if k < 2:
                wait(act, e, *qT[c].free)
                dst = qT[c].t[:, 4 * k:4 * k + 4, :]
            else:
                kT = held["kT"]
                wait(act, e, *(kT.free if c == 0 else ()))
                dst = kT.t[:, 4 * (k - 2):4 * (k - 2) + 4, WIN + c * P:WIN + (c + 1) * P]
            e_qkT[c] = mark("qkT", act.activation(dst, four(bank), ACT.Copy))
            bank.release(e_qkT[c])

        def values(c, r):
            w, e_w = layer_w[l]["v"]
            if r == 0:
                vn[c] = vn_r.take()
            bank = one_bank.take()
            wait(pe, e_w, *bank.free)
            e = mark("pe_v", pe.matmul(bank.t[:, :], held["xs"].t[:, c * P:(c + 1) * P],
                                       w.t[:, r * 512:(r + 1) * 512], start=True, stop=True))
            wait(act, e, *vn[c].free)
            e_vn[c] = mark("vn", act.activation(vn[c].t[:, r * 512:(r + 1) * 512], bank.t[:, :], ACT.Copy))
            bank.release(e_vn[c])
            if (c, r) == (TC - 1, 1):
                held["xs"].release(e)
                if last_of_layer:
                    w.release(e)

        def pair_values(c):
            v2[c] = v2_r.take()
            wait(sp, e_vn[c], e_z, *v2[c].free)
            for g in range(NW):
                for half in range(2):
                    v = NW * c + g - 1 + half
                    if v < 0:
                        continue
                    src = vn[v // NW].t[WIN * (v % NW):WIN * (v % NW + 1), :]
                    for r in range(2):
                        at = 2 * WIN * r + WIN * half
                        e = sg.dma(f"v2_{v2[c].k}", sp.dma_start(v2[c].t[at:at + WIN, g, :],
                                                                 src[:, r * 512:(r + 1) * 512]))
            e_v2[c] = e
            if c == TC - 1:
                vn[0].release(e_v2[0], e)
                vn[1].release(e)

        def scores(c, *windows):
            if windows[0] == 0:
                held["s"] = s_banks.take()
                wait(pe, e_cst, *e_qkT[0:c + 1], *held["s"].free)
                for r in range(2):
                    pe.matmul(held["s"].t[r][:, :], ident_b[:, :],
                              mask_b[:, min(c, 1), :, :].rearrange("p h j -> p (h j)"),
                              start=True, stop=False, skip_group_check=True)
            for g in windows:
                k0 = c * P + g * WIN
                for hp in range(HP):
                    for r in range(2):
                        rows = slice(2 * WIN * r, 2 * WIN * (r + 1))
                        e = pe.matmul(held["s"].t[r][WIN * g:WIN * (g + 1), hp * 2 * WIN:(hp + 1) * 2 * WIN],
                                      qT[c].t[rows, hp, WIN * g:WIN * (g + 1)], held["kT"].t[rows, hp, k0:k0 + 2 * WIN],
                                      start=False, stop=True, skip_group_check=True)
            if windows[-1] == NW - 1:
                e_s[c] = mark("pe_s", e)
                qT[c].release(e_s[c])
                if c == TC - 1:
                    held["kT"].release(e_s[c])

        by_head = lambda bank: bank[:, :].rearrange("p (h j) -> p h j", h=HP)

        def softmax_in(c):
            pb[c], sm[c], s = p_r.take(), sm_r.take(), held["s"]
            wait(dve, e_s[c], *sm[c].free, *pb[c].free)
            for r in range(2):
                e = mark("smax", dve.tensor_reduce(sm[c].t[:, r, 0:HP], by_head(s.t[r]), AX.X, ALU.max))
            wait(dve, e)
            for r in range(2):
                e = mark("smax", dve.tensor_tensor(pb[c].t[:, :, r, :], by_head(s.t[r]), sm[c].t[:, r, 0:HP]
                                                   .unsqueeze(2).to_broadcast([P, HP, 2 * WIN]), ALU.subtract))
            s.release(e)
            wait(act, e)
            e_exp[c] = mark("exp", act.activation(pb[c].t[:, :, :, :], pb[c].t[:, :, :, :], ACT.Exp))

        def softmax_sum(c):
            wait(dve, e_exp[c])
            e = mark("ssum", dve.tensor_reduce(sm[c].t[:, 2, :].rearrange("p (h r) -> p h r", r=2),
                                               pb[c].t[:, :, :, :], AX.X, ALU.add))
            wait(dve, e)
            e_sum[c] = mark("ssum", dve.reciprocal(sm[c].t[:, 3, :], sm[c].t[:, 2, :]))
            held["p_sum", c] = e

        def transpose_p(c, k):
            if k == 0:
                pT[c] = pT_r.take()
            bank = one_bank.take()
            wait(pe, e_exp[c], *bank.free)
            for n in range(4):
                e = mark("pe_pT", pe.transpose(bank.t[:, n * P:(n + 1) * P],
                                               pb[c].t[:, 4 * k + n, :, :].rearrange("p r j -> p (r j)"), ident))
            wait(act, e, *pT[c].free)
            e_pT[c] = mark("pT", act.activation(pT[c].t[:, 4 * k:4 * k + 4, :], four(bank), ACT.Copy))
            bank.release(e_pT[c])
            if k == 1:
                pb[c].release(e, held["p_sum", c])

        def attend(c, *windows):
            if windows[0] == 0:
                held["o"] = o_banks.take()
                wait(pe, e_pT[c], e_v2[c], *held["o"].free)
            for g in windows:
                for hp in range(HP):
                    for r in range(2):
                        rows = slice(2 * WIN * r, 2 * WIN * (r + 1))
                        e = pe.matmul(held["o"].t[r][WIN * g:WIN * (g + 1), hp * DH:(hp + 1) * DH],
                                      pT[c].t[rows, hp, WIN * g:WIN * (g + 1)],
                                      v2[c].t[rows, g, hp * DH:(hp + 1) * DH], start=True, stop=True)
            if windows[-1] == NW - 1:
                e_o[c] = mark("pe_o", e)
                pT[c].release(e_o[c])
                v2[c].release(e_o[c])

        def attended(c):
            oa[c] = oa_r.take()
            wait(dve, e_o[c], e_sum[c], *oa[c].free)
            inv = sm[c].t[:, 3, :].rearrange("p (h r) -> p h r", r=2)
            for r in range(2):
                e_oa[c] = mark("oa", dve.tensor_tensor(oa[c].t[:, :, r, :], by_head(held["o"].t[r]),
                                                       inv[:, :, r:r + 1].to_broadcast([P, HP, DH]), ALU.mult))
            held["o"].release(e_oa[c])
            sm[c].release(e_oa[c])

        def transpose_o(c, k):
            if c == 0 and k == 0:
                held["oT"] = oT_r.take()
            bank, oT = one_bank.take(), held["oT"]
            wait(pe, e_oa[c], *bank.free)
            for n in range(4):
                e = mark("pe_oT", pe.transpose(bank.t[:, n * P:(n + 1) * P],
                                               oa[c].t[:, 4 * k + n, :, :].rearrange("p r e -> p (r e)"), ident))
            if k == 1:
                oa[c].release(e)
            wait(act, e, *oT.free)
            e_oT[c] = mark("oT", act.activation(oT.t[:, 4 * k:4 * k + 4, c * P:(c + 1) * P], four(bank), ACT.Copy))
            bank.release(e_oT[c])

        def project_out():
            (w, e_w), oT, bank = layer_w[l]["o"], held["oT"], one_bank.take()
            wait(pe, *e_oT, e_w, *bank.free)
            for k in range(INNER // P):
                e = mark("pe_wo", pe.matmul(bank.t[:, 0:S], w.t[:, k, :], oT.t[:, k, :],
                                            start=(k == 0), stop=(k == INNER // P - 1)))
            oT.release(e)
            if last_of_layer:
                w.release(e)
                if l + 1 < DEPTH:
                    load_output(l + 1)
            held["wo"] = bank, e

        def add_attention():
            bank, e = held["wo"]
            wait(dve, e)
            held["e_z1"] = mark("z_mid", dve.tensor_tensor(z, z, bank.t[:, 0:S], ALU.add))
            bank.release(held["e_z1"])
            held["xf"] = xf_r.take()
            held["e_xf"] = shifted(held["xf"], z, held["e_z1"])

        def ln_mean():
            bank = one_bank.take()
            wait(pe, held["e_xf"], *bank.free)
            held["mean"] = bank, mark("ln_mean", pe.matmul(bank.t[:, 0:S], ones_d[:, :], held["xf"].t[:, :],
                                                           start=True, stop=True))

        def ln_centre():
            (bank, e), xf, lb = held["mean"], held["xf"], lnf_r.take()
            held["lb"] = lb
            wait(dve, e, held["e_xf"], *lb.free)
            e = mark("ln_xc", dve.tensor_tensor(lb.t[:, 0, :], xf.t[:, :], bank.t[:, 0:S], ALU.subtract))
            bank.release(e)
            xf.release(e)
            wait(act, e)
            held["e_lnsq"] = mark("ln_sq", act.activation(lb.t[:, 1, :], lb.t[:, 0, :], ACT.Square))

        def ln_variance():
            bank, lb = one_bank.take(), held["lb"]
            wait(pe, held["e_lnsq"], *bank.free)
            e = mark("ln_var", pe.matmul(bank.t[:, 0:S], ones_d[:, :], lb.t[:, 1, :], start=True, stop=True))
            wait(act, e)
            held["e_sd"] = mark("ln_sd", act.activation(lb.t[:, 1, :], bank.t[:, 0:S], ACT.Sqrt, bias=eps_ln[:, :]))
            bank.release(held["e_sd"])

        def ln_out():
            lb, hn = held["lb"], hn_r.take()
            xc, sd = lb.t[:, 0, :], lb.t[:, 1, :]
            wait(dve, held["e_sd"])
            e = mark("ln_out", dve.reciprocal(sd, sd))
            wait(dve, e)
            e = mark("ln_out", dve.tensor_tensor(xc, xc, sd, ALU.mult))
            wait(dve, e, *hn.free)
            e = mark("ln_out", dve.tensor_scalar(hn.t[:, :], xc, col("ln_g", l), col("ln_b", l), ALU.mult, ALU.add))
            lb.release(e)
            held["hn"] = hn, e

        def up(j):
            (w, e_w), (hn, e_hn), (at, n) = layer_w[l]["w1"], held["hn"], DIC[j]
            bank, g = one_bank.take(), g_r.take()
            wait(pe, e_hn, e_w, *bank.free)
            pe.matmul(bank.t[0:n, 0:S], w.t[:, at:at + n], hn.t[:, :], start=True, stop=True)
            e_up = mark("pe_w1", pe.matmul(bank.t[0:n, S:2 * S], w.t[:, DI + at:DI + at + n], hn.t[:, :],
                                           start=True, stop=True))
            wait(act, e_up, *g.free)
            e = mark("gelu", act.activation(g.t[0:n, :], bank.t[0:n, S:2 * S], ACT.Gelu,
                                            bias=col("b1", (len(DIC) + j) * DEPTH + l, n)))
            held["up", j] = bank, g, e
            if j == len(DIC) - 1:
                hn.release(e_up)
                if last_of_layer:
                    w.release(e_up)

        def gate(j):
            (bank, g, e), (at, n) = held["up", j], DIC[j]
            if j == 0:
                held["hh"] = hh_r.take()
            hh = held["hh"]
            wait(dve, e, *(hh.free if j == 0 else ()))
            held["e_hh"] = mark("hh", dve.scalar_tensor_tensor(
                out=hh.t[0:n, j, :], in0=bank.t[0:n, 0:S], scalar=col("b1", j * DEPTH + l, n), in1=g.t[0:n, :],
                op0=ALU.add, op1=ALU.mult))
            g.release(held["e_hh"])
            bank.release(held["e_hh"])

        def down():
            (w, e_w), hh, bank = layer_w[l]["w2"], held["hh"], one_bank.take()
            wait(pe, held["e_hh"], e_w, *bank.free)
            for j, (at, n) in enumerate(DIC):
                e = mark("pe_w2", pe.matmul(bank.t[:, 0:S], w.t[0:n, j, :], hh.t[0:n, j, :],
                                            start=(j == 0), stop=(j == len(DIC) - 1)))
            hh.release(e)
            if last_of_layer:
                w.release(e)
                if l + 1 < DEPTH:
                    load_ffn(l + 1)
            held["down"] = bank, e

        def add_ffn():
            bank, e = held["down"]
            wait(dve, e, held["e_xf"])
            z_ready[b] = mark("z_out", dve.scalar_tensor_tensor(out=z, in0=bank.t[:, 0:S], scalar=col("b2", l), in1=z,
                                                                op0=ALU.add, op1=ALU.add))
            bank.release(z_ready[b])

        plan = {}

        def at(slot, step, *args):
            plan.setdefault(slot, []).append((step, args))

        at(0, start)
        for n in range(4):
            at(2 + n, project, 0, n)
            at(6 + n, project, 1, n)
        at(6, square, 0)
        at(7, sum_squares, 0)
        at(8, rotate, 0)
        at(10, square, 1)
        at(11, sum_squares, 1)
        at(11, norm_root)
        at(11, rotate, 1)
        at(12, norm_inverse)
        at(12, normalise, 0)
        at(14, normalise, 1)
        for slot, c, r in ((11, 0, 0), (12, 0, 1), (13, 1, 0), (14, 1, 1)):
            at(slot, values, c, r)
        for slot, c, k in ((13, 0, 0), (14, 0, 1), (14, 0, 2), (15, 0, 3), (15, 1, 0), (16, 1, 1), (17, 1, 2), (18, 1, 3)):
            at(slot, transpose_qk, c, k)
        at(16, pair_values, 0)
        at(18, pair_values, 1)
        for c in range(TC):
            t = 16 + 4 * c
            at(t, scores, c, 0, 1)
            at(t + 1, scores, c, 2)
            at(t + 2, scores, c, 3)
            at(t + 3, softmax_in, c)
            at(t + 5, softmax_sum, c)
            at(t + 5, transpose_p, c, 0)
            at(t + 5, transpose_p, c, 1)
            at(t + 6, attend, c, 0, 1)
            at(t + 7, attend, c, 2)
            at(t + 8, attend, c, 3)
            at(t + 9, attended, c)
            at(t + 11, transpose_o, c, 0)
            at(t + 11, transpose_o, c, 1)
        at(32, project_out)
        at(33, add_attention)
        at(34, ln_mean)
        at(35, ln_centre)
        at(36, ln_variance)
        at(38, ln_out)
        for j in range(len(DIC)):
            at(39 + j, up, j)
            at(40 + j, gate, j)
        at(43, down)
        at(44, add_ffn)
        for slot in range(max(plan) + 1):
            for step, args in plan.get(slot, ()):
                step(*args)
            yield

    interleave([lambda l=l, b=b: unit(l, b) for l in range(DEPTH) for b in range(B)], LATE_SPACING)

    orow = [raw_r.bufs[k % 2][:, (k // 2) * 512:(k // 2 + 1) * 512] for k in range(4)]
    for q in range(NT // 512):
        for b in (2 * q, 2 * q + 1):
            x, z = xT[:, b * S:(b + 1) * S], zT[:, b * S:(b + 1) * S]
            wait(dve, z_ready[b])
            e = mark("final", dve.scalar_tensor_tensor(out=z, in0=z, scalar=mcol(1, 5, b), in1=x,
                                                       op0=ALU.mult, op1=ALU.add))
        bank = one_bank.take()
        wait(pe, e, *bank.free)
        for k in range(4):
            e = mark("pe_out", pe.transpose(bank.t[:, k * P:(k + 1) * P],
                                            zT[:, q * 512 + k * P:q * 512 + (k + 1) * P], ident))
        wait(act, e)
        e = mark("out_rows", act.activation(orow[q], bank.t[:, :], ACT.Copy))
        bank.release(e)
        wait(sp, e)
        e_out = sg.dma("st_out", sp.dma_start(
            out.rearrange("b (c p) d -> p (b c) d", p=P)[:, 4 * q:4 * q + 4, :],
            orow[q].rearrange("p (k d) -> p k d", k=4)))
    wait(sp, e_out)
    ctx.close()


EARLY_SPACING = 10
LATE_SPACING = 8

_INS = ["L0_attn_x", "L0_attn_Wq", "L0_attn_bq", "L0_attn_Wk", "L0_attn_bk", "L0_attn_Wv", "L0_attn_bv",
        "L0_attn_Wo", "L0_attn_bo", "L0_attn_rw", "L0_ffn_W_gate", "L0_ffn_W_in", "L0_ffn_b_in", "L0_ffn_W_out",
        "L0_ffn_b_out", "L0_c", "L0_wmod", "L1_attn_W", "L1_ffn_Wqkv", "L1_ffn_q_scale", "L1_ffn_k_scale",
        "L1_ffn_Wo", "L1_ffn_ln_g", "L1_ffn_ln_b", "L1_ffn_W1", "L1_ffn_b1", "L1_ffn_W2", "L1_ffn_b2", "L1_c",
        "L1_wmod"]


def kernel(**inputs):
    import concourse.bacc as _bacc
    from concourse.bass_utils import run_bass_kernel_spmd as _run

    nc = _bacc.Bacc("TRN2", target_bir_lowering=False, num_devices=1)
    arrays, aps = {}, {}
    for name in _INS:
        arr = np.ascontiguousarray(inputs[name])
        arrays[f"in_{name}_dram"] = arr
        aps[name] = nc.dram_tensor(f"in_{name}_dram", arr.shape, mybir.dt.from_np(arr.dtype),
                                   kind="ExternalInput").ap()
    arrays["const_dram"] = constants()
    aps["const"] = nc.dram_tensor("const_dram", (P, NCONST), F32, kind="ExternalInput").ap()
    out = nc.dram_tensor("out_dram", (B, S, D), F32, kind="ExternalOutput").ap()
    build(nc, aps, out)
    r = _run(nc, [arrays], core_ids=[0])
    return r.results[0]["out_dram"]
```

```python
from contextlib import ExitStack

import numpy as np

import concourse.bass as bass
from concourse import mybir

F32 = mybir.dt.float32
F32R = mybir.dt.float32r
BF16 = mybir.dt.bfloat16
U32 = mybir.dt.uint32
ALU = mybir.AluOpType
ACT = mybir.ActivationFunctionType
AX = mybir.AxisListType

P = 128
D = 128
B, S = 8, 256
NT = B * S
TC = S // P
H0, DK0, F0 = 16, 8, 64
NF = H0 * F0
FC = NF // P
KVW = 2 * DK0 + 2
EPS0 = 1e-6
NE, DM = 8, 512
MC = DM // P
THRESH = 0.01
DEPTH, HEADS, DH, WIN = 6, 16, 64, 32
INNER = HEADS * DH
DI = int(D * 4 * 2 / 3)
DIC = [(j * P, min(P, DI - j * P)) for j in range((DI + P - 1) // P)]
QK_SCALE = 8.0
HP = HEADS // 2
WCHUNKS = 3 * INNER // 512
NW = P // WIN
LN_EPS = 1e-5
NEG = -1.0e30

ROWS = {}
for _name, _n in (("bq", 1), ("bk", 1), ("bo", 1), ("b_in", NE * MC), ("ln_g", DEPTH), ("ln_b", DEPTH),
                  ("b2", DEPTH), ("b1", DEPTH * 2 * len(DIC)), ("c0", B), ("c1", B)):
    ROWS[_name] = sum(n for _, n in ROWS.values()), _n
NROWS = sum(n for _, n in ROWS.values())
CONST = {}
for _name, _n in (("ident", P), ("rot", TC * 4 * DH), ("kvmask", FC * KVW), ("iota", NE), ("head", H0),
                  ("mask", 2 * 2 * WIN)):
    CONST[_name] = sum(n for _, n in CONST.values()), _n
NCONST = sum(n for _, n in CONST.values())
KEPT = CONST["kvmask"][0]


def constants():
    out = np.zeros((P, NCONST), np.float32)

    def put(name, a):
        at, n = CONST[name]
        out[:, at:at + n] = a.reshape(P, n)

    put("ident", np.eye(P, dtype=np.float32))
    f = np.float32
    half = np.arange(0, DH, 2, dtype=f)
    inv_freq = (f(1.0) / np.power(f(10000.0), half / f(DH))).astype(f)
    t = np.arange(S, dtype=f)
    freqs = t[:, None] * inv_freq[None, :]
    base = (half + f(0.4 * DH)) / f(1.4 * DH)
    power = (t - f(S // 2)) / f(WIN // 2)
    scale = np.power(base[None, :], power[:, None]).astype(f)
    cos, sin = np.cos(freqs).astype(f), np.sin(freqs).astype(f)
    two = lambda a, b: np.concatenate([a, b], -1)
    q_cos = two(cos * scale, cos * scale) * f(QK_SCALE)
    q_sin = two(-sin * scale, sin * scale) * f(QK_SCALE)
    inv = f(1.0) / scale
    k_cos = two(cos * inv, cos * inv)
    k_sin = two(-sin * inv, sin * inv)
    rot = np.stack([q_cos, q_sin, k_cos, k_sin], 1)
    put("rot", rot.reshape(TC, P, 4, DH).transpose(1, 0, 2, 3))
    m = np.zeros((P, FC, KVW), f)
    for h in range(2):
        m[h * F0:(h + 1) * F0, :, h * DK0:(h + 1) * DK0] = 1
        m[h * F0:(h + 1) * F0, :, 2 * DK0 + h] = 1
    put("kvmask", m)
    put("head", np.arange(P)[:, None] // DK0 == np.arange(H0)[None, :])
    put("iota", np.tile(np.arange(NE, dtype=f), (P, 1)))
    i, j = (np.arange(P) % WIN)[:, None], np.arange(2 * WIN)[None, :]
    bad = (j < i) | (j > i + WIN)
    first = bad | ((np.arange(P)[:, None] < WIN) & (j < WIN))
    put("mask", np.stack([np.where(first, f(NEG), f(0)), np.where(bad, f(NEG), f(0))], 1))
    return out


class Signals:

    def __init__(self, nc, ctx):
        self.nc, self.ctx = nc, ctx
        self.sems, self.count, self.seen, self.last = {}, {}, {}, {}

    def mark(self, stage, instruction, by=1):
        if stage not in self.sems:
            self.sems[stage] = self.ctx.enter_context(self.nc.semaphore("s_" + stage))
            self.count[stage] = 0
        self.count[stage] += by
        instruction.then_inc(self.sems[stage], by)
        self.last[stage] = (stage, self.count[stage])
        return self.last[stage]

    def dma(self, stage, instruction):
        return self.mark(stage, instruction, 16)

    def wait(self, engine, *events):
        for stage, value in events:
            key = (id(engine), stage)
            if self.seen.get(key, 0) < value:
                self.seen[key] = value
                engine.wait_ge(self.sems[stage], value)


class Slot:
    def __init__(self, ring, k):
        self.ring, self.k, self.t, self.free = ring, k, ring.bufs[k], ring.freed[k]

    def release(self, *events):
        self.ring.freed[self.k] = events
        self.ring.idle.append(self.k)


class Ring:

    def __init__(self, bufs):
        self.bufs, self.freed = bufs, [()] * len(bufs)
        self.idle = list(range(len(bufs)))

    def take(self):
        assert self.idle, "a buffer is taken before its last user is done with it"
        return Slot(self, self.idle.pop(0))


def interleave(units, spacing):
    live, n = [], 0
    slot = 0
    while live or n < len(units):
        if n < len(units) and slot >= n * spacing:
            live.append(units[n]())
            n += 1
        for g in list(live):
            try:
                next(g)
            except StopIteration:
                live.remove(g)
        slot += 1


def build(nc, a, out):
    ctx = ExitStack()
    sg = Signals(nc, ctx)
    mark, wait = sg.mark, sg.wait
    pe, dve, act, pool, sp = nc.tensor, nc.vector, nc.scalar, nc.gpsimd, nc.sync

    def mark_pool(stage, instruction):
        e = mark(stage, instruction)
        wait(pool, e)
        return e

    def sb(name, shape, dt=F32, where=ctx):
        return where.enter_context(nc.sbuf_tensor(name, shape, dt))

    def sb_ring(name, n, shape, dt=F32, where=ctx):
        return Ring([sb(f"{name}{k}", shape, dt, where) for k in range(n)])

    banks = [ctx.enter_context(nc.psum_tensor(f"bank{k}", [P, 512], F32)) for k in range(8)]

    xT = sb("xT", [P, NT])
    zT = sb("zT", [P, NT])
    const = sb("const", [P, KEPT])
    ones_d = sb("ones_d", [P, P])
    eps_ln = sb("eps_ln", [P, 1])
    ident_b = sb("ident_b", [P, P], BF16)
    mask_b = sb("mask_b", [P, 2, HP, 2 * WIN], BF16)
    cols = sb("cols", [P, NROWS])
    mod = [sb(f"mod{k}", [P, 6, B]) for k in range(2)]
    wqkv = [Ring([[sb(f"wqkv{n}_{part}", [P, 512], F32R) for part in ("hi", "lo")]]) for n in range(WCHUNKS)]
    wraw = sb_ring("wraw", 2, [P, 512])
    wo = sb_ring("wo", 1, [P, INNER // P, D])
    w1 = [Ring([[sb(f"w1_{half}_{part}", [P, DI], F32R) for part in ("hi", "lo")]]) for half in range(2)]
    w2 = sb_ring("w2", 1, [P, len(DIC), D])
    rot = sb_ring("rot", 2, [P, TC, 4, DH])
    gain = sb_ring("gain", 1, [P, 2, DH])

    early = ExitStack()
    const_e = sb("const_e", [P, NCONST - KEPT], F32, early)

    def cst(name):
        at, n = CONST[name]
        return const[:, at:at + n] if at < KEPT else const_e[:, at - KEPT:at - KEPT + n]

    ident = cst("ident")

    def col(name, k=0, rows=P):
        at = ROWS[name][0] + k
        return cols[0:rows, at:at + 1]

    def mcol(block, k, b):
        return mod[block][:, k, b:b + 1]

    def esb(name, shape, dt=F32):
        return sb(name, shape, dt, early)

    e_ones = mark_pool("ones", pool.memset(ones_d[:, :], 1.0 / D))
    e_eps = mark_pool("ones", pool.memset(eps_ln[:, :], LN_EPS))
    rows_m = esb("rows_m", [P, P])
    e_zero = mark("zero", dve.memset(rows_m[:, :], 0.0))
    kp_b = sb_ring("e_kp", 1, [P, TC, NF], F32, early)
    x_rows = kp_b.bufs[0][:, :, :].rearrange("p c (t d) -> p (c t) d", d=D)
    ev_ident = sg.dma("ld_ident", sp.dma_start(const[:, 0:P], a["const"][:, 0:P]))
    xr = a["L0_attn_x"].rearrange("b (c p) d -> p (b c) d", p=P)
    ev_x = [sg.dma(f"ld_x{q}", sp.dma_start(x_rows[:, 4 * q:4 * q + 4, :], xr[:, 4 * q:4 * q + 4, :]))
            for q in range(NT // P // 4)]
    wait(act, e_zero)

    def load_rows(name, src, n, k=0, width=P):
        at = ROWS[name][0] + k
        return sg.dma("ld_rows", act.dma_start(rows_m[at:at + n, 0:width], src))

    one_row = lambda v: v.rearrange("(o n) -> o n", o=1)
    load_rows("bq", one_row(a["L0_attn_bq"]), 1)
    load_rows("bk", one_row(a["L0_attn_bk"]), 1)
    load_rows("bo", one_row(a["L0_attn_bo"]), 1)
    load_rows("b_in", a["L0_ffn_b_in"].rearrange("e (m p) -> (e m) p", p=P), NE * MC)
    load_rows("ln_g", a["L1_ffn_ln_g"], DEPTH)
    load_rows("ln_b", a["L1_ffn_ln_b"], DEPTH)
    load_rows("b2", a["L1_ffn_b2"], DEPTH)
    full = len(DIC) - 1
    for part in range(2):
        k, src = part * len(DIC) * DEPTH, a["L1_ffn_b1"][:, part * DI:(part + 1) * DI]
        load_rows("b1", src[:, 0:full * P].rearrange("l (j p) -> j l p", p=P), full * DEPTH, k)
        load_rows("b1", src[:, full * P:], DEPTH, k + full * DEPTH, DI - full * P)
    load_rows("c0", a["L0_c"], B)
    ev_rows = load_rows("c1", a["L1_c"], B)

    wmod = [esb(f"wmod{k}", [P, 6 * D]) for k in range(2)]
    rf_rows = esb("rf_rows", [P, F0])
    w_q, w_k, w_v, w_o = (esb(n, [P, D]) for n in ("w_q", "w_k", "w_v", "w_o"))
    w_rf = esb("w_rf", [P, NF])
    bv_b = esb("bv_b", [P, D])
    w_gate = esb("w_gate", [P, NE])
    w_in = [[esb(f"w_in{e}_{part}", [P, DM], F32R) for part in ("hi", "lo")] for e in range(NE)]
    w_out = esb("w_out", [P, NE, MC, D])
    b_out = esb("b_out", [NE, D])
    w_c = esb("w_c", [P, D])
    ev_wmod = [sg.dma(f"ld_wmod{k}", sp.dma_start(wmod[k][:, :], a[f"L{k}_wmod"])) for k in range(2)]
    for t, n in ((w_q, "L0_attn_Wq"), (w_k, "L0_attn_Wk"), (w_v, "L0_attn_Wv"), (w_o, "L0_attn_Wo")):
        ev_w0 = sg.dma("ld_w0", sp.dma_start(t[:, :], a[n]))
    ev_w0 = sg.dma("ld_w0", sp.dma_start(bv_b[:, :], one_row(a["L0_attn_bv"]).to_broadcast([P, D])))
    ev_rf = sg.dma("ld_rf", sp.dma_start(rf_rows[:, :], a["L0_attn_rw"].rearrange("h d f -> (h d) f")))
    sg.dma("ld_const", sp.dma_start(const[:, P:], a["const"][:, P:KEPT]))
    ev_const = sg.dma("ld_const", sp.dma_start(const_e[:, :], a["const"][:, KEPT:]))
    wait(pool, ev_rf, ev_const)
    e_rf = mark_pool("rf", pool.tensor_tensor(
        w_rf[:, :].rearrange("p (h f) -> p h f", h=H0), rf_rows[:, :].unsqueeze(1).to_broadcast([P, H0, F0]),
        cst("head").unsqueeze(2).to_broadcast([P, H0, F0]), ALU.mult))
    layer_w = {l: {} for l in range(DEPTH)}

    def take_weights(l, name, ring):
        slot = ring.take()
        wait(sp, *slot.free)
        return slot

    def load_gain(l):
        slot = take_weights(l, "gain", gain)
        for j, n in enumerate(("q", "k")):
            e = sg.dma(f"ld_gain{l % 2}", sp.dma_start(slot.t[:, j, :],
                                                       a[f"L1_ffn_{n}_scale"][l:l + 1, :].to_broadcast([P, DH])))
        layer_w[l]["gain"] = slot, e

    chunks = [(l, n) for l in range(-1, DEPTH) for n in range(NE if l < 0 else WCHUNKS + 2)]
    raw_chunks = []

    def load_chunk():
        if not chunks:
            return
        (l, n), slot = chunks.pop(0), wraw.take()
        wait(sp, *slot.free)
        width = 512
        if l < 0:
            dst, src = slot.t[:, :], a["L0_ffn_W_in"][n]
        elif n < 2 * INNER // 512:
            dst, src = slot.t[:, :], a["L1_ffn_Wqkv"][l][:, n * 512:(n + 1) * 512]
        elif n < WCHUNKS:
            dst = slot.t[:, :].rearrange("d (hp e) -> d hp e", e=DH)
            src = a["L1_ffn_Wqkv"][l][:, 2 * INNER:].rearrange("d (hp r e) -> d r hp e", r=2, e=DH)
            src = src[:, n - 2 * INNER // 512, :, :]
        else:
            width, at = DI, (n - WCHUNKS) * DI
            dst, src = slot.t[:, 0:DI], a["L1_ffn_W1"][l][:, at:at + DI]
        raw_chunks.append((slot, width, sg.dma(f"ld_chunk{slot.k}", sp.dma_start(dst, src))))

    def split_chunk(hi, lo, free=()):
        src, width, e_ld = raw_chunks.pop(0)
        wait(pool, e_ld, *free)
        mark_pool("w_hi", pool.tensor_copy(hi[:, :], src.t[:, 0:width]))
        e = mark_pool("w_lo", pool.tensor_tensor(lo[:, :], src.t[:, 0:width], hi[:, :], ALU.subtract))
        src.release(e)
        load_chunk()
        return e

    def split_weights(l, n):
        slot = (wqkv[n] if n < WCHUNKS else w1[n - WCHUNKS]).take()
        layer_w[l][n] = slot, split_chunk(*slot.t, slot.free)

    load_chunk()
    load_chunk()
    ev_moe = sg.dma("ld_moe", sp.dma_start(w_gate[:, :], a["L0_ffn_W_gate"]))
    ev_moe = sg.dma("ld_moe", sp.dma_start(b_out[:, :], a["L0_ffn_b_out"]))
    for e in range(NE):
        ev_moe = sg.dma("ld_moe", sp.dma_start(w_out[:, e, :, :],
                                               a["L0_ffn_W_out"][e].rearrange("(m p) n -> p m n", p=P)))
    ev_wc = sg.dma("ld_wc", sp.dma_start(w_c[:, :], a["L1_attn_W"]))

    def load_output(l):
        slot = take_weights(l, "o", wo)
        layer_w[l]["o"] = slot, sg.dma("ld_wo", sp.dma_start(
            slot.t[:, :, :], a["L1_ffn_Wo"][l].rearrange("(c p) n -> p c n", p=P)))

    def load_down(l):
        slot = take_weights(l, "w2", w2)
        for j, (at, n) in enumerate(DIC):
            e = sg.dma("ld_w2", sp.dma_start(slot.t[0:n, j, :], a["L1_ffn_W2"][l][at:at + n, :]))
        layer_w[l]["w2"] = slot, e

    load_gain(0)
    load_output(0)
    load_down(0)

    work = hid_banks = y_banks = Ring(banks)

    e_xT = []
    for q in range(NT // P // 4):
        bk = work.take()
        wait(pe, ev_ident, ev_x[q], *bk.free)
        for k in range(4):
            e = mark("pe_x", pe.transpose(bk.t[:, k * P:(k + 1) * P], x_rows[:, 4 * q + k, :], ident))
        wait(act, e)
        e_xT.append(mark("xT", act.activation(xT[:, q * 512:(q + 1) * 512], bk.t[:, :], ACT.Copy)))
        bk.release(e_xT[-1])

    kp_b.freed[0] = (e,)

    bk = work.take()
    wait(pe, ev_rows, *bk.free)
    e = mark("pe_misc", pe.transpose(bk.t[:, 0:NROWS], rows_m[0:NROWS, :], ident[0:NROWS, 0:NROWS]))
    wait(dve, e)
    e_cols = mark("cols", dve.tensor_copy(cols[:, :], bk.t[:, 0:NROWS]))
    bk.release(e_cols)

    wcT = esb("wcT", [P, D])
    wsum = esb("wsum", [P, D])
    ones1 = esb("ones1", [P, P])
    prepared = {}
    tmp = esb("mod_tmp", [P, 4, 2 * B])

    def modulation(k):
        silu = esb(f"silu{k}", [P, B])
        at = ROWS[f"c{k}"][0]
        wait(act, e_cols)
        e_silu = mark("silu", act.activation(silu[:, :], cols[:, at:at + B], ACT.Silu))
        bk = work.take()
        wait(pe, e_silu, ev_wmod[k], *bk.free)
        for j in range(6):
            e = mark("pe_misc", pe.matmul(bk.t[:, j * B:(j + 1) * B], wmod[k][:, j * D:(j + 1) * D],
                                          silu[:, :], start=True, stop=True))
        wait(dve, e)
        e = mark("mod", dve.tensor_copy(mod[k][:, :, :], bk.t[:, 0:6 * B].rearrange("p (j b) -> p j b", b=B)))
        bk.release(e)
        wait(dve, e)
        for j in (1, 4):
            e = mark("mod", dve.tensor_scalar(mod[k][:, j, :], mod[k][:, j, :], 1.0, None, ALU.add))
        for j in (2, 5):
            g = mod[k][:, j, :]
            neg, mag, sgn = tmp[:, 0, 0:B], tmp[:, 1, 0:B], tmp[:, 2, 0:B]
            wait(dve, e)
            e = mark("mod", dve.tensor_scalar(neg, g, -1.0, None, ALU.mult))
            wait(dve, e)
            e = mark("mod", dve.tensor_tensor(mag, neg, g, ALU.max))
            e = mark("mod", dve.tensor_scalar(sgn, g, 0.0, 2.0, ALU.is_ge, ALU.mult))
            wait(dve, e)
            e = mark("mod", dve.tensor_scalar(mag, mag, 0.25, None, ALU.max))
            e = mark("mod", dve.tensor_scalar(sgn, sgn, -1.0, None, ALU.add))
            wait(dve, e)
            e = mark("mod", dve.tensor_tensor(g, mag, sgn, ALU.mult))
        return e

    prepared["mod0"] = modulation(0)

    def prepare_block1():
        prepared["mod1"] = modulation(1)
        wait(dve, ev_const)
        dve.tensor_copy(ident_b[:, :], ident)
        mview = cst("mask").rearrange("p (k j) -> p k j", k=2)
        for k in range(2):
            prepared["cst"] = mark("cst", dve.tensor_copy(mask_b[:, k, :, :],
                                                mview[:, k, :].unsqueeze(1).to_broadcast([P, HP, 2 * WIN])))

        e_one1 = mark_pool("ones", pool.memset(ones1[:, :], 1.0))
        bk = work.take()
        wait(pe, ev_wc, *bk.free)
        e = mark("pe_misc", pe.transpose(bk.t[:, 0:P], w_c[:, :], ident))
        wait(dve, e)
        e = mark("wsum", dve.tensor_copy(wcT[:, :], bk.t[:, 0:P]))
        bk.release(e)
        bk = work.take()
        wait(pe, e, e_one1, *bk.free)
        e = mark("pe_misc", pe.matmul(bk.t[:, 0:D], ones1[:, :], wcT[:, :], start=True, stop=True))
        wait(dve, e)
        e = prepared["wsum"] = mark("wsum", dve.tensor_copy(wsum[:, :], bk.t[:, 0:D]))
        bk.release(e)

    def pause(name):
        for _ in range(EARLY_PAUSES[name]):
            yield

    def layer_norm(src, ready, ring, buf, gain, shift, dst, dst_free, tag):
        xc, sq = buf[:, 0, :], buf[:, 1, :]
        bank = ring.take()
        mean = bank.t[:, 0:S]
        wait(pe, e_ones, *ready, *bank.free)
        e = mark("ln_mean", pe.matmul(mean, ones_d[:, :], src, start=True, stop=True))
        wait(dve, e, *ready)
        e_xc = mark("ln_xc", dve.tensor_tensor(xc, src, mean, ALU.subtract))
        wait(act, e_xc)
        bank.release(e_xc)
        e = mark("ln_sq", act.activation(sq, xc, ACT.Square))
        yield from pause(f"ln_sq_{tag}")
        bank = ring.take()
        var = bank.t[:, 0:S]
        wait(pe, e, *bank.free)
        e = mark("ln_var", pe.matmul(var, ones_d[:, :], sq, start=True, stop=True))
        wait(act, e, e_eps)
        e_sd = mark("ln_sd", act.activation(sq, var, ACT.Sqrt, bias=eps_ln[:, :]))
        bank.release(e_sd)
        yield from pause(f"ln_sd_{tag}")
        wait(dve, e_sd)
        e = mark("ln_out", dve.reciprocal(sq, sq))
        wait(dve, e)
        e = mark("ln_out", dve.tensor_tensor(xc, xc, sq, ALU.mult))
        wait(dve, e, *dst_free)
        e = mark("ln_out", dve.tensor_scalar(dst, xc, gain, shift, ALU.mult, ALU.add))
        yield from pause(f"ln_out_{tag}")
        return e

    def er(name, n, shape, dt=F32):
        return sb_ring(name, n, shape, dt, early)

    ln_buf = er("e_ln", 4, [P, 2, S])
    h_buf = er("e_h", 4, [P, S])
    qkT_b = er("e_qkT", 2, [P, 2, S])
    v_ext = er("e_vext", 2, [P, TC, FC, KVW])
    qp_b = er("e_qp", 1, [P, FC, S])
    kv_b = er("e_kv", 2, [P, FC, KVW])
    o_b = er("e_o", 3, [P, TC, D])
    oT_b = er("e_oT", 2, [P, S])
    sm_b = er("e_small", 4, [P, 64])
    hs_b = er("e_hs", 2, [P, 2, S], F32R)
    hid = er("e_hid", 3, [P, MC, S])
    acc_b = er("e_acc", 2, [P, TC, D])
    gate_b = er("e_gate", 3, [P, TC, 8 * NE])
    idx_b = er("e_idx", 3, [P, TC, NE], U32)
    cT_b = er("e_cT", 3, [NE, S])
    prob_b = er("e_prob", 2, [P, TC, S])
    sp_b = er("e_sp", 1, [P, TC, S])
    spT_b = er("e_spT", 2, [P, TC, S])
    hr_b = er("e_hr", 2, [P, TC, P])

    for slot in v_ext.bufs:
        e_vones = mark_pool("v_ones", pool.memset(slot[:, :, :, 2 * DK0:], 1.0))

    def early_unit(b):
        x = xT[:, b * S:(b + 1) * S]
        tok = lambda t, c: t[:, c * P:(c + 1) * P]
        x_in = e_xT[b * S // 512]

        lb, h = ln_buf.take(), h_buf.take()
        wait(dve, *lb.free, prepared["mod0"])
        e_h = yield from layer_norm(x, [x_in], work, lb.t, mcol(0, 1, b), mcol(0, 0, b), h.t[:, :], h.free, "a")
        lb.release(e_h)
        bank, qkT = work.take(), qkT_b.take()
        wait(pe, e_h, ev_w0, *bank.free)
        pe.matmul(bank.t[:, 0:S], w_q[:, :], h.t[:, :], start=True, stop=True)
        e = mark("pe_qk0", pe.matmul(bank.t[:, S:2 * S], w_k[:, :], h.t[:, :], start=True, stop=True))
        wait(act, e, e_cols, *qkT.free)
        act.activation(qkT.t[:, 0, :], bank.t[:, 0:S], ACT.Identity, bias=col("bq"))
        e_qk = mark("qkT0", act.activation(qkT.t[:, 1, :], bank.t[:, S:2 * S], ACT.Identity, bias=col("bk")))
        bank.release(e_qk)
        bank, vx = work.take(), v_ext.take()
        wait(pe, *bank.free)
        for c in range(TC):
            e_v = mark("pe_v0", pe.matmul(bank.t[:, c * D:(c + 1) * D], tok(h.t, c), w_v[:, :],
                                          start=True, stop=True))
        h.release(e_v)
        wait(dve, e_v, ev_w0, e_vones, *vx.free)
        for c in range(TC):
            e_vx = mark("vx", dve.tensor_tensor(
                vx.t[:, c, :, 0:2 * DK0],
                bank.t[:, c * D:(c + 1) * D].rearrange("p (f w) -> p f w", w=2 * DK0),
                bv_b[:, :].rearrange("p (f w) -> p f w", w=2 * DK0), ALU.add))
        bank.release(e_vx)
        yield from pause("features")
        kp = kp_b.take()
        wait(dve, *kp.free)
        for c in range(TC):
            for n in range(NF // 512):
                bank = work.take()
                wait(pe, e_qk, e_rf, *bank.free)
                e = mark("pe_kp", pe.matmul(bank.t[:, :], qkT.t[:, 1, c * P:(c + 1) * P],
                                            w_rf[:, n * 512:(n + 1) * 512], start=True, stop=True))
                wait(dve, e)
                e_kp = mark("kp", dve.tensor_scalar(kp.t[:, c, n * 512:(n + 1) * 512], bank.t[:, :],
                                                    0.0, EPS0, ALU.max, ALU.add))
                bank.release(e_kp)
            yield from pause("k_features")
        qp = qp_b.take()
        wait(dve, *qp.free)
        for f in range(0, FC, 2):
            bank = work.take()
            wait(pe, *bank.free)
            for k in range(2):
                e = mark("pe_qp", pe.matmul(bank.t[:, k * S:(k + 1) * S], w_rf[:, (f + k) * P:(f + k + 1) * P],
                                            qkT.t[:, 0, :], start=True, stop=True))
            wait(dve, e)
            e_qp = mark("qp", dve.tensor_scalar(qp.t[:, f:f + 2, :],
                                                bank.t[:, :].rearrange("p (k s) -> p k s", k=2),
                                                0.0, EPS0, ALU.max, ALU.add))
            bank.release(e_qp)
            if f == 2:
                yield from pause("q_features")
        qkT.release(e)
        yield from pause("q_features2")
        bank, kv = work.take(), kv_b.take()
        wait(pe, e_kp, e_vx, *bank.free)
        for f in range(FC):
            for c in range(TC):
                e_kv = mark("pe_kv", pe.matmul(bank.t[:, f * KVW:(f + 1) * KVW], kp.t[:, c, f * P:(f + 1) * P],
                                               vx.t[:, c, f, :], start=(c == 0), stop=(c == TC - 1)))
        kp.release(e_kv)
        vx.release(e_kv)
        wait(dve, e_kv, *kv.free)
        e_kvm = mark("kvm", dve.tensor_tensor(kv.t[:, :, :], bank.t[:, 0:FC * KVW].rearrange("p (f w) -> p f w", f=FC),
                                              cst("kvmask").rearrange("p (f w) -> p f w", f=FC), ALU.mult))
        bank.release(e_kvm)
        yield from pause("sums")
        bank, o, sm = work.take(), o_b.take(), sm_b.take()
        wait(pe, e_kvm, e_qp, *bank.free)
        for c in range(TC):
            for f in range(FC):
                at = c * S + f * KVW
                e = mark("pe_o0", pe.matmul(bank.t[:, at:at + KVW], qp.t[:, f, c * P:(c + 1) * P], kv.t[:, f, :],
                                            start=True, stop=True))
        qp.release(e)
        kv.release(e)
        wait(dve, e, *sm.free, *o.free)
        view = bank.t[:, :].rearrange("p (c n) -> p c n", c=TC)[:, :, 0:FC * KVW]\
            .rearrange("p c (f w) -> p c f w", w=KVW)
        for c in range(TC):
            e = mark("o0", dve.tensor_scalar(sm.t[:, c * H0:(c + 1) * H0].rearrange("p (f h) -> p f h", h=2),
                                             view[:, c, :, 2 * DK0:], EPS0, None, ALU.add))
        wait(dve, e)
        e = mark("o0", dve.reciprocal(sm.t[:, 0:TC * H0], sm.t[:, 0:TC * H0]))
        wait(dve, e)
        for c in range(TC):
            e_o = mark("o0", dve.tensor_tensor(
                o.t[:, c, :].rearrange("p (f h w) -> p f h w", h=2, w=DK0),
                view[:, c, :, 0:2 * DK0].rearrange("p f (h w) -> p f h w", h=2),
                sm.t[:, c * H0:(c + 1) * H0].rearrange("p (f h) -> p f h", h=2).unsqueeze(3)
                .to_broadcast([P, FC, 2, DK0]), ALU.mult))
        sm.release(e_o)
        bank.release(e_o)
        yield from pause("quotient")
        bank, oT = work.take(), oT_b.take()
        wait(pe, e_o, *bank.free)
        for c in range(TC):
            e = mark("pe_oT0", pe.transpose(bank.t[:, c * P:(c + 1) * P], o.t[:, c, :], ident))
        o.release(e)
        wait(act, e, *oT.free)
        e = mark("oT0", act.activation(oT.t[:, :], bank.t[:, 0:S], ACT.Copy))
        bank.release(e)
        yield from pause("oT")
        bank = work.take()
        wait(pe, e, *bank.free)
        e = mark("pe_wo0", pe.matmul(bank.t[:, 0:S], w_o[:, :], oT.t[:, :], start=True, stop=True))
        wait(dve, e)
        e = mark("x1", dve.tensor_scalar(oT.t[:, :], bank.t[:, 0:S], col("bo"), mcol(0, 2, b), ALU.add, ALU.mult))
        bank.release(e)
        wait(dve, e)
        e_x = mark("x1", dve.tensor_tensor(x, x, oT.t[:, :], ALU.add))
        oT.release(e_x)
        yield from pause("out0")

        if b == 0:
            prepare_block1()
        split_weights(0, b)

        lb, h = ln_buf.take(), h_buf.take()
        wait(dve, *lb.free)
        e_h = yield from layer_norm(x, [e_x], work, lb.t, mcol(0, 4, b), mcol(0, 3, b), h.t[:, :], h.free, "b")
        lb.release(e_h)
        hs = hs_b.take()
        wait(act, e_h, *hs.free)
        e = mark("h_hi", act.activation(hs.t[:, 0, :], h.t[:, :], ACT.Copy))
        wait(pool, e, e_h)
        e_hs = mark_pool("h_lo", pool.tensor_tensor(hs.t[:, 1, :], h.t[:, :], hs.t[:, 0, :], ALU.subtract))
        bank, gt, ix = work.take(), gate_b.take(), idx_b.take()
        wait(pe, e_h, ev_moe, *bank.free)
        for c in range(TC):
            e = e_gate = mark("pe_gate", pe.matmul(bank.t[:, c * NE:(c + 1) * NE], tok(h.t, c), w_gate[:, :],
                                          start=True, stop=True))
        LOG, TOP, IDX, COMB, TMP, SC = (slice(k * NE, (k + 1) * NE) for k in range(6))
        wait(dve, e, *gt.free, *ix.free)
        e = mark("gate", dve.tensor_copy(gt.t[:, :, LOG], bank.t[:, 0:TC * NE].rearrange("p (c n) -> p c n", c=TC)))
        bank.release(e)
        wait(dve, e)
        for c in range(TC):
            e = mark("gate", dve.max(gt.t[:, c, TOP], gt.t[:, c, LOG]))
            wait(dve, e)
            e = mark("gate", dve.max_index(ix.t[:, c, :], gt.t[:, c, TOP], gt.t[:, c, LOG]))
        wait(dve, e)
        e = mark("gate", dve.tensor_copy(gt.t[:, :, IDX], ix.t[:, :, :]))
        s0 = SC.start
        e_d = mark("gate", dve.tensor_tensor(gt.t[:, :, s0:s0 + 1], gt.t[:, :, NE + 1:NE + 2], gt.t[:, :, NE:NE + 1],
                                             ALU.subtract))
        ix.release(e_d)
        wait(act, e_d)
        e = mark("gate_exp", act.activation(gt.t[:, :, s0 + 1:s0 + 2], gt.t[:, :, s0:s0 + 1], ACT.Exp))
        yield from pause("top2")
        wait(dve, e)
        e = mark("gate", dve.tensor_scalar(gt.t[:, :, s0 + 2:s0 + 3], gt.t[:, :, s0 + 1:s0 + 2], 1.0, None, ALU.add))
        wait(dve, e)
        e = mark("gate", dve.reciprocal(gt.t[:, :, s0 + 3:s0 + 4], gt.t[:, :, s0 + 2:s0 + 3]))
        wait(dve, e)
        e = mark("gate", dve.tensor_tensor(gt.t[:, :, s0 + 4:s0 + 5], gt.t[:, :, s0 + 3:s0 + 4],
                                           gt.t[:, :, s0 + 1:s0 + 2], ALU.mult))
        wait(dve, e)
        for c in range(TC):
            dve.tensor_scalar(gt.t[:, c, COMB], cst("iota"), gt.t[:, c, 2 * NE:2 * NE + 1],
                              gt.t[:, c, s0 + 3:s0 + 4], ALU.is_equal, ALU.mult)
            e = mark("gate", dve.tensor_scalar(gt.t[:, c, TMP], cst("iota"), gt.t[:, c, 2 * NE + 1:2 * NE + 2],
                                               gt.t[:, c, s0 + 4:s0 + 5], ALU.is_equal, ALU.mult))
        wait(dve, e)
        e_comb = mark("gate", dve.tensor_tensor(gt.t[:, :, COMB], gt.t[:, :, COMB], gt.t[:, :, TMP], ALU.add))
        yield from pause("weights")
        bank, cT, acc = work.take(), cT_b.take(), acc_b.take()
        wait(pe, e_comb, *bank.free)
        for c in range(TC):
            e = mark("pe_cT", pe.transpose(bank.t[0:NE, c * P:(c + 1) * P], gt.t[:, c, COMB], ident))
        wait(dve, e, *cT.free)
        e = mark("gate", dve.tensor_copy(cT.t[:, :], bank.t[0:NE, 0:S]))
        bank.release(e)
        yield from pause("combine")
        bank = work.take()
        wait(pe, e, *bank.free)
        for c in range(TC):
            e = mark("pe_bout", pe.matmul(bank.t[:, c * D:(c + 1) * D], cT.t[:, c * P:(c + 1) * P], b_out[:, :],
                                          start=True, stop=True))
        cT.release(e)
        wait(dve, e, *acc.free)
        e_acc = mark("acc", dve.tensor_copy(acc.t[:, :, :], bank.t[:, 0:TC * D].rearrange("p (c n) -> p c n", c=TC)))
        bank.release(e_acc)
        h.release(e_gate, e_hs)
        hidden = {}
        for ex in range(NE + 1):
            if ex < NE:
                hd = hid.take()
                wait(act, *hd.free)
                for m in range(0, MC, 2):
                    bank = hid_banks.take()
                    wait(pe, e_hs, ev_w_in[ex], *bank.free)
                    for k in range(2):
                        (hi, lo), at = w_in[ex], slice((m + k) * P, (m + k + 1) * P)
                        y = bank.t[:, k * S:(k + 1) * S]
                        pe.matmul(y, hi[:, at], hs.t[:, 0, :], start=True, stop=False)
                        pe.matmul(y, hi[:, at], hs.t[:, 1, :], start=False, stop=False)
                        e = mark("pe_hid", pe.matmul(y, lo[:, at], hs.t[:, 0, :], start=False, stop=True))
                    wait(act, e)
                    for k in range(2):
                        e_hd = mark("hid", act.activation(hd.t[:, m + k, :], bank.t[:, k * S:(k + 1) * S], ACT.Gelu,
                                                          bias=col("b_in", ex * MC + m + k)))
                    bank.release(e_hd)
                hidden[ex] = hd, e_hd
                if ex == NE - 1:
                    hs.release(e)
            if ex > 0:
                hd, e_hd = hidden.pop(ex - 1)
                bank = y_banks.take()
                wait(pe, e_hd, *bank.free)
                for c in range(TC):
                    for m in range(MC):
                        e = mark("pe_y", pe.matmul(bank.t[:, c * D:(c + 1) * D], hd.t[:, m, c * P:(c + 1) * P],
                                                   w_out[:, ex - 1, m, :], start=(m == 0), stop=(m == MC - 1)))
                hd.release(e)
                wait(dve, e, e_acc)
                for c in range(TC):
                    e_acc = mark("acc", dve.scalar_tensor_tensor(
                        out=acc.t[:, c, :], in0=bank.t[:, c * D:(c + 1) * D],
                        scalar=gt.t[:, c, COMB.start + ex - 1:COMB.start + ex], in1=acc.t[:, c, :],
                        op0=ALU.mult, op1=ALU.add))
                bank.release(e_acc)
            yield from pause("experts")
        gt.release(e_acc)
        bank = work.take()
        wait(pe, e_acc, *bank.free)
        for c in range(TC):
            e = mark("pe_accT", pe.transpose(bank.t[:, c * P:(c + 1) * P], acc.t[:, c, :], ident))
        acc.release(e)
        wait(dve, e)
        e_x = mark("x2", dve.scalar_tensor_tensor(out=x, in0=bank.t[:, 0:S], scalar=mcol(0, 5, b), in1=x,
                                                  op0=ALU.mult, op1=ALU.add))
        bank.release(e_x)
        yield from pause("moe_out")

        lb, h = ln_buf.take(), h_buf.take()
        wait(dve, *lb.free, prepared["mod1"])
        e_h = yield from layer_norm(x, [e_x], work, lb.t, mcol(1, 1, b), mcol(1, 0, b), h.t[:, :], h.free, "c")
        lb.release(e_h)
        bank, hr = work.take(), hr_b.take()
        wait(pe, e_h, *bank.free)
        for c in range(TC):
            e = mark("pe_hr", pe.transpose(bank.t[:, c * P:(c + 1) * P], tok(h.t, c), ident))
        wait(act, e, *hr.free)
        e_hr = mark("hr", act.activation(hr.t[:, :, :], bank.t[:, 0:S].rearrange("p (c n) -> p c n", c=TC), ACT.Copy))
        bank.release(e_hr)
        bank, pr, sm = work.take(), prob_b.take(), sm_b.take()
        wait(pe, *bank.free)
        for c in range(TC):
            e = mark("pe_s1", pe.matmul(bank.t[:, c * S:(c + 1) * S], tok(h.t, c), h.t[:, :], start=True, stop=True))
        h.release(e)
        NM, SUM, RS, SPS, VAC = (slice(k * TC, (k + 1) * TC) for k in range(5))
        one = lambda s, c: sm.t[:, s.start + c:s.start + c + 1]
        scale = float(np.float32(1.0) / np.sqrt(np.float32(D)))
        wait(dve, e, *sm.free)
        e = mark("p1", dve.tensor_reduce(sm.t[:, NM], bank.t[:, :].rearrange("p (c s) -> p c s", c=TC), AX.X, ALU.max))
        wait(dve, e)
        e = mark("p1", dve.tensor_scalar(sm.t[:, NM], sm.t[:, NM], -scale, None, ALU.mult))
        yield from pause("scores")
        wait(act, e, *pr.free)
        for c in range(TC):
            e = mark("exp1", act.activation(pr.t[:, c, :], bank.t[:, c * S:(c + 1) * S], ACT.Exp, bias=one(NM, c),
                                            scale=scale, accum_out=one(SUM, c)))
        bank.release(e)
        yield from pause("exp")
        wait(dve, e)
        e = mark("p1", dve.reciprocal(sm.t[:, RS], sm.t[:, SUM]))
        wait(dve, e)
        spb = sp_b.take()
        for c in range(TC):
            e = mark("p1", dve.tensor_scalar(pr.t[:, c, :], pr.t[:, c, :], one(RS, c), None, ALU.mult))
        wait(dve, e, *spb.free)
        for c in range(TC):
            e = mark("p1", dve.scalar_tensor_tensor(out=spb.t[:, c, :], in0=pr.t[:, c, :], scalar=THRESH,
                                                    in1=pr.t[:, c, :], op0=ALU.is_lt, op1=ALU.mult,
                                                    accum_out=one(VAC, c)))
            wait(dve, e)
            e = mark("p1", dve.scalar_tensor_tensor(out=spb.t[:, c, :], in0=pr.t[:, c, :], scalar=THRESH,
                                                    in1=pr.t[:, c, :], op0=ALU.is_ge, op1=ALU.mult,
                                                    accum_out=one(SPS, c)))
        e_sp = e
        pr.release(e)
        wait(dve, e)
        e = mark("p1", dve.tensor_scalar(sm.t[:, SPS], sm.t[:, SPS], 1e-9, None, ALU.add))
        wait(dve, e)
        e = mark("p1", dve.reciprocal(sm.t[:, SPS], sm.t[:, SPS]))
        e = mark("p1", dve.tensor_scalar(sm.t[:, VAC], sm.t[:, VAC], 0.01, None, ALU.mult))
        e_sm = e
        yield from pause("threshold")
        bank, spT = work.take(), spT_b.take()
        wait(pe, e_sp, *bank.free)
        for k in range(TC):
            for c in range(TC):
                e = mark("pe_spT", pe.transpose(bank.t[:, k * S + c * P:k * S + (c + 1) * P],
                                                spb.t[:, c, k * P:(k + 1) * P], ident))
        spb.release(e)
        wait(act, e, *spT.free)
        e = mark("spT", act.activation(spT.t[:, :, :], bank.t[:, :].rearrange("p (k s) -> p k s", k=TC), ACT.Copy))
        bank.release(e)
        yield from pause("spT")
        bank, o = work.take(), o_b.take()
        wait(pe, e, e_hr, *bank.free)
        for c in range(TC):
            for k in range(TC):
                e = mark("pe_at1", pe.matmul(bank.t[:, c * D:(c + 1) * D], spT.t[:, k, c * P:(c + 1) * P],
                                             hr.t[:, k, :], start=(k == 0), stop=(k == TC - 1)))
        spT.release(e)
        hr.release(e)
        wait(dve, e, e_sm, prepared["wsum"], *o.free)
        for c in range(TC):
            e = mark("at1", dve.tensor_scalar(o.t[:, c, :], bank.t[:, c * D:(c + 1) * D], one(SPS, c), None, ALU.mult))
        bank.release(e)
        wait(dve, e)
        for c in range(TC):
            e = mark("at1", dve.scalar_tensor_tensor(out=o.t[:, c, :], in0=wsum[:, :], scalar=one(VAC, c),
                                                     in1=o.t[:, c, :], op0=ALU.mult, op1=ALU.add))
        sm.release(e)
        yield from pause("attend")
        bank = work.take()
        wait(pe, e, *bank.free)
        for c in range(TC):
            e = mark("pe_atT", pe.transpose(bank.t[:, c * P:(c + 1) * P], o.t[:, c, :], ident))
        o.release(e)
        wait(dve, e)
        e_x = mark("x3", dve.scalar_tensor_tensor(out=x, in0=bank.t[:, 0:S], scalar=mcol(1, 2, b), in1=x,
                                                  op0=ALU.mult, op1=ALU.add))
        bank.release(e_x)
        yield from pause("back")
        lb = ln_buf.take()
        wait(dve, *lb.free)
        e = yield from layer_norm(x, [e_x], work, lb.t, mcol(1, 4, b), mcol(1, 3, b), zT[:, b * S:(b + 1) * S], (), "d")
        lb.release(e)
        early_done.append(e)

    ev_w_in = [split_chunk(*w_in[e]) for e in range(NE)]
    early_done = []
    interleave([lambda b=b: early_unit(b) for b in range(B)], EARLY_SPACING)

    everything = [sg.last[s] for s in sg.last if not s.startswith("ld_")] + [ev_rows]
    for engine in (pe, dve, act, pool, sp):
        wait(engine, *everything)
    early.close()

    one_bank = Ring(banks[0:4])
    s_banks = Ring([banks[4:6]])
    o_banks = Ring([banks[6:8]])

    xs_r = sb_ring("xs", 2, [P, 2, S], F32R)
    raw_r = sb_ring("raw", 2, [P, 2 * INNER])
    rt_r = sb_ring("rt", 2, [P, 2 * INNER])
    t2_r = sb_ring("t2", 1, [P, 2 * INNER])
    rn_r = sb_ring("rn", 2, [P, TC, 2 * HEADS])
    qT_r = sb_ring("qT", 2, [P, HP, P])
    kT_r = sb_ring("kT", 2, [P, HP, WIN + S])
    vn_r = sb_ring("vn", 2, [P, INNER])
    v2_r = sb_ring("v2", 3, [P, NW, HP * DH])
    p_r = sb_ring("p", 2, [P, HP, 2, 2 * WIN])
    pT_r = sb_ring("pT", 2, [P, HP, P])
    sm_r = sb_ring("sm", 2, [P, 4, HEADS])
    oa_r = sb_ring("oa", 1, [P, HP, 2, DH])
    oT_r = sb_ring("oT", 1, [P, INNER // P, S])
    xf_r = sb_ring("xf", 2, [P, S])
    lnf_r = sb_ring("lnf", 1, [P, 2, S])
    hn_r = sb_ring("hn", 1, [P, 2, S], F32R)
    g_r = sb_ring("g", 2, [P, S])
    hh_r = sb_ring("hh", 1, [P, len(DIC), S])

    for t in xf_r.bufs:
        e_z = mark_pool("zpad", pool.memset(t[DH:P, 0:1], 0.0))
    for t in xs_r.bufs:
        e_z = mark_pool("zpad", pool.memset(t[DH:P, :, 0:1].bitcast(F32), 0.0))
    for t in kT_r.bufs:
        e_z = mark_pool("zpad", pool.memset(t[:, :, 0:WIN], 0.0))
    for t in v2_r.bufs:
        e_z = mark_pool("zpad", pool.memset(t[:, 0, :], 0.0))

    z_ready = {b: early_done[b] for b in range(B)}
    tables = {}

    def layer_tables(l):
        slot = rot.take()
        src = cst("rot").rearrange("p (c k d) -> p c k d", c=TC, k=4)
        gn, e_gain = layer_w[l]["gain"]
        wait(dve, e_gain, *slot.free)
        for k in range(4):
            g = gn.t[:, k // 2, :].rearrange("p (h d) -> p h d", h=2)
            if k % 2:
                g = g[:, ::-1, :]
            for c in range(TC):
                e = mark("tables", dve.tensor_tensor(
                    slot.t[:, c, k, :].rearrange("p (h d) -> p h d", h=2),
                    src[:, c, k, :].rearrange("p (h d) -> p h d", h=2), g, ALU.mult))
        gn.release(e)
        tables[l] = slot, e

    def shifted(dst, src):
        act.activation(dst[0:DH, :], src[0:DH, :], ACT.Copy)
        return mark("shift", act.activation(dst[DH:P, 1:S], src[DH:P, 0:S - 1], ACT.Copy))

    def store(q):
        for b in (2 * q, 2 * q + 1):
            x, z = xT[:, b * S:(b + 1) * S], zT[:, b * S:(b + 1) * S]
            wait(dve, z_ready[b])
            e = mark("final", dve.scalar_tensor_tensor(out=z, in0=z, scalar=mcol(1, 5, b), in1=x,
                                                       op0=ALU.mult, op1=ALU.add))
        bank, rows = one_bank.take(), wraw.take()
        wait(pe, e, *bank.free)
        for k in range(4):
            e = mark("pe_out", pe.transpose(bank.t[:, k * P:(k + 1) * P],
                                            zT[:, q * 512 + k * P:q * 512 + (k + 1) * P], ident))
        wait(act, e, *rows.free)
        e = mark("out_rows", act.activation(rows.t[:, :], bank.t[:, :], ACT.Copy))
        bank.release(e)
        wait(sp, e)
        e = sg.dma(f"st_out{rows.k}", sp.dma_start(
            out.rearrange("b (c p) d -> p (b c) d", p=P)[:, 4 * q:4 * q + 4, :],
            rows.t[:, :].rearrange("p (k d) -> p k d", k=4)))
        rows.release(e)
        stored.append(e)

    stored = []

    def unit(l, b):
        z = zT[:, b * S:(b + 1) * S]
        last_of_layer = b == B - 1
        pairs = lambda t, n=HEADS: t.rearrange("p (n h d) -> p n h d", h=2, d=DH // 2)
        heads = lambda t: t.rearrange("p (n d) -> p n d", d=DH)
        four = lambda bank: bank.t[:, :].rearrange("p (n i) -> p n i", n=4)
        per_chunk = lambda: [None] * TC
        raw, rt, t2, vn, v2, qT, pb, sm, pT, oa = (per_chunk() for _ in range(10))
        e_cos, e_sin = per_chunk(), per_chunk()
        e_raw, e_ss, e_rot, e_nrm, e_qkT, e_vn, e_v2, e_s, e_exp, e_sum, e_pT, e_o, e_oa, e_oT = \
            (per_chunk() for _ in range(14))
        held = {}

        def start():
            if b == 0:
                layer_tables(l)
            if b == 2 and l + 1 < DEPTH:
                load_gain(l + 1)
            xs = held["xs"] = xs_r.take()
            wait(act, z_ready[b], e_z, *xs.free)
            held["e_xh"] = shifted(xs.t[:, 0, :], z)

        def split_xs():
            hi, lo = held["xs"].t[:, 0, :], held["xs"].t[:, 1, :]
            wait(pool, held["e_xh"])
            mark_pool("xs_lo", pool.tensor_tensor(lo[0:DH, :], z[0:DH, :], hi[0:DH, :], ALU.subtract))
            held["e_xs"] = mark_pool("xs_lo", pool.tensor_tensor(lo[DH:P, 1:S], z[DH:P, 0:S - 1], hi[DH:P, 1:S],
                                                                 ALU.subtract))

        def product(stage, bank, c, n):
            w, e_w = layer_w[l][n]
            tok = slice(c * P, (c + 1) * P)
            hi, lo = held["xs"].t[:, 0, tok], held["xs"].t[:, 1, tok]
            wait(pe, held["e_xs"], e_w, *bank.free)
            pe.matmul(bank.t[:, :], hi, w.t[0][:, :], start=True, stop=False)
            pe.matmul(bank.t[:, :], hi, w.t[1][:, :], start=False, stop=False)
            e = mark(stage, pe.matmul(bank.t[:, :], lo, w.t[0][:, :], start=False, stop=True))
            if last_of_layer and c == TC - 1:
                w.release(e)
            return e

        def next_weights(n):
            if last_of_layer and l + 1 < DEPTH:
                split_weights(l + 1, n)

        def project(c, n):
            if n == 0:
                raw[c] = raw_r.take()
            bank = one_bank.take()
            e = product("pe_qk", bank, c, n)
            wait(act, e, *raw[c].free)
            e_raw[c] = mark("raw", act.activation(raw[c].t[:, n * 512:(n + 1) * 512], bank.t[:, :], ACT.Copy))
            bank.release(e_raw[c])

        def square(c):
            held["sq"] = t2_r.take()
            wait(act, e_raw[c], *held["sq"].free)
            held["e_sq"] = mark("sq", act.activation(held["sq"].t[:, :], raw[c].t[:, :], ACT.Square))

        def sum_squares(c):
            if c == 0:
                held["rn"] = rn_r.take()
            rn = held["rn"]
            wait(dve, held["e_sq"], *(rn.free if c == 0 else ()))
            e_ss[c] = mark("ss", dve.tensor_reduce(rn.t[:, c, :], heads(held["sq"].t[:, :]), AX.X, ALU.add))
            held["sq"].release(e_ss[c])

        def rotate(c):
            tab, e_tab = tables[l]
            rt[c], t2[c] = rt_r.take(), t2_r.take()
            wait(pool, e_raw[c], e_tab, *rt[c].free)
            wait(dve, e_raw[c], e_tab, *t2[c].free)
            for k in range(2):
                part = slice(k * INNER, (k + 1) * INNER)
                cosv = tab.t[:, c, 2 * k, :].unsqueeze(1).to_broadcast([P, HEADS, DH])
                sinv = tab.t[:, c, 2 * k + 1, :].rearrange("p (h d) -> p h d", h=2).unsqueeze(1)\
                    .to_broadcast([P, HEADS, 2, DH // 2])
                e_cos[c] = mark_pool("rot_cos", pool.tensor_tensor(heads(rt[c].t[:, part]), heads(raw[c].t[:, part]),
                                                                   cosv, ALU.mult))
                e_sin[c] = mark("rot_sin", dve.tensor_tensor(pairs(t2[c].t[:, part]),
                                                             pairs(raw[c].t[:, part])[:, :, ::-1, :], sinv, ALU.mult))
            raw[c].release(e_cos[c], e_sin[c])
            if last_of_layer and c == TC - 1:
                tab.release(e_cos[c], e_sin[c])

        def rotate_add(c):
            wait(pool, e_sin[c])
            e_rot[c] = mark_pool("rot_add", pool.tensor_tensor(rt[c].t[:, :], rt[c].t[:, :], t2[c].t[:, :], ALU.add))
            t2[c].release(e_rot[c])

        def norm_root():
            rn = held["rn"]
            wait(act, *e_ss)
            held["e_norm"] = mark("norm", act.activation(rn.t[:, :, :], rn.t[:, :, :], ACT.Sqrt))

        def norm_inverse():
            rn = held["rn"]
            wait(dve, held["e_norm"])
            e = mark("rn", dve.tensor_scalar(rn.t[:, :, :], rn.t[:, :, :], 1e-12, None, ALU.max))
            wait(dve, e)
            held["e_rn"] = mark("rn", dve.reciprocal(rn.t[:, :, :], rn.t[:, :, :]))

        def normalise(c):
            v, rn = heads(rt[c].t[:, :]), held["rn"]
            wait(dve, held["e_rn"], e_rot[c])
            e_nrm[c] = mark("nrm", dve.tensor_tensor(v, v, rn.t[:, c, :].unsqueeze(2)
                                                     .to_broadcast([P, 2 * HEADS, DH]), ALU.mult))
            if c == TC - 1:
                rn.release(e_nrm[c])

        def transpose_qk(c, k):
            if k == 0:
                qT[c] = qT_r.take()
                if c == 0:
                    held["kT"] = kT_r.take()
            bank = one_bank.take()
            wait(pe, e_nrm[c], *bank.free)
            for n in range(4):
                at = (4 * k + n) * P
                e = mark("pe_qkT", pe.transpose(bank.t[:, n * P:(n + 1) * P], rt[c].t[:, at:at + P], ident))
            if k == 3:
                rt[c].release(e)
            if k < 2:
                wait(act, e, *qT[c].free)
                dst = qT[c].t[:, 4 * k:4 * k + 4, :]
            else:
                kT = held["kT"]
                wait(act, e, *(kT.free if c == 0 else ()))
                dst = kT.t[:, 4 * (k - 2):4 * (k - 2) + 4, WIN + c * P:WIN + (c + 1) * P]
            e_qkT[c] = mark("qkT", act.activation(dst, four(bank), ACT.Copy))
            bank.release(e_qkT[c])

        def values(c, r):
            if r == 0:
                vn[c] = vn_r.take()
            bank = one_bank.take()
            e = product("pe_v", bank, c, 2 * INNER // 512 + r)
            wait(act, e, *vn[c].free)
            e_vn[c] = mark("vn", act.activation(vn[c].t[:, r * 512:(r + 1) * 512], bank.t[:, :], ACT.Copy))
            bank.release(e_vn[c])
            if (c, r) == (TC - 1, 1):
                held["xs"].release(e)

        def pair_values(c):
            v2[c] = v2_r.take()
            wait(sp, e_vn[c], e_z, *v2[c].free)
            for g in range(NW):
                for half in range(2):
                    v = NW * c + g - 1 + half
                    if v < 0:
                        continue
                    src = vn[v // NW].t[WIN * (v % NW):WIN * (v % NW + 1), :]
                    for r in range(2):
                        at = 2 * WIN * r + WIN * half
                        e = sg.dma(f"v2_{v2[c].k}", sp.dma_start(v2[c].t[at:at + WIN, g, :],
                                                                 src[:, r * 512:(r + 1) * 512]))
            e_v2[c] = e
            if c == TC - 1:
                vn[0].release(e_v2[0], e)
                vn[1].release(e)

        def scores(c, *windows):
            if windows[0] == 0:
                held["s"] = s_banks.take()
                wait(pe, prepared["cst"], *e_qkT[0:c + 1], *held["s"].free)
                for r in range(2):
                    pe.matmul(held["s"].t[r][:, :], ident_b[:, :],
                              mask_b[:, min(c, 1), :, :].rearrange("p h j -> p (h j)"),
                              start=True, stop=False, skip_group_check=True)
            for g in windows:
                k0 = c * P + g * WIN
                for hp in range(HP):
                    for r in range(2):
                        rows = slice(2 * WIN * r, 2 * WIN * (r + 1))
                        e = pe.matmul(held["s"].t[r][WIN * g:WIN * (g + 1), hp * 2 * WIN:(hp + 1) * 2 * WIN],
                                      qT[c].t[rows, hp, WIN * g:WIN * (g + 1)], held["kT"].t[rows, hp, k0:k0 + 2 * WIN],
                                      start=False, stop=True, skip_group_check=True)
            if windows[-1] == NW - 1:
                e_s[c] = mark("pe_s", e)
                qT[c].release(e_s[c])
                if c == TC - 1:
                    held["kT"].release(e_s[c])

        by_head = lambda bank: bank[:, :].rearrange("p (h j) -> p h j", h=HP)

        def softmax_in(c):
            pb[c], sm[c], s = p_r.take(), sm_r.take(), held["s"]
            wait(dve, e_s[c], *sm[c].free, *pb[c].free)
            for r in range(2):
                e = mark("smax", dve.tensor_reduce(sm[c].t[:, r, 0:HP], by_head(s.t[r]), AX.X, ALU.max))
            wait(dve, e)
            for r in range(2):
                e = mark("smax", dve.tensor_tensor(pb[c].t[:, :, r, :], by_head(s.t[r]), sm[c].t[:, r, 0:HP]
                                                   .unsqueeze(2).to_broadcast([P, HP, 2 * WIN]), ALU.subtract))
            s.release(e)
            wait(act, e)
            e_exp[c] = mark("exp", act.activation(pb[c].t[:, :, :, :], pb[c].t[:, :, :, :], ACT.Exp))

        def softmax_sum(c):
            wait(dve, e_exp[c])
            e = mark("ssum", dve.tensor_reduce(sm[c].t[:, 2, :].rearrange("p (h r) -> p h r", r=2),
                                               pb[c].t[:, :, :, :], AX.X, ALU.add))
            wait(dve, e)
            e_sum[c] = mark("ssum", dve.reciprocal(sm[c].t[:, 3, :], sm[c].t[:, 2, :]))
            held["p_sum", c] = e

        def transpose_p(c, k):
            if k == 0:
                pT[c] = pT_r.take()
            bank = one_bank.take()
            wait(pe, e_exp[c], *bank.free)
            for n in range(4):
                e = mark("pe_pT", pe.transpose(bank.t[:, n * P:(n + 1) * P],
                                               pb[c].t[:, 4 * k + n, :, :].rearrange("p r j -> p (r j)"), ident))
            wait(act, e, *pT[c].free)
            e_pT[c] = mark("pT", act.activation(pT[c].t[:, 4 * k:4 * k + 4, :], four(bank), ACT.Copy))
            bank.release(e_pT[c])
            if k == 1:
                pb[c].release(e, held["p_sum", c])

        def attend(c, *windows):
            if windows[0] == 0:
                held["o"] = o_banks.take()
                wait(pe, e_pT[c], e_v2[c], *held["o"].free)
            for g in windows:
                for hp in range(HP):
                    for r in range(2):
                        rows = slice(2 * WIN * r, 2 * WIN * (r + 1))
                        e = pe.matmul(held["o"].t[r][WIN * g:WIN * (g + 1), hp * DH:(hp + 1) * DH],
                                      pT[c].t[rows, hp, WIN * g:WIN * (g + 1)],
                                      v2[c].t[rows, g, hp * DH:(hp + 1) * DH], start=True, stop=True)
            if windows[-1] == NW - 1:
                e_o[c] = mark("pe_o", e)
                pT[c].release(e_o[c])
                v2[c].release(e_o[c])

        def attended(c):
            oa[c] = oa_r.take()
            wait(dve, e_o[c], e_sum[c], *oa[c].free)
            inv = sm[c].t[:, 3, :].rearrange("p (h r) -> p h r", r=2)
            for r in range(2):
                e_oa[c] = mark("oa", dve.tensor_tensor(oa[c].t[:, :, r, :], by_head(held["o"].t[r]),
                                                       inv[:, :, r:r + 1].to_broadcast([P, HP, DH]), ALU.mult))
            held["o"].release(e_oa[c])
            sm[c].release(e_oa[c])

        def transpose_o(c, k):
            if c == 0 and k == 0:
                held["oT"] = oT_r.take()
            bank, oT = one_bank.take(), held["oT"]
            wait(pe, e_oa[c], *bank.free)
            for n in range(4):
                e = mark("pe_oT", pe.transpose(bank.t[:, n * P:(n + 1) * P],
                                               oa[c].t[:, 4 * k + n, :, :].rearrange("p r e -> p (r e)"), ident))
            if k == 1:
                oa[c].release(e)
            wait(act, e, *oT.free)
            e_oT[c] = mark("oT", act.activation(oT.t[:, 4 * k:4 * k + 4, c * P:(c + 1) * P], four(bank), ACT.Copy))
            bank.release(e_oT[c])

        def project_out():
            (w, e_w), oT, bank = layer_w[l]["o"], held["oT"], one_bank.take()
            wait(pe, *e_oT, e_w, *bank.free)
            for k in range(INNER // P):
                e = mark("pe_wo", pe.matmul(bank.t[:, 0:S], w.t[:, k, :], oT.t[:, k, :],
                                            start=(k == 0), stop=(k == INNER // P - 1)))
            oT.release(e)
            if last_of_layer:
                w.release(e)
                if l + 1 < DEPTH:
                    load_output(l + 1)
            held["wo"] = bank, e

        def add_attention():
            bank, e = held["wo"]
            wait(dve, e)
            held["e_z1"] = mark("z_mid", dve.tensor_tensor(z, z, bank.t[:, 0:S], ALU.add))
            bank.release(held["e_z1"])
            held["xf"] = xf_r.take()
            wait(act, held["e_z1"], e_z, *held["xf"].free)
            held["e_xf"] = shifted(held["xf"].t, z)

        def ln_mean():
            bank = one_bank.take()
            wait(pe, held["e_xf"], *bank.free)
            held["mean"] = bank, mark("ln_mean", pe.matmul(bank.t[:, 0:S], ones_d[:, :], held["xf"].t[:, :],
                                                           start=True, stop=True))

        def ln_centre():
            (bank, e), xf, lb = held["mean"], held["xf"], lnf_r.take()
            held["lb"] = lb
            wait(dve, e, held["e_xf"], *lb.free)
            e = mark("ln_xc", dve.tensor_tensor(lb.t[:, 0, :], xf.t[:, :], bank.t[:, 0:S], ALU.subtract))
            bank.release(e)
            xf.release(e)
            wait(act, e)
            held["e_lnsq"] = mark("ln_sq", act.activation(lb.t[:, 1, :], lb.t[:, 0, :], ACT.Square))

        def ln_variance():
            bank, lb = one_bank.take(), held["lb"]
            wait(pe, held["e_lnsq"], *bank.free)
            e = mark("ln_var", pe.matmul(bank.t[:, 0:S], ones_d[:, :], lb.t[:, 1, :], start=True, stop=True))
            wait(act, e)
            held["e_sd"] = mark("ln_sd", act.activation(lb.t[:, 1, :], bank.t[:, 0:S], ACT.Sqrt, bias=eps_ln[:, :]))
            bank.release(held["e_sd"])

        def ln_out():
            lb, hn = held["lb"], hn_r.take()
            xc, sd = lb.t[:, 0, :], lb.t[:, 1, :]
            wait(dve, held["e_sd"])
            e = mark("ln_out", dve.reciprocal(sd, sd))
            wait(dve, e)
            e = mark("ln_out", dve.tensor_tensor(xc, xc, sd, ALU.mult))
            wait(dve, e)
            e = mark("ln_out", dve.tensor_scalar(xc, xc, col("ln_g", l), col("ln_b", l), ALU.mult, ALU.add))
            wait(dve, e, *hn.free)
            e = mark("ln_out", dve.tensor_copy(hn.t[:, 0, :], xc))
            wait(dve, e)
            e = mark("ln_out", dve.tensor_tensor(hn.t[:, 1, :], xc, hn.t[:, 0, :], ALU.subtract))
            lb.release(e)
            held["hn"] = hn, e

        def up(j):
            (hn, e_hn), (at, n) = held["hn"], DIC[j]
            bank, g = one_bank.take(), g_r.take()
            wait(pe, e_hn, *bank.free)
            for half in range(2):
                w, e_w = layer_w[l][WCHUNKS + half]
                y, cut = bank.t[0:n, half * S:(half + 1) * S], slice(at, at + n)
                wait(pe, e_w)
                pe.matmul(y, w.t[0][:, cut], hn.t[:, 0, :], start=True, stop=False)
                pe.matmul(y, w.t[0][:, cut], hn.t[:, 1, :], start=False, stop=False)
                e_up = mark("pe_w1", pe.matmul(y, w.t[1][:, cut], hn.t[:, 0, :], start=False, stop=True))
                if last_of_layer and j == len(DIC) - 1:
                    w.release(e_up)
            wait(act, e_up, *g.free)
            e = mark("gelu", act.activation(g.t[0:n, :], bank.t[0:n, S:2 * S], ACT.Gelu,
                                            bias=col("b1", (len(DIC) + j) * DEPTH + l, n)))
            held["up", j] = bank, g, e
            if j == len(DIC) - 1:
                hn.release(e_up)

        def gate(j):
            (bank, g, e), (at, n) = held["up", j], DIC[j]
            if j == 0:
                held["hh"] = hh_r.take()
            hh = held["hh"]
            wait(dve, e, *(hh.free if j == 0 else ()))
            held["e_hh"] = mark("hh", dve.scalar_tensor_tensor(
                out=hh.t[0:n, j, :], in0=bank.t[0:n, 0:S], scalar=col("b1", j * DEPTH + l, n), in1=g.t[0:n, :],
                op0=ALU.add, op1=ALU.mult))
            g.release(held["e_hh"])
            bank.release(held["e_hh"])

        def down():
            (w, e_w), hh, bank = layer_w[l]["w2"], held["hh"], one_bank.take()
            wait(pe, held["e_hh"], e_w, *bank.free)
            for j, (at, n) in enumerate(DIC):
                e = mark("pe_w2", pe.matmul(bank.t[:, 0:S], w.t[0:n, j, :], hh.t[0:n, j, :],
                                            start=(j == 0), stop=(j == len(DIC) - 1)))
            hh.release(e)
            if last_of_layer:
                w.release(e)
                if l + 1 < DEPTH:
                    load_down(l + 1)
            held["down"] = bank, e

        def add_ffn():
            bank, e = held["down"]
            wait(dve, e, held["e_xf"])
            z_ready[b] = mark("z_out", dve.scalar_tensor_tensor(out=z, in0=bank.t[:, 0:S], scalar=col("b2", l), in1=z,
                                                                op0=ALU.add, op1=ALU.add))
            bank.release(z_ready[b])

        def finish():
            if l == DEPTH - 1 and b % 2:
                store(b // 2)

        steps = dict(start=start, split_xs=split_xs, project=project, next_weights=next_weights, square=square,
                     sum_squares=sum_squares, rotate=rotate, rotate_add=rotate_add, norm_root=norm_root,
                     norm_inverse=norm_inverse, normalise=normalise, transpose_qk=transpose_qk, values=values,
                     pair_values=pair_values, scores=scores, softmax_in=softmax_in, softmax_sum=softmax_sum,
                     transpose_p=transpose_p, attend=attend, attended=attended, transpose_o=transpose_o,
                     project_out=project_out, add_attention=add_attention, ln_mean=ln_mean, ln_centre=ln_centre,
                     ln_variance=ln_variance, ln_out=ln_out, up=up, gate=gate, down=down, add_ffn=add_ffn,
                     finish=finish)
        for slot in range(max(s for s, *_ in LATE_PLAN) + 1):
            for s, step, *args in LATE_PLAN:
                if s == slot:
                    steps[step](*args)
            yield

    interleave([lambda l=l, b=b: unit(l, b) for l in range(DEPTH) for b in range(B)], LATE_SPACING)

    wait(sp, *stored)
    ctx.close()


EARLY_SPACING = 10
EARLY_PAUSES = {
    "weights": 1, "ln_out_a": 1, "ln_out_b": 1, "ln_out_c": 1, "ln_out_d": 0, "features": 1, "k_features": 2,
    "q_features": 1, "q_features2": 1, "sums": 1, "quotient": 1, "oT": 1, "out0": 1, "top2": 1, "combine": 1,
    "experts": 1, "moe_out": 1, "scores": 1, "exp": 0, "threshold": 1, "spT": 1, "attend": 1, "back": 1,
    "ln_sq_a": 2, "ln_sd_a": 1, "ln_sq_b": 1, "ln_sd_b": 1, "ln_sq_c": 1, "ln_sd_c": 1, "ln_sq_d": 1,
    "ln_sd_d": 2,
}
LATE_SPACING = 8
LATE_PLAN = [
    (0, "start"),
    (1, "split_xs"),
    (2, "project", 0, 0),
    (2, "project", 0, 1),
    (3, "project", 0, 2),
    (4, "project", 0, 3),
    (5, "project", 1, 0),
    (5, "square", 0),
    (7, "next_weights", 0),
    (7, "project", 1, 1),
    (7, "sum_squares", 0),
    (7, "rotate", 0),
    (8, "next_weights", 1),
    (8, "project", 1, 2),
    (8, "project", 1, 3),
    (8, "rotate_add", 0),
    (9, "next_weights", 2),
    (10, "square", 1),
    (10, "sum_squares", 1),
    (11, "next_weights", 3),
    (11, "norm_root"),
    (11, "rotate", 1),
    (11, "rotate_add", 1),
    (11, "norm_inverse"),
    (11, "normalise", 0),
    (11, "values", 0, 0),
    (12, "values", 0, 1),
    (13, "normalise", 1),
    (13, "values", 1, 0),
    (13, "transpose_qk", 0, 0),
    (13, "transpose_qk", 0, 1),
    (13, "values", 1, 1),
    (14, "transpose_qk", 0, 2),
    (14, "transpose_qk", 0, 3),
    (15, "next_weights", 4),
    (15, "transpose_qk", 1, 0),
    (15, "transpose_qk", 1, 1),
    (15, "pair_values", 0),
    (15, "scores", 0, 0, 1),
    (16, "next_weights", 5),
    (16, "transpose_qk", 1, 2),
    (16, "transpose_qk", 1, 3),
    (16, "pair_values", 1),
    (16, "scores", 0, 2),
    (16, "scores", 0, 3),
    (17, "softmax_in", 0),
    (19, "scores", 1, 0, 1),
    (21, "softmax_sum", 0),
    (21, "transpose_p", 0, 0),
    (21, "transpose_p", 0, 1),
    (21, "scores", 1, 2),
    (22, "attend", 0, 0, 1),
    (22, "scores", 1, 3),
    (23, "attend", 0, 2),
    (23, "softmax_in", 1),
    (24, "attend", 0, 3),
    (24, "attended", 0),
    (25, "softmax_sum", 1),
    (25, "transpose_p", 1, 0),
    (25, "transpose_p", 1, 1),
    (25, "transpose_o", 0, 0),
    (25, "transpose_o", 0, 1),
    (26, "attend", 1, 0, 1),
    (26, "attend", 1, 2),
    (27, "attend", 1, 3),
    (28, "attended", 1),
    (30, "transpose_o", 1, 0),
    (30, "transpose_o", 1, 1),
    (31, "project_out"),
    (32, "add_attention"),
    (34, "ln_mean"),
    (34, "ln_centre"),
    (35, "ln_variance"),
    (36, "ln_out"),
    (38, "up", 0),
    (39, "gate", 0),
    (39, "up", 1),
    (39, "gate", 1),
    (39, "up", 2),
    (40, "gate", 2),
    (41, "next_weights", 6),
    (42, "next_weights", 7),
    (42, "down"),
    (42, "add_ffn"),
    (43, "finish"),
]

_INS = ["L0_attn_x", "L0_attn_Wq", "L0_attn_bq", "L0_attn_Wk", "L0_attn_bk", "L0_attn_Wv", "L0_attn_bv",
        "L0_attn_Wo", "L0_attn_bo", "L0_attn_rw", "L0_ffn_W_gate", "L0_ffn_W_in", "L0_ffn_b_in", "L0_ffn_W_out",
        "L0_ffn_b_out", "L0_c", "L0_wmod", "L1_attn_W", "L1_ffn_Wqkv", "L1_ffn_q_scale", "L1_ffn_k_scale",
        "L1_ffn_Wo", "L1_ffn_ln_g", "L1_ffn_ln_b", "L1_ffn_W1", "L1_ffn_b1", "L1_ffn_W2", "L1_ffn_b2", "L1_c",
        "L1_wmod"]


def kernel(**inputs):
    import concourse.bacc as _bacc
    from concourse.bass_utils import run_bass_kernel_spmd as _run

    nc = _bacc.Bacc("TRN2", target_bir_lowering=False, num_devices=1)
    arrays, aps = {}, {}
    for name in _INS:
        arr = np.ascontiguousarray(inputs[name])
        arrays[f"in_{name}_dram"] = arr
        aps[name] = nc.dram_tensor(f"in_{name}_dram", arr.shape, mybir.dt.from_np(arr.dtype),
                                   kind="ExternalInput").ap()
    arrays["const_dram"] = constants()
    aps["const"] = nc.dram_tensor("const_dram", (P, NCONST), F32, kind="ExternalInput").ap()
    out = nc.dram_tensor("out_dram", (B, S, D), F32, kind="ExternalOutput").ap()
    build(nc, aps, out)
    r = _run(nc, [arrays], core_ids=[0])
    return r.results[0]["out_dram"]
```
